# Optimizing a Trainium2 kernel written in Bass

```python
import numpy as np
import jax
import jax.numpy as jnp

def _softmax(x, axis=-1):
    return jax.nn.softmax(x, axis=axis)

def _gelu(x):
    return jax.nn.gelu(x, approximate=True)

def _silu(x):
    return jax.nn.silu(x)

def _sigmoid(x):
    return jax.nn.sigmoid(x)

def _layernorm(x, axis=-1, eps=1e-05):
    m = jnp.mean(x, axis=axis, keepdims=True)
    v = jnp.var(x, axis=axis, keepdims=True)
    return (x - m) / jnp.sqrt(v + eps)

def _scatter_add(tgt, idx, src, axis=0):
    return tgt.at[idx].add(src)

def _segment_sum(src, seg, n):
    return jax.ops.segment_sum(src, seg, n)
kernel_name = 'mk_xattn_ffn_d4_seqx_r8_0bc476'

def setup_inputs(seed: int=0):
    np.random.seed(seed)
    _w = jnp.asarray

    def _rec_inputs():
        import jax
        import jax.numpy as jnp
        _rk = jax.random.key(seed)
        x = 7.22e-05 + 1 * jax.random.normal(jax.random.fold_in(_rk, 1), (8, 128, 512), jnp.float32)
        _lenS = 128 - jax.random.randint(jax.random.fold_in(_rk, 7), (8,), 0, max(1, 128 // 4) + 1, jnp.int32)
        _lenS2 = 128 - jax.random.randint(jax.random.fold_in(_rk, 8), (8,), 0, max(1, 128 // 4) + 1, jnp.int32)
        _ctx_4096P = jax.random.normal(jax.random.fold_in(_rk, 11), (8, 16, 512), jnp.float32)
        _ctx_4096c = jax.random.dirichlet(jax.random.fold_in(_rk, 511), 0.3 * jnp.ones((16,), jnp.float32), (8, 128))
        _ctx_4096t = jnp.einsum('bsk,bkd->bsd', _ctx_4096c, _ctx_4096P)
        _ctx_4096t = _ctx_4096t * jax.lax.rsqrt(jnp.mean(jnp.square(_ctx_4096t)) + 1e-12) * 0.953939
        ctx_4096 = 4.13588e-05 + 0.999923 * (_ctx_4096t + 0.3 * jax.random.normal(jax.random.fold_in(_rk, 611), (8, 128, 512), jnp.float32))
        _validS = jnp.arange(128)[None, :] < _lenS[:, None]
        _validS2 = jnp.arange(128)[None, :] < _lenS2[:, None]
        _causal = jnp.tril(jnp.ones((128, 128), dtype=bool))
        mask_BxSxS2_bk0 = jnp.logical_not(jnp.broadcast_to(_validS2[:, None, :], (8, 128, 128)))
        mask_Bx1x4096_ff1 = jnp.where(jnp.ones((8, 1, 512), dtype=bool), 1.0, 0.0).astype(jnp.float32)
        mask_1x1xSxS2_ff0 = jnp.where(jnp.ones((1, 1, 128, 128), dtype=bool), 0.0, -1000000000.0).astype(jnp.float32)
        return (x, ctx_4096, mask_BxSxS2_bk0, mask_Bx1x4096_ff1, mask_1x1xSxS2_ff0)
    x, ctx_4096, mask_BxSxS2_bk0, mask_Bx1x4096_ff1, mask_1x1xSxS2_ff0 = _rec_inputs()

    def _L0_xattn_setup():
        import jax, jax.numpy as jnp
        import numpy as np
        B, LQ, LK, D, H, DH = (2, 128, 128, 512, 32, 128)
        EPS = 1e-05

        def _rmsnorm(x, weight):
            var = jnp.mean(jnp.square(x), axis=-1, keepdims=True)
            return x * jax.lax.rsqrt(var + EPS) * weight
        key = jax.random.key(seed)
        ks = jax.random.split(key, 8)
        scale = 0.02
        return {'hidden_states': jax.random.normal(ks[0], (B, LQ, D), jnp.float32), 'key_value_states': jax.random.normal(ks[1], (B, LK, D), jnp.float32), 'attention_mask': jax.random.randint(ks[2], (B, LQ, LK), 0, 2) > 0, 'position_bias': jax.random.normal(ks[3], (H, LQ, LK), jnp.float32), 'ln_weight': jnp.ones((D,), jnp.float32), 'w_q': jax.random.normal(ks[4], (H * DH, D), jnp.float32) * scale, 'w_k': jax.random.normal(ks[5], (H * DH, D), jnp.float32) * scale, 'w_v': jax.random.normal(ks[6], (H * DH, D), jnp.float32) * scale, 'w_out': jax.random.normal(ks[7], (D, H * DH), jnp.float32) * scale}
    _L0_xattn_all = _L0_xattn_setup()
    _L0_xattn_in = {k: v for k, v in _L0_xattn_all.items() if k in ('position_bias', 'ln_weight', 'w_q', 'w_k', 'w_v', 'w_out')}
    del _L0_xattn_all

    def _L0_ffn_setup():
        import jax, jax.numpy as jnp
        import numpy as np
        DIM = 512
        HID = 1376
        R = 16
        SCALING = 32.0 / 16.0

        def _lora_linear(x, w, a, b):
            base = jnp.einsum('bsd,od->bso', x, w)
            low = jnp.einsum('bsr,or->bso', jnp.einsum('bsd,rd->bsr', x, a), b)
            return base + low * SCALING
        key = jax.random.key(seed)
        ks = jax.random.split(key, 10)
        s_in = 1.0 / np.sqrt(DIM)
        s_hid = 1.0 / np.sqrt(HID)
        return {'x': jax.random.normal(ks[0], (4, 256, DIM), jnp.float32), 'w1': jax.random.normal(ks[1], (HID, DIM), jnp.float32) * s_in, 'w3': jax.random.normal(ks[2], (HID, DIM), jnp.float32) * s_in, 'w2': jax.random.normal(ks[3], (DIM, HID), jnp.float32) * s_hid, 'lora_A1': jax.random.normal(ks[4], (R, DIM), jnp.float32) * s_in, 'lora_B1': jax.random.normal(ks[5], (HID, R), jnp.float32) * 0.02, 'lora_A3': jax.random.normal(ks[6], (R, DIM), jnp.float32) * s_in, 'lora_B3': jax.random.normal(ks[7], (HID, R), jnp.float32) * 0.02, 'lora_A2': jax.random.normal(ks[8], (R, HID), jnp.float32) * s_hid, 'lora_B2': jax.random.normal(ks[9], (DIM, R), jnp.float32) * 0.02}
    _L0_ffn_all = _L0_ffn_setup()
    _L0_ffn_in = {k: v for k, v in _L0_ffn_all.items() if k in ('w1', 'w3', 'w2', 'lora_A1', 'lora_B1', 'lora_A3', 'lora_B3', 'lora_A2', 'lora_B2')}
    del _L0_ffn_all

    def _L1_xattn_setup():
        import jax, jax.numpy as jnp
        import numpy as np
        W = 128
        H = 8
        D = 128
        DK = D // 2

        def _to_patches(x):
            b, d, s = x.shape
            np_ = s // W
            return x.reshape(b, d, np_, W).transpose(0, 2, 1, 3).reshape(b * np_, d, W)
        key = jax.random.key(seed)
        ks = jax.random.split(key, 10)
        B, S = (8, 512)
        qk = jax.random.normal(ks[0], (B, D, S), dtype=jnp.float32)
        v = jax.random.normal(ks[1], (B, D, S), dtype=jnp.float32)
        masks = jnp.ones((B, 1, S), dtype=jnp.float32)
        sc = 1.0 / np.sqrt(D)
        Wq = jax.random.normal(ks[2], (DK, D), dtype=jnp.float32) * sc
        bq = jnp.zeros((DK,), dtype=jnp.float32)
        Wk = jax.random.normal(ks[3], (DK, D), dtype=jnp.float32) * sc
        bk = jnp.zeros((DK,), dtype=jnp.float32)
        Wv = jax.random.normal(ks[4], (DK, D), dtype=jnp.float32) * sc
        bv = jnp.zeros((DK,), dtype=jnp.float32)
        Wo = jax.random.normal(ks[5], (D, DK), dtype=jnp.float32) * (1.0 / np.sqrt(DK))
        bo = jnp.zeros((D,), dtype=jnp.float32)
        return dict(qk=qk, v=v, masks=masks, Wq=Wq, bq=bq, Wk=Wk, bk=bk, Wv=Wv, bv=bv, Wo=Wo, bo=bo)
    _L1_xattn_all = _L1_xattn_setup()
    _L1_xattn_in = {k: v for k, v in _L1_xattn_all.items() if k in ('Wq', 'bq', 'Wk', 'bk', 'Wv', 'bv', 'Wo', 'bo')}
    del _L1_xattn_all

    def _L1_ffn_setup():
        import jax, jax.numpy as jnp
        import numpy as np
        DIM = 512
        INTER = 1792
        SPARSITY = 32
        RANK = 16
        key = jax.random.key(seed)
        ks = jax.random.split(key, 5)
        B, T = (32, 1)
        x = jax.random.normal(ks[0], (B, T, DIM), dtype=jnp.float32)
        c1_w = jax.random.normal(ks[1], (RANK, DIM), dtype=jnp.float32) * (1.0 / np.sqrt(DIM))
        c2_w = jax.random.normal(ks[2], (INTER, RANK), dtype=jnp.float32) * (1.0 / np.sqrt(RANK))
        w1 = jax.random.normal(ks[3], (INTER, DIM), dtype=jnp.float32) * (1.0 / np.sqrt(DIM))
        w2t = jax.random.normal(ks[4], (INTER, DIM), dtype=jnp.float32) * (1.0 / np.sqrt(INTER))
        return {'x': x, 'c1_w': c1_w, 'c2_w': c2_w, 'w1': w1, 'w2t': w2t}
    _L1_ffn_all = _L1_ffn_setup()
    _L1_ffn_in = {k: v for k, v in _L1_ffn_all.items() if k in ('c1_w', 'c2_w', 'w1', 'w2t')}
    del _L1_ffn_all

    def _L2_xattn_setup():
        import jax, jax.numpy as jnp
        import numpy as np
        B, Q, K, D = (1, 128, 6404, 512)
        H, KVH, HD = (32, 8, 128)
        GROUPS = H // KVH
        EPS = 1e-05

        def _rmsnorm(x, w):
            xf = x.astype(jnp.float32)
            var = jnp.mean(xf * xf, axis=-1, keepdims=True)
            return (xf * jax.lax.rsqrt(var + EPS)).astype(x.dtype) * w
        key = jax.random.key(seed)
        ks = jax.random.split(key, 8)
        s = 0.02
        return {'hidden_states': jax.random.normal(ks[0], (B, Q, D), jnp.float32), 'cross_attention_states': jax.random.normal(ks[1], (B, K, D), jnp.float32), 'attention_mask': jnp.zeros((B, 1, Q, K), jnp.float32), 'Wq': jax.random.normal(ks[2], (H * HD, D), jnp.float32) * s, 'Wk': jax.random.normal(ks[3], (KVH * HD, D), jnp.float32) * s, 'Wv': jax.random.normal(ks[4], (KVH * HD, D), jnp.float32) * s, 'Wo': jax.random.normal(ks[5], (D, H * HD), jnp.float32) * s, 'q_norm_w': jnp.ones((HD,), jnp.float32), 'k_norm_w': jnp.ones((HD,), jnp.float32)}
    _L2_xattn_all = _L2_xattn_setup()
    _L2_xattn_in = {k: v for k, v in _L2_xattn_all.items() if k in ('Wq', 'Wk', 'Wv', 'Wo', 'q_norm_w', 'k_norm_w')}
    del _L2_xattn_all

    def _L2_ffn_setup():
        import jax, jax.numpy as jnp
        import numpy as np
        R = 16
        NUM_EXPERTS = 8
        TOP_K = 2
        LORA_ALPHA = 32
        SCALING = LORA_ALPHA / R
        key = jax.random.key(seed)
        ks = jax.random.split(key, 6)
        d_in, d_out = (512, 512)
        x = jax.random.normal(ks[0], (4, 256, d_in), dtype=jnp.float32)
        W_base = jax.random.normal(ks[1], (d_out, d_in), dtype=jnp.float32) * 0.02
        b_base = jax.random.normal(ks[2], (d_out,), dtype=jnp.float32) * 0.02
        W_router = jax.random.normal(ks[3], (NUM_EXPERTS, d_in), dtype=jnp.float32) * 0.01
        A = jax.random.normal(ks[4], (NUM_EXPERTS, R, d_in), dtype=jnp.float32) * 0.02
        B = jax.random.normal(ks[5], (NUM_EXPERTS, d_out, R), dtype=jnp.float32) * 0.02
        return {'x': x, 'W_base': W_base, 'b_base': b_base, 'W_router': W_router, 'A': A, 'B': B}
    _L2_ffn_all = _L2_ffn_setup()
    _L2_ffn_in = {k: v for k, v in _L2_ffn_all.items() if k in ('W_base', 'b_base', 'W_router', 'A', 'B')}
    del _L2_ffn_all

    def _L3_xattn_setup():
        import jax, jax.numpy as jnp
        import numpy as np
        HID = 512
        NHEAD = 32
        NKV = 8
        HDIM = 128
        G = NHEAD // NKV
        key = jax.random.key(seed)
        ks = jax.random.split(key, 6)
        s = 0.02
        B, L = (2, 256)
        return {'query': jax.random.normal(ks[0], (B, L, HID), jnp.float32), 'kv': jax.random.normal(ks[1], (B, L, HID), jnp.float32), 'Wq': jax.random.normal(ks[2], (HID, NHEAD * HDIM), jnp.float32) * s, 'bq': jnp.zeros((NHEAD * HDIM,), jnp.float32), 'Wkv': jax.random.normal(ks[3], (HID, 2 * NKV * HDIM), jnp.float32) * s, 'bkv': jnp.zeros((2 * NKV * HDIM,), jnp.float32), 'Wo': jax.random.normal(ks[4], (NHEAD * HDIM, HID), jnp.float32) * s, 'bo': jnp.zeros((HID,), jnp.float32)}
    _L3_xattn_all = _L3_xattn_setup()
    _L3_xattn_in = {k: v for k, v in _L3_xattn_all.items() if k in ('Wq', 'bq', 'Wkv', 'bkv', 'Wo', 'bo')}
    del _L3_xattn_all

    def _L3_ffn_setup():
        import jax, jax.numpy as jnp
        import numpy as np
        B, S, D, F = (4, 256, 512, 2048)
        key = jax.random.key(seed)
        k = jax.random.split(key, 5)
        scale_in = 1.0 / np.sqrt(D)
        scale_out = 1.0 / np.sqrt(F)
        return {'input': jax.random.normal(k[0], (B, S, D), dtype=jnp.float32), 'inter_w': jax.random.normal(k[1], (D, F), dtype=jnp.float32) * scale_in, 'inter_b': jax.random.normal(k[2], (F,), dtype=jnp.float32) * 0.02, 'output_w': jax.random.normal(k[3], (F, D), dtype=jnp.float32) * scale_out, 'output_b': jax.random.normal(k[4], (D,), dtype=jnp.float32) * 0.02}
    _L3_ffn_all = _L3_ffn_setup()
    _L3_ffn_in = {k: v for k, v in _L3_ffn_all.items() if k in ('inter_w', 'inter_b', 'output_w', 'output_b')}
    del _L3_ffn_all
    return {'x': x, 'ctx_4096': ctx_4096, 'mask_BxSxS2_bk0': mask_BxSxS2_bk0, 'mask_Bx1x4096_ff1': mask_Bx1x4096_ff1, 'mask_1x1xSxS2_ff0': mask_1x1xSxS2_ff0, 'L0_xattn_position_bias': _L0_xattn_in['position_bias'], 'L0_xattn_ln_weight': _L0_xattn_in['ln_weight'], 'L0_xattn_w_q': _L0_xattn_in['w_q'], 'L0_xattn_w_k': _L0_xattn_in['w_k'], 'L0_xattn_w_v': _L0_xattn_in['w_v'], 'L0_xattn_w_out': _L0_xattn_in['w_out'], 'L0_ffn_w1': _L0_ffn_in['w1'], 'L0_ffn_w3': _L0_ffn_in['w3'], 'L0_ffn_w2': _L0_ffn_in['w2'], 'L0_ffn_lora_A1': _L0_ffn_in['lora_A1'], 'L0_ffn_lora_B1': _L0_ffn_in['lora_B1'], 'L0_ffn_lora_A3': _L0_ffn_in['lora_A3'], 'L0_ffn_lora_B3': _L0_ffn_in['lora_B3'], 'L0_ffn_lora_A2': _L0_ffn_in['lora_A2'], 'L0_ffn_lora_B2': _L0_ffn_in['lora_B2'], 'L1_xattn_Wq': _L1_xattn_in['Wq'], 'L1_xattn_bq': _L1_xattn_in['bq'], 'L1_xattn_Wk': _L1_xattn_in['Wk'], 'L1_xattn_bk': _L1_xattn_in['bk'], 'L1_xattn_Wv': _L1_xattn_in['Wv'], 'L1_xattn_bv': _L1_xattn_in['bv'], 'L1_xattn_Wo': _L1_xattn_in['Wo'], 'L1_xattn_bo': _L1_xattn_in['bo'], 'L1_ffn_c1_w': _L1_ffn_in['c1_w'], 'L1_ffn_c2_w': _L1_ffn_in['c2_w'], 'L1_ffn_w1': _L1_ffn_in['w1'], 'L1_ffn_w2t': _L1_ffn_in['w2t'], 'L2_xattn_Wq': _L2_xattn_in['Wq'], 'L2_xattn_Wk': _L2_xattn_in['Wk'], 'L2_xattn_Wv': _L2_xattn_in['Wv'], 'L2_xattn_Wo': _L2_xattn_in['Wo'], 'L2_xattn_q_norm_w': _L2_xattn_in['q_norm_w'], 'L2_xattn_k_norm_w': _L2_xattn_in['k_norm_w'], 'L2_ffn_W_base': _L2_ffn_in['W_base'], 'L2_ffn_b_base': _L2_ffn_in['b_base'], 'L2_ffn_W_router': _L2_ffn_in['W_router'], 'L2_ffn_A': _L2_ffn_in['A'], 'L2_ffn_B': _L2_ffn_in['B'], 'L3_xattn_Wq': _L3_xattn_in['Wq'], 'L3_xattn_bq': _L3_xattn_in['bq'], 'L3_xattn_Wkv': _L3_xattn_in['Wkv'], 'L3_xattn_bkv': _L3_xattn_in['bkv'], 'L3_xattn_Wo': _L3_xattn_in['Wo'], 'L3_xattn_bo': _L3_xattn_in['bo'], 'L3_ffn_inter_w': _L3_ffn_in['inter_w'], 'L3_ffn_inter_b': _L3_ffn_in['inter_b'], 'L3_ffn_output_w': _L3_ffn_in['output_w'], 'L3_ffn_output_b': _L3_ffn_in['output_b']}

def reference(x, ctx_4096, mask_BxSxS2_bk0, mask_Bx1x4096_ff1, mask_1x1xSxS2_ff0, L0_xattn_position_bias, L0_xattn_ln_weight, L0_xattn_w_q, L0_xattn_w_k, L0_xattn_w_v, L0_xattn_w_out, L0_ffn_w1, L0_ffn_w3, L0_ffn_w2, L0_ffn_lora_A1, L0_ffn_lora_B1, L0_ffn_lora_A3, L0_ffn_lora_B3, L0_ffn_lora_A2, L0_ffn_lora_B2, L1_xattn_Wq, L1_xattn_bq, L1_xattn_Wk, L1_xattn_bk, L1_xattn_Wv, L1_xattn_bv, L1_xattn_Wo, L1_xattn_bo, L1_ffn_c1_w, L1_ffn_c2_w, L1_ffn_w1, L1_ffn_w2t, L2_xattn_Wq, L2_xattn_Wk, L2_xattn_Wv, L2_xattn_Wo, L2_xattn_q_norm_w, L2_xattn_k_norm_w, L2_ffn_W_base, L2_ffn_b_base, L2_ffn_W_router, L2_ffn_A, L2_ffn_B, L3_xattn_Wq, L3_xattn_bq, L3_xattn_Wkv, L3_xattn_bkv, L3_xattn_Wo, L3_xattn_bo, L3_ffn_inter_w, L3_ffn_inter_b, L3_ffn_output_w, L3_ffn_output_b):
    import jax
    import jax.numpy as jnp

    def _L0_xattn_ref(hidden_states, key_value_states, attention_mask, position_bias, ln_weight, w_q, w_k, w_v, w_out):
        import jax, jax.numpy as jnp
        import numpy as np
        B, LQ, LK, D, H, DH = (2, 128, 128, 512, 32, 128)
        EPS = 1e-05

        def _rmsnorm(x, weight):
            var = jnp.mean(jnp.square(x), axis=-1, keepdims=True)
            return x * jax.lax.rsqrt(var + EPS) * weight
        x = _rmsnorm(hidden_states, ln_weight)
        b, lq, _ = x.shape
        lk = key_value_states.shape[1]
        h_q = (x @ w_q.T).reshape(b, lq, H, DH)
        h_k = (key_value_states @ w_k.T).reshape(b, lk, H, DH)
        h_v = (key_value_states @ w_v.T).reshape(b, lk, H, DH)
        score = jnp.einsum('bqhd,bkhd->bhqk', h_q, h_k)
        score = score + position_bias[None]
        m = attention_mask[:, None]
        score = jnp.where(m, score, -jnp.inf)
        score = jax.nn.softmax(score, axis=-1)
        score = jnp.where(m, score, 0.0)
        attn = jnp.einsum('bhqk,bkhd->bqhd', score, h_v).reshape(b, lq, H * DH)
        out = attn @ w_out.T
        return hidden_states + out

    def _L0_ffn_ref(x, w1, w3, w2, lora_A1, lora_B1, lora_A3, lora_B3, lora_A2, lora_B2):
        import jax, jax.numpy as jnp
        import numpy as np
        DIM = 512
        HID = 1376
        R = 16
        SCALING = 32.0 / 16.0

        def _lora_linear(x, w, a, b):
            base = jnp.einsum('bsd,od->bso', x, w)
            low = jnp.einsum('bsr,or->bso', jnp.einsum('bsd,rd->bsr', x, a), b)
            return base + low * SCALING
        h1 = _lora_linear(x, w1, lora_A1, lora_B1)
        h3 = _lora_linear(x, w3, lora_A3, lora_B3)
        g = jax.nn.silu(h1) * h3
        return _lora_linear(g, w2, lora_A2, lora_B2)

    def _L1_xattn_ref(qk, v, masks, Wq, bq, Wk, bk, Wv, bv, Wo, bo):
        import jax, jax.numpy as jnp
        import numpy as np
        W = 128
        H = 8
        D = 128
        DK = D // 2

        def _to_patches(x):
            b, d, s = x.shape
            np_ = s // W
            return x.reshape(b, d, np_, W).transpose(0, 2, 1, 3).reshape(b * np_, d, W)
        B, _, S = qk.shape
        np_ = S // W
        qp = _to_patches(qk)
        vp = _to_patches(v)
        mp = _to_patches(masks)
        q = jnp.einsum('ed,bdw->bew', Wq, qp) + bq[:, None]
        k = jnp.einsum('ed,bdw->bew', Wk, qp) + bk[:, None]
        val = jnp.einsum('ed,bdw->bew', Wv, vp) + bv[:, None]
        BN = q.shape[0]
        dh = DK // H
        qh = q.reshape(BN, H, dh, W)
        kh = k.reshape(BN, H, dh, W)
        vh = val.reshape(BN, H, dh, W)
        scores = jnp.einsum('bhdi,bhdj->bhij', qh, kh) / jnp.sqrt(jnp.asarray(dh, qh.dtype))
        scores = jnp.where(mp[:, :, None, :] > 0, scores, jnp.asarray(-1000000000.0, scores.dtype))
        attn = jax.nn.softmax(scores, axis=-1)
        o = jnp.einsum('bhij,bhdj->bhdi', attn, vh).reshape(BN, DK, W)
        o = jax.nn.gelu(o, approximate=False)
        out = jnp.einsum('de,bew->bdw', Wo, o) + bo[:, None]
        out = out.reshape(B, np_, D, W).transpose(0, 2, 1, 3).reshape(B, D, S)
        out = out * masks
        return out

    def _L1_ffn_ref(x, c1_w, c2_w, w1, w2t):
        import jax, jax.numpy as jnp
        import numpy as np
        DIM = 512
        INTER = 1792
        SPARSITY = 32
        RANK = 16
        B, T, M = x.shape
        xf = x.reshape(B * T, M)
        inter = xf @ c1_w.T @ c2_w.T
        n_blocks = INTER // SPARSITY
        blk = inter.reshape(B * T, n_blocks, SPARSITY)
        idx = jnp.argmax(blk, axis=-1) + jnp.arange(0, INTER, SPARSITY)
        w1_g = w1[idx]
        w2_g = w2t[idx]
        h = jax.nn.relu(jnp.einsum('bkm,bm->bk', w1_g, xf))
        out = jnp.einsum('bk,bkm->bm', h, w2_g)
        return out.reshape(B, T, M)

    def _L2_xattn_ref(hidden_states, cross_attention_states, attention_mask, Wq, Wk, Wv, Wo, q_norm_w, k_norm_w):
        import jax, jax.numpy as jnp
        import numpy as np
        B, Q, K, D = (1, 128, 6404, 512)
        H, KVH, HD = (32, 8, 128)
        GROUPS = H // KVH
        EPS = 1e-05

        def _rmsnorm(x, w):
            xf = x.astype(jnp.float32)
            var = jnp.mean(xf * xf, axis=-1, keepdims=True)
            return (xf * jax.lax.rsqrt(var + EPS)).astype(x.dtype) * w
        bsz, q_len, _ = hidden_states.shape
        kv_len = cross_attention_states.shape[1]
        q = (hidden_states @ Wq.T).reshape(bsz, q_len, H, HD).transpose(0, 2, 1, 3)
        k = (cross_attention_states @ Wk.T).reshape(bsz, kv_len, KVH, HD).transpose(0, 2, 1, 3)
        v = (cross_attention_states @ Wv.T).reshape(bsz, kv_len, KVH, HD).transpose(0, 2, 1, 3)
        q = _rmsnorm(q, q_norm_w)
        k = jnp.repeat(k, GROUPS, axis=1)
        v = jnp.repeat(v, GROUPS, axis=1)
        k = _rmsnorm(k, k_norm_w)
        scale = 1.0 / np.sqrt(HD)
        scores = jnp.einsum('bhqd,bhkd->bhqk', q, k) * scale
        scores = scores + attention_mask[:, :, :, :kv_len]
        probs = jax.nn.softmax(scores.astype(jnp.float32), axis=-1).astype(q.dtype)
        out = jnp.einsum('bhqk,bhkd->bhqd', probs, v)
        out = out.transpose(0, 2, 1, 3).reshape(bsz, q_len, H * HD)
        return out @ Wo.T

    def _L2_ffn_ref(x, W_base, b_base, W_router, A, B):
        import jax, jax.numpy as jnp
        import numpy as np
        R = 16
        NUM_EXPERTS = 8
        TOP_K = 2
        LORA_ALPHA = 32
        SCALING = LORA_ALPHA / R
        orig_shape = x.shape
        d_in = x.shape[-1]
        x_flat = x.reshape(-1, d_in)
        logits = x_flat @ W_router.T
        probs = jax.nn.softmax(logits, axis=-1)
        topk_probs, topk_idx = jax.lax.top_k(probs, TOP_K)
        topk_probs = topk_probs / jnp.sum(topk_probs, axis=-1, keepdims=True)
        onehot = jax.nn.one_hot(topk_idx, NUM_EXPERTS, dtype=x.dtype)
        combine = jnp.einsum('nk,nke->ne', topk_probs, onehot)
        h = jnp.einsum('nd,erd->ner', x_flat, A)
        hw = h * combine[:, :, None]
        expert_out = jnp.einsum('ner,eor->no', hw, B) * SCALING
        base_out = x_flat @ W_base.T + b_base
        out = base_out + expert_out
        return out.reshape(*orig_shape[:-1], W_base.shape[0])

    def _L3_xattn_ref(query, kv, Wq, bq, Wkv, bkv, Wo, bo):
        import jax, jax.numpy as jnp
        import numpy as np
        HID = 512
        NHEAD = 32
        NKV = 8
        HDIM = 128
        G = NHEAD // NKV
        B, L, _ = query.shape
        Lk = kv.shape[1]
        scale = jnp.asarray(1.0 / np.sqrt(HDIM), query.dtype)
        q = (query @ Wq + bq).reshape(B, L, NKV, G, HDIM)
        k_, v_ = jnp.split(kv @ Wkv + bkv, 2, axis=-1)
        k = k_.reshape(B, Lk, NKV, HDIM)
        v = v_.reshape(B, Lk, NKV, HDIM)
        scores = jnp.einsum('blkgd,bmkd->bkglm', q, k) * scale
        attn = jax.nn.softmax(scores, axis=-1)
        o = jnp.einsum('bkglm,bmkd->blkgd', attn, v).reshape(B, L, NHEAD * HDIM)
        return o @ Wo + bo

    def _L3_ffn_ref(input, inter_w, inter_b, output_w, output_b):
        import jax, jax.numpy as jnp
        import numpy as np
        B, S, D, F = (4, 256, 512, 2048)
        h = jax.nn.gelu(jnp.einsum('bsd,df->bsf', input, inter_w) + inter_b, approximate=True)
        out = jnp.einsum('bsf,fd->bsd', h, output_w) + output_b
        return out
    x = x + _L0_xattn_ref(_layernorm(x, axis=-1), ctx_4096, mask_BxSxS2_bk0, L0_xattn_position_bias, L0_xattn_ln_weight, L0_xattn_w_q, L0_xattn_w_k, L0_xattn_w_v, L0_xattn_w_out)
    x = x + _L0_ffn_ref(_layernorm(x, axis=-1), L0_ffn_w1, L0_ffn_w3, L0_ffn_w2, L0_ffn_lora_A1, L0_ffn_lora_B1, L0_ffn_lora_A3, L0_ffn_lora_B3, L0_ffn_lora_A2, L0_ffn_lora_B2)
    x = x + _L1_xattn_ref(_layernorm(x, axis=-1), ctx_4096, mask_Bx1x4096_ff1, L1_xattn_Wq, L1_xattn_bq, L1_xattn_Wk, L1_xattn_bk, L1_xattn_Wv, L1_xattn_bv, L1_xattn_Wo, L1_xattn_bo)
    x = x + _L1_ffn_ref(_layernorm(x, axis=-1), L1_ffn_c1_w, L1_ffn_c2_w, L1_ffn_w1, L1_ffn_w2t)
    x = x + _L2_xattn_ref(_layernorm(x, axis=-1), ctx_4096, mask_1x1xSxS2_ff0, L2_xattn_Wq, L2_xattn_Wk, L2_xattn_Wv, L2_xattn_Wo, L2_xattn_q_norm_w, L2_xattn_k_norm_w)
    x = x + _L2_ffn_ref(_layernorm(x, axis=-1), L2_ffn_W_base, L2_ffn_b_base, L2_ffn_W_router, L2_ffn_A, L2_ffn_B)
    x = x + _L3_xattn_ref(_layernorm(x, axis=-1), ctx_4096, L3_xattn_Wq, L3_xattn_bq, L3_xattn_Wkv, L3_xattn_bkv, L3_xattn_Wo, L3_xattn_bo)
    x = x + _L3_ffn_ref(_layernorm(x, axis=-1), L3_ffn_inter_w, L3_ffn_inter_b, L3_ffn_output_w, L3_ffn_output_b)
    return x

_drawn_inputs = setup_inputs


def setup_inputs(seed=0):
    import zlib

    import numpy as np

    out = dict(_drawn_inputs(seed))
    spreads = {'L0_xattn_ln_weight': (1.0, 0.2),
     'L1_xattn_bq': (0.0, 0.8),
     'L1_xattn_bk': (0.0, 2.0),
     'L1_xattn_bv': (0.0, 0.332),
     'L1_xattn_bo': (0.0, 0.1),
     'L2_xattn_q_norm_w': (1.0, 0.6),
     'L2_xattn_k_norm_w': (1.0, 0.6),
     'L3_xattn_bq': (0.0, 2.0),
     'L3_xattn_bkv': (0.0, 0.1),
     'L3_xattn_bo': (0.0, 0.1)}
    factors = {'L2_ffn_b_base': 6.633,
     'L2_ffn_W_router': 8.461,
     'L3_xattn_Wq': 5.953,
     'L3_ffn_inter_b': 8.0,
     'L3_ffn_output_b': 7.018}
    for name, (base, spread) in spreads.items():
        noise = np.random.default_rng([zlib.crc32(name.encode()), seed]).standard_normal(out[name].shape)
        drawn = base * np.exp(spread * noise) if base else spread * noise
        out[name] = jnp.asarray(drawn.astype(out[name].dtype))
    for name, factor in factors.items():
        out[name] = (out[name] * factor).astype(out[name].dtype)
    return out
```

```python
from contextlib import ExitStack

import numpy as np

import concourse.bass as bass
from concourse import mybir

F32 = mybir.dt.float32
F32R = mybir.dt.float32r
I32 = mybir.dt.int32
U8 = mybir.dt.uint8
ALU = mybir.AluOpType
ACT = mybir.ActivationFunctionType
AX = mybir.AxisListType

P = 128
B = 8
S = 128
D = 512
DC = D // P
T = B * S
HALF = T // 2
BH = B // 2
NH = 32
GH = 4
NG = NH // GH
NPAIR = NH // 2
EPS = 1e-5
MASKED = 1e30
RSQRT_MAGIC = 0x5F3759DF
RSQRT_OPS = 11
PASSES = ((0, 0), (0, 1), (1, 0))

C_IDENT = 0
C_ONES = 128
C_HEADS = 256
C_ZERO = 264
C_MEAN = 265
C_FIRST = 266
C_LESS = 298
C_COUNT = 362

V_LNW, V_BQ3, V_BK3, V_BV3, V_QN, V_KN, V_BQ1, V_BK1, V_BO1, V_BI = 0, 4, 36, 44, 52, 53, 54, 55, 56, 57
V_COUNT = 89


def wait(engine, semaphore, value):
    if isinstance(value, int) and value <= 0:
        return
    engine.wait_ge(semaphore, value)


class Events:

    def __init__(self, semaphores, before, totals):
        self.semaphores = semaphores
        self.before = before
        self.after = dict(before)
        for name, n in totals.items():
            self.after[name] = before.get(name, 0) + n

    def __getitem__(self, name):
        return self.semaphores[name]

    def wait(self, engine, name, n):
        if isinstance(n, int) and n <= 0:
            return
        engine.wait_ge(self.semaphores[name], n + self.before.get(name, 0))


class Attention:

    def __init__(self, layer, stage, semaphores, before):
        self.layer = layer
        self.scale = float(P) ** -0.5
        self.stage = stage
        self.own_kv = layer == 0
        self.normed = layer == 2
        kv = GH if self.own_kv else 1
        self.tiles = 2 * kv + 2 * GH
        self.ring = 4 if self.own_kv else 5
        self.projections = 2 * kv + GH
        self.turns = 16 if self.own_kv else 17 if self.normed else 10
        self.turns_first = 6 if self.normed else 2
        units, heads = 2 * NH, NH
        turns = self.turns_first + self.turns * NG - (6 if self.normed else 2)
        calls = heads + NG if self.normed else 0
        totals = dict(split=self.tiles * NG, high_w=self.tiles * NG, sfull=units, rowmax=units, negmax=units,
                      exps=units, rinv=units, pready=units, tfull=turns, tfree=turns, pv=units, high=units,
                      low=units, outfull=B * NPAIR, added=B * NPAIR, sfree=units if layer != 3 else 0,
                      masked=units if layer == 0 else 0, rlive=units if layer == 0 else 0,
                      squared=calls, shifted=2 * calls, newton=9 * calls,
                      rsq=heads if self.normed else 0, diag=2 * NG if self.normed else 0)
        for i in range(2):
            totals["pfull", i] = totals["pfree", i] = self.projections * NG
            totals["bias_landed", i] = 16 * NPAIR if layer == 0 else 0
        for i in range(self.ring):
            totals["landed", i] = 16 * self.tiles // self.ring * NG
        self.events = Events(semaphores, before, totals)

    NAMES = ("split high_w sfull sfree masked rowmax negmax exps rinv rlive pready tfull tfree pv high low "
             "outfull added squared shifted newton rsq diag").split() + [
                 (n, i) for n in ("pfull", "pfree", "bias_landed") for i in range(2)] + [("landed", i) for i in range(5)]

    def new_kv(self, j):
        return self.own_kv or j == 0

    def tile(self, g, j, what):
        if self.own_kv:
            return self.tiles * g + 4 * j + "kvqo".index(what)
        return self.tiles * g + ("kv".index(what) if what in "kv" else 2 + 2 * j + "qo".index(what))

    def projection(self, g, j, what):
        if self.own_kv:
            return self.projections * g + 3 * j + "kvq".index(what)
        return self.projections * g + ("kv".index(what) if what in "kv" else 2 + j)

    def turn(self, g, j, what):
        if self.own_kv:
            order = ["T0", "T1", "V0", "V1"]
            at = 4 * j
        elif self.normed:
            order = ["T0", "T1", "Q"] if j < 3 else ["K", "T0", "T1", "V0", "V1", "Q", "B0", "B1"]
            at = 3 * j
            if isinstance(g, int) and g == NG - 1 and j == GH - 1:
                order = ["T0", "T1"]
        else:
            order = ["T0", "T1", "V0", "V1"]
            at = 2 * j
        if isinstance(g, int) and g < 0:
            return [x for x in order if x[0] != "T"].index(what)
        return self.turns_first + self.turns * g + at + order.index(what)


class FeedForward:

    def __init__(self, name, stage, kind, chunks, semaphores, before, small=(), row=None):
        self.name, self.stage, self.kind, self.chunks, self.row = name, stage, kind, chunks, row
        self.low_rank = kind != "gelu"
        self.what = ["in", "in2", "out"] if kind == "silu" else ["in", "out"]
        self.ring = 2 * len(self.what)
        n, halves, pre = chunks, 2 * chunks, int(self.low_rank)
        nt = len(self.what) * chunks
        silu, pick = halves * (kind == "silu"), halves * (kind == "pick")
        outs = B * ((chunks + 1) // 2)
        totals = dict(split=nt, high_w=nt, pre_landed=16 * pre, pre_split=2 * pre, small_landed=16 * len(small),
                      sfull=silu + pick, tfull=pick, made=halves, high=halves, low=halves, outfull=outs, added=outs,
                      lowfull=silu, low2=2 * (kind == "silu"), bmax=pick, equal=pick, weighed=pick, fmax=pick,
                      picked=pick)
        for i in range(2):
            totals["pfull", i] = n + pre
            totals["pfree", i] = (n + pre) * (kind != "gelu")
        for i in range(self.ring):
            totals["landed", i] = 16 * len(range(i, nt, self.ring))
        self.small = small
        self.events = Events(semaphores, before, totals)

    NAMES = ("split high_w pre_landed pre_split small_landed sfull tfull made high low outfull added lowfull low2 "
             "bmax equal weighed fmax picked").split() + [
                 (n, i) for n in ("pfull", "pfree") for i in range(2)] + [("landed", i) for i in range(6)]

    def tile(self, g, j, k):
        return len(self.what) * (GH * g + j) + k

    def out_tile(self, pair, slots):
        return len(self.what) * (2 * pair + len(slots))


def small_attention(sem):
    names = ("w_landed ones normed qk_full q_made k_biased k_made v_full v_made blocked sfull rowmax shifted exps "
             "tfull tfree av osum onorm v_inv oturned gelu out_full out_biased added").split()
    found = {n: sem(f"L1_{n}") for n in names}
    for n in ("ctx_landed", "mask_landed"):
        for i in range(2):
            found[n, i] = sem(f"L1_{n}{i}")
    return found


def mixture(sem):
    names = ("a_landed w_landed b_landed a_split w_split a_high w_high full copied route routed expd weighted "
             "turned high outfull added").split()
    return {n: sem(f"M2_{n}") for n in names}


def build(nc, ins, out):
    with ExitStack() as ctx:
        def sb(name, shape, dt=F32):
            return ctx.enter_context(nc.sbuf_tensor(name, shape, dt))

        def bank(name):
            return ctx.enter_context(nc.psum_tensor(name, [P, 512], F32))

        def sem(name):
            return ctx.enter_context(nc.semaphore(name))

        x = sb("x", [P, B, D])
        ctxT = sb("ctxT", [P, 2, DC, T], F32R)
        xnT = sb("xnT", [P, 2, DC, T], F32R)
        acts = sb("acts", [P, 4, 2, T], F32R)
        w_in = sb("w_in", [P, 2, 2, D], F32R)
        w_kv = sb("w_kv", [P, 2, 2, D], F32R)
        w_out = sb("w_out", [P, 4, 2, D], F32R)
        sq = sb("sq", [P, T])
        kblock = sb("kblock", [P, 2, 8, P])
        ring = sb("ring", [P, 6, D])
        big = sb("big", [P, 4, T])
        qT, kT, vT, v = (big[:, i, :] for i in range(4))
        tbuf = sb("tbuf", [P, 2, 512])
        pbuf = sb("pbuf", [P, 2, 512])
        ptbuf = sb("ptbuf", [P, 2, 512])
        mask_bytes = sb("mask_bytes", [P, T // 4], I32)
        maskadd = sb("maskadd", [P, B, S])
        biasbuf = sb("biasbuf", [P, 2, S])
        brow = sb("brow", [P, D])
        consts = sb("consts", [P, C_COUNT])
        vecs = sb("vecs", [P, V_COUNT])
        kqn = sb("kqn", [P, 1])
        live = sb("live", [P, B])
        stats = sb("stats", [P, B, 6])
        moments = sb("moments", [P, B, 2])
        rstd = sb("rstd", [P, B])
        rrms = sb("rrms", [P, B])
        nw_v = sb("nw_v", [P, B])
        nw_t = sb("nw_t", [P, B])
        rq = sb("rq", [P, B])
        rk = sb("rk", [P, B])
        rowmax = sb("rowmax", [P, 2, 8])
        blockmax = sb("blockmax", [P, 2, 16])
        firstmax = sb("firstmax", [P, 2, 16])
        negmax = sb("negmax", [P, 2, 8])
        rowsum = sb("rowsum", [P, 2, 8])
        rinv = sb("rinv", [P, 2, 8])
        ident = consts[:, C_IDENT:C_IDENT + P]
        ones = consts[:, C_ONES:C_ONES + P]
        zeros512 = consts[:, C_ZERO:C_ZERO + 1].broadcast_to([P, 512])

        proj = [bank(f"proj{i}") for i in range(2)]
        score = [bank(f"score{i}") for i in range(2)]
        turn = bank("turn")
        heado = bank("heado")
        outp = [bank(f"outp{i}") for i in range(2)]

        x_landed = sem("x_landed")
        consts_landed = sem("consts_landed")
        mask_landed = sem("mask_landed")
        ctx_landed = [sem(f"ctx_landed{i}") for i in range(4)]
        ctx_high = sem("ctx_high")
        ctx_split = sem("ctx_split")
        mask_made = sem("mask_made")
        kqn_made = sem("kqn_made")
        ln_stats, ln_moments, ln_shifted, ln_newton, ln_rstd, ln_normed, ln_full, ln_high, ln_low, ln_rms, ln_kept = (
            sem(f"ln_{n}") for n in "stats moments shifted newton rstd normed full high low rms kept".split())
        out_landed = sem("out_landed")
        row_landed = sem("row_landed")
        row_added = sem("row_added")
        flat = big[:, :, :].rearrange("p a n -> p (a n)")
        attention_sems = {n: sem("A_" + n if isinstance(n, str) else f"A_{n[0]}{n[1]}") for n in Attention.NAMES}
        ffn_sems = {n: sem("F_" + n if isinstance(n, str) else f"F_{n[0]}{n[1]}") for n in FeedForward.NAMES}
        LA = {0: Attention(0, 0, attention_sems, {})}
        LA[2] = Attention(2, 4, attention_sems, LA[0].events.after)
        LA[3] = Attention(3, 6, attention_sems, LA[2].events.after)
        a2 = flat[:, T + 11 * P + D:T + 11 * P + D + 11 * 16]
        b2 = flat[0:16, T + 11 * P:T + 11 * P + D]
        F0 = FeedForward("F0", 1, "silu", 11, ffn_sems, {}, small=[
            (flat[0:16, T:T + 11 * P], ins["F0_b1"]), (flat[32:48, T:T + 11 * P], ins["F0_b3"]),
            (b2, ins["F0_b2"]), (a2, ins["F0_a2"])])
        F1 = FeedForward("F1", 3, "pick", 14, ffn_sems, F0.events.after,
                         small=[(flat[0:16, T:T + 14 * P], ins["F1_c2"])])
        F3 = FeedForward("F3", 7, "gelu", 16, ffn_sems, F1.events.after, row=2)
        L1 = small_attention(sem)
        M2 = mixture(sem)
        LA[0].before = None
        F0.before, F1.before, F3.before = (LA[0].events, B * NPAIR), (F0.events, B * 6), (LA[3].events, B * NPAIR)
        LA[2].before = (F1.events, B * 7)
        LA[3].before = None

        def pe_matmuls(pe, bank_ap, w_ap, rhs, chunks=DC, first=True, last=True):
            for c in range(chunks):
                for n, (a, b) in enumerate(PASSES):
                    mm = pe.matmul(bank_ap, w_ap(a, c), rhs(b, c), start=first and c == 0 and n == 0,
                                   stop=last and c == chunks - 1 and n == len(PASSES) - 1)
            return mm

        def pe_project(pe, w, slot, actT, half):
            return pe_matmuls(pe, proj[half][:, :], lambda a, c: w[:, slot, a, c * P:(c + 1) * P],
                              lambda b, c: actT[:, b, c, half * HALF:(half + 1) * HALF])

        def pe_out(pe, b, slots, last=True):
            for n, s in enumerate(slots):
                mm = pe_matmuls(pe, outp[b % 2][:, :], lambda a, c: acts[:, s, a, b * S:(b + 1) * S],
                                lambda a, c: w_out[:, s, a, :], chunks=1, first=n == 0,
                                last=last and n == len(slots) - 1)
            return mm

        def dve_rsqrt(dve, y, arg, tmp, shifted, newton, calls):
            base = calls * 9
            dve.tensor_scalar(tmp.bitcast(I32), arg.bitcast(I32), 1, None, ALU.logical_shift_right).then_inc(shifted, 1)
            dve.wait_ge(shifted, calls * 2 + 1)
            dve.tensor_scalar(y.bitcast(I32), tmp.bitcast(I32), -1.0, float(RSQRT_MAGIC), ALU.mult,
                              ALU.add).then_inc(shifted, 1)
            dve.wait_ge(shifted, calls * 2 + 2)
            for n in range(3):
                dve.scalar_tensor_tensor(tmp, y, -0.5, y, ALU.mult, ALU.mult).then_inc(newton, 1)
                dve.wait_ge(newton, base + (3 * n + 1))
                dve.tensor_tensor(tmp, tmp, arg, ALU.mult).then_inc(newton, 1)
                dve.wait_ge(newton, base + (3 * n + 2))
                dve.scalar_tensor_tensor(y, tmp, 1.5, y, ALU.add, ALU.mult).then_inc(newton, 1)
                dve.wait_ge(newton, base + (3 * n + 3))

        normed = [tbuf[:, 0, :], tbuf[:, 1, :], pbuf[:, 0, :], pbuf[:, 1, :]]
        ln_banks = [turn, heado]
        ln_calls = [0]
        LN_CALLS_AT_L1 = 4 + 2 + 2
        LN_STAGES = [0, 1, 3, 4, 5, 6, 7]

        def ln_no(n):
            return LN_STAGES.index(n)

        def dve_ln_stats(dve, n, b):
            dve.bn_stats(stats[:, b, :], x[:, b, :]).then_inc(ln_stats, 1)
            dve.wait_ge(ln_stats, 8 * n + b + 1)
            dve.bn_aggr(moments[:, b, :], stats[:, b, :]).then_inc(ln_moments, 1)

        def dve_ln_rstd(dve, n, half):
            cols = slice(half * BH, half * BH + BH)
            dve.wait_ge(ln_moments, 8 * n + half * BH + BH)
            dve.tensor_scalar(nw_v[:, cols], moments[:, cols, 1], EPS, None, ALU.add).then_inc(ln_rstd, 1)
            dve.wait_ge(ln_rstd, 2 * n + half + 1)
            dve_rsqrt(dve, rstd[:, cols], nw_v[:, cols], nw_t[:, cols], ln_shifted, ln_newton, ln_calls[0])
            ln_calls[0] += 1
            if n == 0:
                dve.scalar_tensor_tensor(rrms[:, cols], rstd[:, cols], 1.0, rstd[:, cols], ALU.mult,
                                         ALU.mult).then_inc(ln_rms, 1)
                dve.wait_ge(ln_rms, 3 * half + 1)
                dve.tensor_tensor(rrms[:, cols], rrms[:, cols], moments[:, cols, 1], ALU.mult).then_inc(ln_rms, 1)
                dve.wait_ge(ln_rms, 3 * half + 2)
                dve.tensor_scalar(nw_v[:, cols], rrms[:, cols], EPS, None, ALU.add).then_inc(ln_rms, 1)
                dve.wait_ge(ln_rms, 3 * half + 3)
                dve_rsqrt(dve, rrms[:, cols], nw_v[:, cols], nw_t[:, cols], ln_shifted, ln_newton, ln_calls[0])
                ln_calls[0] += 1

        def dve_ln_norm(dve, n, b):
            m = ln_no(n)
            out_ap = normed[b % 4]
            if b >= 4:
                dve.wait_ge(ln_full, 8 * m + b - 3)
            norm = dve.tensor_scalar(out_ap, x[:, b, :], moments[:, b, 0:1], rstd[:, b:b + 1], ALU.subtract, ALU.mult)
            if n == 0:
                norm.then_inc(ln_kept, 1)
                dve.wait_ge(ln_kept, 2 * b + 1)
                dve.tensor_tensor(x[:, b, :], x[:, b, :], out_ap, ALU.add).then_inc(ln_kept, 1)
                dve.wait_ge(ln_kept, 2 * b + 2)
                dve.tensor_scalar(out_ap, out_ap, rrms[:, b:b + 1], None, ALU.mult).then_inc(ln_normed, 1)
            else:
                norm.then_inc(ln_normed, 1)

        def pe_ln_turn(pe, n, b):
            m = ln_no(n)
            pe.wait_ge(ln_normed, 8 * m + b + 1)
            if b >= 2:
                pe.wait_ge(ln_low, 8 * m + b - 1)
            for c in range(DC):
                mm = pe.transpose(ln_banks[b % 2][:, c * P:(c + 1) * P], normed[b % 4][:, c * P:(c + 1) * P], ident)
            mm.then_inc(ln_full, 1)

        def act_ln_high(act, n, b):
            m = ln_no(n)
            act.wait_ge(ln_full, 8 * m + b + 1)
            src = ln_banks[b % 2][:, :].rearrange("p (c t) -> p c t", c=DC)
            if n == 0:
                for c in range(DC):
                    a = act.activation(xnT[:, 0, c, b * S:(b + 1) * S], src[:, c, :], ACT.Copy,
                                       scale=vecs[:, V_LNW + c:V_LNW + c + 1])
            else:
                a = act.activation(xnT[:, 0, :, b * S:(b + 1) * S], src, ACT.Copy)
            a.then_inc(ln_high, 1)

        def dve_ln_low(dve, n, b):
            m = ln_no(n)
            dve.wait_ge(ln_high, 8 * m + b + 1)
            src = ln_banks[b % 2][:, :].rearrange("p (c t) -> p c t", c=DC)
            if n == 0:
                for c in range(DC):
                    a = dve.scalar_tensor_tensor(xnT[:, 1, c, b * S:(b + 1) * S], src[:, c, :],
                                                 vecs[:, V_LNW + c:V_LNW + c + 1],
                                                 xnT[:, 0, c, b * S:(b + 1) * S].bitcast(F32), ALU.mult, ALU.subtract)
            else:
                a = dve.tensor_tensor(xnT[:, 1, :, b * S:(b + 1) * S], src, xnT[:, 0, :, b * S:(b + 1) * S].bitcast(F32),
                                      ALU.subtract)
            a.then_inc(ln_low, 1)

        def pe_tail(pe, n, out_of):
            for b in range(B):
                if out_of:
                    out_of(b)
                if n in LN_STAGES and b >= 4:
                    pe_ln_turn(pe, n, b - 4)
            if n in LN_STAGES:
                for b in range(4, B):
                    pe_ln_turn(pe, n, b)

        def act_tail(act, n):
            if n in LN_STAGES:
                for b in range(B):
                    act_ln_high(act, n, b)

        def dve_tail(dve, n, add_of):
            for b in range(B):
                if add_of:
                    add_of(b)
                if n > 7:
                    continue
                dve_ln_stats(dve, n, b)
                if b == BH - 1:
                    dve_ln_rstd(dve, n, 0)
                    if n in LN_STAGES:
                        for k in range(4):
                            dve_ln_norm(dve, n, k)
                elif b >= BH and n in LN_STAGES:
                    dve_ln_low(dve, n, b - BH)
            if n > 7:
                return
            dve_ln_rstd(dve, n, 1)
            if n in LN_STAGES:
                for b in range(4, B):
                    dve_ln_norm(dve, n, b)
                for b in range(4, B):
                    dve_ln_low(dve, n, b)

        def attention_sp(sp, A):
            m = A.events
            wk, wv, wq, wo = (ins[f"L{A.layer}_{k}"] for k in ("wk", "wv", "wq", "wo"))

            def load(g, j, what, source):
                n = A.tile(g, j, what)
                slot = A.tile(0, j, what) % A.ring
                m.wait(sp, "split", n - (A.ring - 1))
                sp.dma_start(ring[:, slot, :], source).then_inc(m["landed", slot], 16)

            def group(g):
                for j in range(GH):
                    h = GH * g + j
                    kv = h if A.own_kv else g
                    if A.layer == 0:
                        m.wait(sp, "masked", 2 * h - 2)
                        sp.dma_start(biasbuf[:, j % 2, :], ins["position_bias"][bass.ds(h, 1)].rearrange("a p n -> (a p) n"))\
                          .then_inc(m["bias_landed", j % 2], 16)
                    if A.new_kv(j):
                        load(g, j, "k", wk[bass.ds(kv, 1)].rearrange("a p n -> (a p) n"))
                        load(g, j, "v", wv[bass.ds(kv, 1)].rearrange("a p n -> (a p) n"))
                    load(g, j, "q", wq[bass.ds(h, 1)].rearrange("a p n -> (a p) n"))
                    load(g, j, "o", wo[bass.ds(h, 1)].rearrange("a p n -> (a p) n"))

            group(0)
            with sp.Fori(1, NG) as g:
                group(g)

        def attention_pool(pool, A):
            m = A.events

            def split(g, j, what, dst, slot):
                n = A.tile(g, j, what)
                pos = A.tile(0, j, what)
                r = pos % A.ring
                m.wait(pool, ("landed", r), 16 * ((A.tiles // A.ring) * g + (pos // A.ring + 1)))
                pool.tensor_tensor(dst[:, slot, 0, :], ring[:, r, :], zeros512, ALU.add).then_inc(m["high_w"], 1)
                m.wait(pool, "high_w", n + 1)
                pool.tensor_tensor(dst[:, slot, 1, :], ring[:, r, :], dst[:, slot, 0, :].bitcast(F32),
                                   ALU.subtract).then_inc(m["split"], 1)

            def square(g, j, what, src):
                n = A.projection(g, j, what)
                for half in range(2):
                    m.wait(pool, ("pfree", half), n + 1)
                if what == "k":
                    if not (isinstance(g, int) and g == 0):
                        m.wait(pool, "tfull", A.turn(g - 1, 2, "Q") + 1)
                elif j == 0:
                    m.wait(pool, "tfull", A.turn(g - 1, 3, "K") + 1)
                elif j == 1:
                    m.wait(pool, "tfull", A.turn(g - 1, 3, "Q") + 1)
                else:
                    m.wait(pool, "tfull", A.turn(g, j - 2, "Q") + 1)
                pool.tensor_tensor(sq[:, :], src, src, ALU.mult).then_inc(m["squared"], 1)

            def group(g):
                first = isinstance(g, int)
                for j in range(GH):
                    if A.new_kv(j):
                        if not (first and j == 0):
                            before = (g, j - 1) if A.own_kv and j else (g - 1, GH - 1 if A.own_kv else 0)
                            m.wait(pool, ("pfull", 1), A.projection(*before, "k") + 1)
                        split(g, j, "k", w_kv, 0)
                        if not (first and j == 0):
                            m.wait(pool, ("pfull", 1), A.projection(*before, "v") + 1)
                        split(g, j, "v", w_kv, 1)
                    if not (first and j < 2):
                        before = (g, j - 2) if j >= 2 else (g - 1, j + 2)
                        m.wait(pool, ("pfull", 1), A.projection(*before, "q") + 1)
                    split(g, j, "q", w_in, j % 2)
                    if not first:
                        m.wait(pool, "outfull", B * (2 * g + (j // 2 - 1)))
                    split(g, j, "o", w_out, j)
                    if A.normed:
                        if j == 0:
                            square(g, j, "k", kT)
                        square(g, j, "q", qT)

            if A.before:
                A.before[0].wait(pool, "outfull", A.before[1])
            if A.layer == 3:
                pool.wait_ge(M2["outfull"], B)
            group(0)
            with pool.Fori(1, NG) as g:
                group(g)

        def after(g, j):
            return (g, j + 1) if j < GH - 1 else (g + 1, 0)

        def needed_next(A, j):
            return "kvq" if A.new_kv((j + 1) % GH) else "q"

        def attention_pe(pe, A):
            m = A.events
            unit = lambda g, j, half: 2 * (GH * g + j) + half

            def project(g, j, what):
                n = A.projection(g, j, what)
                w, slot, act = {"k": (w_kv, 0, ctxT), "v": (w_kv, 1, ctxT), "q": (w_in, j % 2, xnT)}[what]
                m.wait(pe, "split", A.tile(g, j, what) + 1)
                for half in range(2):
                    m.wait(pe, ("pfree", half), n)
                    if what == "q" and isinstance(g, int) and g == 0 and j == 0:
                        pe.wait_ge(ln_low, 8 * ln_no(A.stage) + BH * (half + 1))
                    pe_project(pe, w, slot, act, half).then_inc(m["pfull", half], 1)

            def use_turn(n):
                m.wait(pe, "tfree", n)

            def turn_values(g, j):
                for half in range(2):
                    n = A.turn(g, j, f"V{half}")
                    use_turn(n)
                    if half == 0:
                        k = A.projection(*after(g, j), "v") if not (isinstance(g, int) and g < 0) else 1
                        for i in range(2):
                            m.wait(pe, ("pfree", i), k + 1)
                    for b in range(BH):
                        mm = pe.transpose(turn[:, b * P:(b + 1) * P], vT[:, (half * BH + b) * S:(half * BH + b + 1) * S], ident)
                    mm.then_inc(m["tfull"], 1)

            def sum_squares(g, j, what, g2, j2):
                use_turn(A.turn(g, j, what))
                m.wait(pe, "squared", 5 * g2 + (1 if what == "K" else 2 + j2))
                for b in range(B):
                    mm = pe.matmul(turn[:, b:b + 1], sq[:, b * S:(b + 1) * S], consts[:, C_MEAN:C_MEAN + 1],
                                   start=True, stop=True)
                mm.then_inc(m["tfull"], 1)

            def spread(g, j, g2):
                for half in range(2):
                    use_turn(A.turn(g, j, f"B{half}"))
                    m.wait(pe, "diag", 2 * g2 + (half + 1))
                    for b in range(BH):
                        mm = pe.matmul(turn[:, b * P:(b + 1) * P], ones, ptbuf[:, half, b * P:(b + 1) * P],
                                       start=True, stop=True)
                    mm.then_inc(m["tfull"], 1)

            def out_product(g, pair, bs):
                p = 2 * g + pair
                if bs[0] == 0:
                    m.wait(pe, "low", 4 * (p + 1))
                    m.wait(pe, "split", A.tile(g, 2 * pair + 1, "o") + 1)
                for b in bs:
                    m.wait(pe, "added", B * p + (b - 1))
                    pe_out(pe, b, (2 * pair, 2 * pair + 1)).then_inc(m["outfull"], 1)

            def step(g, j, first=False, last=False):
                h = GH * g + j
                kv = h if A.own_kv else g
                more = not (last and j == GH - 1)
                new = needed_next(A, j) if more else ""
                for half in range(2):
                    u = unit(g, j, half)
                    if half == 0:
                        for i in range(2):
                            m.wait(pe, ("pfree", i), A.projection(g, j, "q") + 1)
                        if A.normed:
                            m.wait(pe, "tfree", A.turn(g - 1, 3, "B1") + 1)
                    m.wait(pe, "exps" if A.layer == 3 else "sfree", u - 1)
                    for b in range(BH):
                        t = slice((half * BH + b) * S, (half * BH + b + 1) * S)
                        mm = pe.matmul(score[half][:, b * P:(b + 1) * P], qT[:, t], kT[:, t], start=True, stop=True)
                    mm.then_inc(m["sfull"], 1)
                for what in new:
                    project(*after(g, j), what)
                if A.normed and "k" in new:
                    sum_squares(g, j, "K", g + 1, 0)
                for half in range(2):
                    n = A.turn(g, j, f"T{half}")
                    use_turn(n)
                    m.wait(pe, "pready", unit(g, j, half) + 1)
                    for b in range(BH):
                        mm = pe.transpose(turn[:, b * P:(b + 1) * P], pbuf[:, half, b * P:(b + 1) * P], ident)
                    mm.then_inc(m["tfull"], 1)
                    if half == 0 and j % 2 == 0 and not (first and j == 0):
                        out_product(g if j else g - 1, 0 if j else 1, range(0, BH))
                    if half == 1 and j % 2 == 0 and not (first and j == 0):
                        out_product(g if j else g - 1, 0 if j else 1, range(BH, B))
                    m.wait(pe, "tfree", n + 1)
                    m.wait(pe, "low", unit(g, j, half))
                    for b in range(BH):
                        mm = pe.matmul(heado[:, b * P:(b + 1) * P], v[:, (half * BH + b) * S:(half * BH + b + 1) * S],
                                       ptbuf[:, half, b * P:(b + 1) * P], start=True, stop=True)
                    mm.then_inc(m["pv"], 1)
                if "v" in new:
                    turn_values(g, j)
                if A.normed and more:
                    sum_squares(g, j, "Q", *after(g, j))
                    if "k" in new:
                        spread(g, j, g + 1)

            def group(g, first=False, last=False):
                for j in range(GH):
                    step(g, j, first, last)

            project(0, 0, "k")
            project(0, 0, "v")
            if A.normed:
                sum_squares(-1, 3, "K", 0, 0)
            turn_values(-1, 3)
            project(0, 0, "q")
            if A.normed:
                sum_squares(-1, 3, "Q", 0, 0)
                spread(-1, 3, 0)
            group(0, first=True)
            with pe.Fori(1, NG - 1) as g:
                group(g)
            group(NG - 1, last=True)
            pe_tail(pe, A.stage + 1, lambda b: out_product(NG - 1, 1, [b]))

        def copy_projection(engine, on_act, dst, src, bias):
            if on_act:
                if bias is None:
                    return engine.activation(dst, src, ACT.Copy)
                return engine.activation(dst, src, ACT.Identity, bias=bias)
            if bias is None:
                return engine.tensor_copy(dst, src)
            return engine.tensor_scalar(dst, src, bias, None, ALU.add)

        def take_projection(engine, on_act, A, g, j, what):
            m = A.events
            half = 0 if on_act else 1
            m.wait(engine, ("pfull", half), A.projection(g, j, what) + 1)
            dst = {"k": kT, "v": vT, "q": qT}[what][:, half * HALF:(half + 1) * HALF]
            bias = None
            if A.layer == 3:
                base, n = {"k": (V_BK3, g), "v": (V_BV3, g), "q": (V_BQ3, GH * g + j)}[what]
                bias = vecs[:, bass.ds(base + n, 1)]
            copy_projection(engine, on_act, dst, proj[half][:, :], bias).then_inc(m["pfree", half], 1)

        def take_values(engine, on_act, A, g, j):
            m = A.events
            half = 0 if on_act else 1
            m.wait(engine, "tfull", A.turn(g, j, f"V{half}") + 1)
            dst = v[:, half * HALF:(half + 1) * HALF]
            copy_projection(engine, on_act, dst, turn[:, :], None).then_inc(m["tfree"], 1)

        def attention_act(act, A):
            m = A.events

            def step(g, j, last=False):
                more = not (last and j == GH - 1)
                new = needed_next(A, j) if more else ""
                for half in range(2):
                    u = 2 * (GH * g + j) + half
                    src = score[half] if A.layer == 3 else tbuf[:, half, :]
                    scale = A.scale if A.layer == 3 else 1.0
                    m.wait(act, "negmax", u + 1)
                    for b in range(BH):
                        a = act.activation(pbuf[:, half, b * P:(b + 1) * P], src[:, b * P:(b + 1) * P], ACT.Exp,
                                           bias=negmax[:, half, b:b + 1], scale=scale,
                                           accum_out=rowsum[:, half, b:b + 1])
                    a.then_inc(m["exps"], 1)
                for what in new:
                    take_projection(act, True, A, *after(g, j), what)
                for half in range(2):
                    u = 2 * (GH * g + j) + half
                    m.wait(act, "tfull", A.turn(g, j, f"T{half}") + 1)
                    act.activation(ptbuf[:, half, :], turn[:, :], ACT.Copy).then_inc(m["tfree"], 1)
                    m.wait(act, "pv", u + 1)
                    act.activation(acts[:, j, 0, half * HALF:(half + 1) * HALF], heado[:, :], ACT.Copy)\
                       .then_inc(m["high"], 1)
                if "v" in new:
                    take_values(act, True, A, g, j)

            def group(g, last=False):
                for j in range(GH):
                    step(g, j, last)

            for what in "kv":
                take_projection(act, True, A, 0, 0, what)
            take_values(act, True, A, -1, 3)
            take_projection(act, True, A, 0, 0, "q")
            group(0)
            with act.Fori(1, NG - 1) as g:
                group(g)
            group(NG - 1, last=True)
            act_tail(act, A.stage + 1)

        def attention_dve(dve, A):
            m = A.events

            def scores(g, j, half):
                h = GH * g + j
                u = 2 * h + half
                blocks = lambda ap: ap.rearrange("p (b k) -> p b k", b=BH)
                m.wait(dve, "sfull", u + 1)
                src = blocks(score[half][:, :])
                if A.layer == 0:
                    if half == 0:
                        m.wait(dve, ("bias_landed", j % 2), 16 * (2 * g + (j // 2 + 1)))
                    t = blocks(tbuf[:, half, :])
                    dve.tensor_tensor(t, src, biasbuf[:, j % 2:j % 2 + 1, :].broadcast_to([P, BH, S]), ALU.add)\
                       .then_inc(m["sfree"], 1)
                    m.wait(dve, "sfree", u + 1)
                    dve.tensor_tensor(t, t, maskadd[:, half * BH:(half + 1) * BH, :], ALU.add).then_inc(m["masked"], 1)
                    m.wait(dve, "masked", u + 1)
                    src = t
                elif A.layer == 2:
                    for b in range(BH):
                        n = half * BH + b
                        a = dve.scalar_tensor_tensor(tbuf[:, half, b * P:(b + 1) * P], score[half][:, b * P:(b + 1) * P],
                                                     rq[:, n:n + 1], maskadd[:, 0, :], ALU.mult, ALU.add)
                    a.then_inc(m["sfree"], 1)
                    m.wait(dve, "sfree", u + 1)
                    src = blocks(tbuf[:, half, :])
                dve.tensor_reduce(rowmax[:, half, 0:BH], src, AX.X, ALU.max).then_inc(m["rowmax"], 1)
                m.wait(dve, "rowmax", u + 1)
                dve.tensor_scalar(negmax[:, half, 0:BH], rowmax[:, half, 0:BH], -A.scale if A.layer == 3 else -1.0,
                                  None, ALU.mult).then_inc(m["negmax"], 1)

            def normalise(g, j, half):
                u = 2 * (GH * g + j) + half
                m.wait(dve, "exps", u + 1)
                dve.reciprocal(rinv[:, half, 0:BH], rowsum[:, half, 0:BH]).then_inc(m["rinv"], 1)
                m.wait(dve, "rinv", u + 1)
                if A.layer == 0:
                    dve.tensor_tensor(rinv[:, half, 0:BH], rinv[:, half, 0:BH], live[:, half * BH:(half + 1) * BH],
                                      ALU.mult).then_inc(m["rlive"], 1)
                    m.wait(dve, "rlive", u + 1)
                pb = pbuf[:, half, :].rearrange("p (b k) -> p b k", b=BH)
                dve.tensor_tensor(pb, pb, rinv[:, half, 0:BH].unsqueeze(2).broadcast_to([P, BH, S]), ALU.mult)\
                   .then_inc(m["pready"], 1)

            def rms(g, j, what):
                order = {"K": 3, "Q": 4 if j == 3 else j}[what]
                calls = ({"K": 0, "Q": 1}[what]) if isinstance(g, int) and g < 0 else 2 + 5 * g + order
                dst = rk if what == "K" else rq
                m.wait(dve, "tfull", A.turn(g, j, what) + 1)
                dve.tensor_scalar(nw_v[:, :], turn[:, 0:B], EPS, None, ALU.add).then_inc(m["tfree"], 1)
                m.wait(dve, "tfree", A.turn(g, j, what) + 1)
                dve_rsqrt(dve, dst[:, :], nw_v[:, :], nw_t[:, :], m["shifted"], m["newton"], calls)
                if what == "Q":
                    dve.tensor_scalar(rq[:, :], rq[:, :], A.scale, None, ALU.mult).then_inc(m["rsq"], 1)
                    m.wait(dve, "rsq", (0 if isinstance(g, int) and g < 0 else GH * g + (j + 1)) + 1)

            def norm_keys(g, j, g2):
                for half in range(2):
                    for b in range(BH):
                        a = dve.tensor_scalar(ptbuf[:, half, b * P:(b + 1) * P], ident,
                                              rk[:, half * BH + b:half * BH + b + 1], None, ALU.mult)
                    a.then_inc(m["diag"], 1)
                for half in range(2):
                    cols = slice(half * HALF, (half + 1) * HALF)
                    m.wait(dve, "tfull", A.turn(g, j, f"B{half}") + 1)
                    for i in range(2):
                        m.wait(dve, ("pfree", i), A.projection(g2, 0, "k") + 1)
                    dve.scalar_tensor_tensor(kT[:, cols], kT[:, cols], kqn[:, 0:1], turn[:, :], ALU.mult, ALU.mult)\
                       .then_inc(m["tfree"], 1)
                    m.wait(dve, "tfree", A.turn(g, j, f"B{half}") + 1)

            def add(p, b):
                m.wait(dve, "added", B * p + (b - B + 1))
                m.wait(dve, "outfull", B * p + (b + 1))
                dve.tensor_tensor(x[:, b, :], x[:, b, :], outp[b % 2][:, :], ALU.add).then_inc(m["added"], 1)

            def step(g, j, first=False, last=False):
                more = not (last and j == GH - 1)
                new = needed_next(A, j) if more else ""
                for half in range(2):
                    scores(g, j, half)
                for half in range(2):
                    normalise(g, j, half)
                for what in new:
                    take_projection(dve, False, A, *after(g, j), what)
                if A.normed and "k" in new:
                    rms(g, j, "K")
                for half in range(2):
                    if j % 2 == 0 and not (first and j == 0):
                        p = 2 * g + (0 if j else -1)
                        for b in range(half * BH, (half + 1) * BH):
                            add(p, b)
                    u = 2 * (GH * g + j) + half
                    m.wait(dve, "high", u + 1)
                    cols = slice(half * HALF, (half + 1) * HALF)
                    dve.tensor_tensor(acts[:, j, 1, cols], heado[:, :], acts[:, j, 0, cols].bitcast(F32), ALU.subtract)\
                       .then_inc(m["low"], 1)
                if "v" in new:
                    take_values(dve, False, A, g, j)
                if A.normed and more:
                    rms(g, j, "Q")
                    if "k" in new:
                        norm_keys(g, j, g + 1)

            def group(g, first=False, last=False):
                for j in range(GH):
                    step(g, j, first, last)

            if A.layer == 3:
                add_row(dve, 1)
            for what in "kv":
                take_projection(dve, False, A, 0, 0, what)
            if A.normed:
                rms(-1, 3, "K")
            take_values(dve, False, A, -1, 3)
            take_projection(dve, False, A, 0, 0, "q")
            if A.normed:
                rms(-1, 3, "Q")
                norm_keys(-1, 3, 0)
            group(0, first=True)
            with dve.Fori(1, NG - 1) as g:
                group(g)
            group(NG - 1, last=True)

            def last_add(b):
                add(NPAIR - 1, b)
                m.wait(dve, "added", B * (NPAIR - 1) + b + 1)

            dve_tail(dve, A.stage + 1, last_add)

        def ffn_run(engine, A, emit):
            last = (A.chunks - 1) // GH
            emit(0, range(GH))
            if last > 2:
                with engine.Fori(1, last) as g:
                    emit(g, range(GH))
            else:
                emit(1, range(GH))
            emit(last, range(A.chunks - GH * last))

        def ffn_sp(sp, A):
            m = A.events
            if A.low_rank:
                sp.dma_start(brow[:, :], ins[f"{A.name}_pre"]).then_inc(m["pre_landed"], 16)
                for dst, src in A.small:
                    sp.dma_start(dst, src).then_inc(m["small_landed"], 16)

            def chunks(g, js):
                for j in js:
                    c = GH * g + j
                    for k, what in enumerate(A.what):
                        n = A.tile(g, j, k)
                        slot = (len(A.what) * j + k) % A.ring
                        m.wait(sp, "split", n - (A.ring - 1))
                        sp.dma_start(ring[:, slot, :], ins[f"{A.name}_{what}"][bass.ds(c, 1)].rearrange("a p n -> (a p) n"))\
                          .then_inc(m["landed", slot], 16)

            ffn_run(sp, A, chunks)

        def ffn_pool(pool, A):
            m = A.events

            def tiles_of(g, j):
                for k, what in enumerate(A.what):
                    r = (len(A.what) * j + k) % A.ring
                    n = A.tile(g, j, k)
                    early = isinstance(g, int) and g == 0
                    if what == "in":
                        dst = w_in[:, j % 2]
                        if not (early and j < 2):
                            m.wait(pool, ("pfull", 1), GH * g + (j - 2 + A.low_rank + 1))
                    elif what == "in2":
                        dst = w_kv[:, j % 2]
                        if not (early and j < 2):
                            m.wait(pool, "sfull", 2 * (GH * g + (j - 2)) + 2)
                        elif j == 1 and A.low_rank:
                            m.wait(pool, ("pfull", 1), 1)
                    else:
                        dst = w_out[:, j]
                        if not early:
                            m.wait(pool, "outfull", B * (2 * g + (j // 2 - 1)))
                    m.wait(pool, ("landed", r), 16 * ((GH * len(A.what) // A.ring) * g + ((len(A.what) * j + k) // A.ring + 1)))
                    pool.tensor_tensor(dst[:, 0, :], ring[:, r, :], zeros512, ALU.add).then_inc(m["high_w"], 1)
                    m.wait(pool, "high_w", n + 1)
                    pool.tensor_tensor(dst[:, 1, :], ring[:, r, :], dst[:, 0, :].bitcast(F32), ALU.subtract)\
                        .then_inc(m["split"], 1)

            def chunks(g, js):
                for j in js:
                    c = GH * g + j
                    if not (isinstance(c, int) and c == A.chunks - 1):
                        tiles_of(*after(g, j))
                    for half in range(2):
                        if A.kind == "pick":
                            u = 2 * c + half
                            m.wait(pool, "equal", u + 1)
                            e = ptbuf[:, half, :].rearrange("p (k i) -> p k i", i=32)
                            pool.tensor_tensor(e, e, consts[:, C_FIRST:C_FIRST + 32].unsqueeze(1).broadcast_to([P, 16, 32]),
                                               ALU.mult).then_inc(m["weighed"], 1)
                    for half in range(2):
                        u = 2 * c + half
                        m.wait(pool, "made", u + 1)
                        if not (isinstance(g, int) and g == 0):
                            m.wait(pool, "outfull", B * (2 * g + (j // 2 - 1)))
                        pool.tensor_tensor(acts[:, j, 0, half * HALF:(half + 1) * HALF], pbuf[:, half, :], zeros512,
                                           ALU.add).then_inc(m["high"], 1)

            A.before[0].wait(pool, "outfull", A.before[1])
            if A.low_rank:
                m.wait(pool, "pre_landed", 16)
                pool.tensor_tensor(w_kv[:, 1, 0, :], brow[:, :], zeros512, ALU.add).then_inc(m["pre_split"], 1)
                m.wait(pool, "pre_split", 1)
                pool.tensor_tensor(w_kv[:, 1, 1, :], brow[:, :], w_kv[:, 1, 0, :].bitcast(F32), ALU.subtract)\
                    .then_inc(m["pre_split"], 1)
            tiles_of(0, 0)
            ffn_run(pool, A, chunks)

        def ffn_pe(pe, A):
            m = A.events
            pre = int(A.low_rank)
            low = big[0:48, 0, :]

            def second_low(g, j):
                c = GH * g + j
                for half in range(2):
                    m.wait(pe, "made", 2 * c + half + 1)
                    mm = pe.matmul(ln_banks[half][0:16, :], a2[:, c * 16:(c + 1) * 16], pbuf[:, half, :], start=isinstance(c, int) and c == 0,
                                   stop=isinstance(c, int) and c == A.chunks - 1)
                    mm.then_inc(m["lowfull"], 1)

            def out_product(p, slots, bs, last):
                if bs[0] == 0:
                    m.wait(pe, "low", 4 * p + 2 * len(slots))
                    m.wait(pe, "split", A.out_tile(p, slots))
                for b in bs:
                    m.wait(pe, "added", B * p + (b - 1))
                    more = last and A.kind == "silu"
                    mm = pe_out(pe, b, slots, last=not more)
                    if more:
                        if b == 0:
                            m.wait(pe, "low2", 2)
                        mm = pe.matmul(outp[b % 2][:, :], sq[0:16, b * S:(b + 1) * S], b2, start=False, stop=True)
                    mm.then_inc(m["outfull"], 1)

            def chunks(g, js):
                for j in js:
                    c = GH * g + j
                    first = isinstance(c, int) and c == 0
                    if A.kind == "pick":
                        for half in range(2):
                            if half == 0:
                                m.wait(pe, "equal", 2 * c)
                            for b in range(BH):
                                t = half * BH + b
                                mm = pe.matmul(score[half][:, b * P:(b + 1) * P], low[0:16, t * S:(t + 1) * S],
                                               flat[0:16, bass.ds(T + P * c, P)], start=True, stop=True)
                            mm.then_inc(m["sfull"], 1)
                    m.wait(pe, "split", A.tile(g, j, 0) + 1)
                    for half in range(2):
                        if A.kind == "gelu":
                            m.wait(pe, "made", 2 * c + half - 1)
                        else:
                            m.wait(pe, ("pfree", half), c + pre)
                        mm = pe_matmuls(pe, proj[half][:, :], lambda a, k: w_in[:, j % 2, a, k * P:(k + 1) * P],
                                        lambda b, k: xnT[:, b, k, half * HALF:(half + 1) * HALF], last=A.kind != "silu")
                        if A.kind == "silu":
                            mm = pe.matmul(proj[half][:, :], flat[0:16, T + c * P:T + (c + 1) * P], big[0:16, 0, half * HALF:(half + 1) * HALF],
                                           start=False, stop=True)
                        mm.then_inc(m["pfull", half], 1)
                    if A.kind == "silu":
                        if not first:
                            second_low(*((g, j - 1) if j else (g - 1, GH - 1)))
                        m.wait(pe, "split", A.tile(g, j, 1) + 1)
                        for half in range(2):
                            m.wait(pe, "made", 2 * c + half - 1)
                            pe_matmuls(pe, score[half][:, :], lambda a, k: w_kv[:, j % 2, a, k * P:(k + 1) * P],
                                       lambda b, k: xnT[:, b, k, half * HALF:(half + 1) * HALF], last=False)
                            pe.matmul(score[half][:, :], flat[32:48, T + c * P:T + (c + 1) * P], big[32:48, 0, half * HALF:(half + 1) * HALF],
                                      start=False, stop=True).then_inc(m["sfull"], 1)
                    if j % 2 == 0 and not first:
                        out_product(2 * g + (0 if j else -1), (0, 1) if j else (2, 3), range(B), False)
                    if A.kind == "pick":
                        for half in range(2):
                            m.wait(pe, "made", 2 * c + half - 1)
                            m.wait(pe, "picked", 2 * c + half + 1)
                            for b in range(BH):
                                mm = pe.transpose(ln_banks[half][:, b * P:(b + 1) * P], ptbuf[:, half, b * P:(b + 1) * P],
                                                  ident)
                            mm.then_inc(m["tfull"], 1)

            if A.kind == "pick":
                m.wait(pe, "small_landed", 16)
            if A.low_rank:
                m.wait(pe, "pre_split", 2)
                m.wait(pe, "small_landed", 16 * len(A.small))
                for half in range(2):
                    pe.wait_ge(ln_low, 8 * ln_no(A.stage) + BH * (half + 1))
                    pe_project(pe, w_kv, 1, xnT, half).then_inc(m["pfull", half], 1)
                for half in range(2):
                    m.wait(pe, ("pfree", half), 1)
            else:
                pe.wait_ge(ln_low, 8 * ln_no(A.stage) + B)
            ffn_run(pe, A, chunks)
            if A.kind == "silu":
                second_low(*divmod(A.chunks - 1, GH))
            p = (A.chunks - 1) // 2
            s = 2 * (p % 2)
            slots = (s, s + 1) if A.chunks % 2 == 0 else (s,)
            pe_tail(pe, A.stage + 1, lambda b: out_product(p, slots, [b], True))

        def ffn_act(act, A):
            m = A.events
            pre = int(A.low_rank)

            def chunks(g, js):
                for j in js:
                    c = GH * g + j
                    for half in range(2):
                        m.wait(act, ("pfull", half), c + pre + 1)
                        if A.kind == "gelu":
                            m.wait(act, "low", 2 * c + half - 1)
                            a = act.activation(pbuf[:, half, :], proj[half][:, :], ACT.Gelu_apprx_tanh,
                                               bias=vecs[:, bass.ds(V_BI + 16 * half + c, 1)])
                            a.then_inc(m["made"], 1)
                            continue
                        m.wait(act, "made", 2 * c + half - 1)
                        act.activation(tbuf[:, half, :], proj[half][:, :], ACT.Silu if A.kind == "silu" else ACT.Relu)\
                           .then_inc(m["pfree", half], 1)

            if A.low_rank:
                for half in range(2):
                    m.wait(act, ("pfull", half), 1)
                    act.activation(big[0:48, 0, half * HALF:(half + 1) * HALF], proj[half][0:48, :], ACT.Copy,
                                   scale=2.0 if A.kind == "silu" else 1.0).then_inc(m["pfree", half], 1)
            ffn_run(act, A, chunks)
            if A.kind == "silu":
                m.wait(act, "lowfull", 2 * A.chunks)
                for half in range(2):
                    act.activation(sq[0:16, half * HALF:(half + 1) * HALF], ln_banks[half][0:16, :], ACT.Copy, scale=2.0)\
                       .then_inc(m["low2"], 1)
            act_tail(act, A.stage + 1)

        def ffn_dve(dve, A):
            m = A.events

            def add(p, b):
                m.wait(dve, "added", B * p + (b - B + 1))
                m.wait(dve, "outfull", B * p + (b + 1))
                dve.tensor_tensor(x[:, b, :], x[:, b, :], outp[b % 2][:, :], ALU.add).then_inc(m["added"], 1)

            def low_part(c, j, half):
                m.wait(dve, "high", 2 * c + half + 1)
                cols = slice(half * HALF, (half + 1) * HALF)
                dve.tensor_tensor(acts[:, j, 1, cols], pbuf[:, half, :], acts[:, j, 0, cols].bitcast(F32), ALU.subtract)\
                   .then_inc(m["low"], 1)

            def pick(c):
                blocks = lambda ap: ap.rearrange("p (k i) -> p k i", i=32)
                spread = lambda ap: ap.unsqueeze(2).broadcast_to([P, 16, 32])
                for half in range(2):
                    u = 2 * c + half
                    m.wait(dve, "sfull", u + 1)
                    dve.tensor_reduce(blockmax[:, half, :], blocks(score[half][:, :]), AX.X, ALU.max).then_inc(m["bmax"], 1)
                    m.wait(dve, "bmax", u + 1)
                    m.wait(dve, "tfull", u - 1)
                    dve.tensor_tensor(blocks(ptbuf[:, half, :]), blocks(score[half][:, :]), spread(blockmax[:, half, :]),
                                      ALU.is_equal).then_inc(m["equal"], 1)
                for half in range(2):
                    u = 2 * c + half
                    m.wait(dve, "weighed", u + 1)
                    dve.tensor_reduce(firstmax[:, half, :], blocks(ptbuf[:, half, :]), AX.X, ALU.max).then_inc(m["fmax"], 1)
                    m.wait(dve, "fmax", u + 1)
                    dve.tensor_tensor(blocks(ptbuf[:, half, :]), blocks(ptbuf[:, half, :]), spread(firstmax[:, half, :]),
                                      ALU.is_equal).then_inc(m["picked"], 1)

            def chunks(g, js):
                for j in js:
                    c = GH * g + j
                    first = isinstance(c, int) and c == 0
                    adds = [] if j % 2 or first else range(B)
                    p = 2 * g + (0 if j else -1)
                    if A.kind == "silu":
                        for half in range(2):
                            u = 2 * c + half
                            m.wait(dve, "sfull", u + 1)
                            m.wait(dve, ("pfree", half), c + 2)
                            m.wait(dve, "lowfull", u - 1)
                            m.wait(dve, "low", u - 1)
                            dve.tensor_tensor(pbuf[:, half, :], score[half][:, :], tbuf[:, half, :], ALU.mult)\
                               .then_inc(m["made"], 1)
                    if A.kind == "pick":
                        pick(c)
                        for b in adds:
                            add(p, b)
                        for half in range(2):
                            u = 2 * c + half
                            m.wait(dve, "tfull", u + 1)
                            m.wait(dve, ("pfree", half), c + 2)
                            m.wait(dve, "low", u - 1)
                            dve.tensor_tensor(pbuf[:, half, :], ln_banks[half][:, :], tbuf[:, half, :], ALU.mult)\
                               .then_inc(m["made"], 1)
                        adds = []
                    for b in list(adds)[:BH]:
                        add(p, b)
                    for half in range(2):
                        low_part(c, j, half)
                    for b in list(adds)[BH:]:
                        add(p, b)

            if A.row is not None:
                add_row(dve, A.row)
            ffn_run(dve, A, chunks)
            p = (A.chunks - 1) // 2

            def last_add(b):
                add(p, b)
                m.wait(dve, "added", B * p + b + 1)

            dve_tail(dve, A.stage + 1, last_add)

        def row_sp(sp, n, name):
            wait(sp, row_added, B * n)
            if n == 0:
                sp.wait_ge(L1["v_made"], B)
                sp.wait_ge(L1["out_full"], B)
            sp.dma_start(brow[:, :], ins[name].partition_broadcast(P)).then_inc(row_landed, 16)

        def add_row(dve, n):
            dve.wait_ge(row_landed, 16 * (n + 1))
            for b in range(B):
                dve.tensor_tensor(x[:, b, :], x[:, b, :], brow[:, :], ALU.add).then_inc(row_added, 1)
            dve.wait_ge(row_added, B * (n + 1))

        PATCH = D // P
        H1, DH1 = 8, 8
        E1 = H1 * DH1
        xn1 = [sq[:, i * D:(i + 1) * D] for i in range(2)]
        wq1, wk1, wv1 = (brow[:, i * E1:(i + 1) * E1] for i in range(3))
        wo1 = brow[0:E1, 3 * E1:3 * E1 + P]
        bv1 = brow[:, 3 * E1 + P:4 * E1 + P]
        q1 = maskadd[:, 0:BH, :].rearrange("p a n -> p (a n)")
        k1 = maskadd[:, BH:B, :].rearrange("p a n -> p (a n)")
        v1 = [ring[:, 4 + i, 0:PATCH * H1 * (DH1 + 1)].rearrange("p (n h d) -> p n h d", n=PATCH, h=H1)
              for i in range(2)]
        o1 = flat[:, 0:B * PATCH * E1]
        og = [flat[0:E1, B * PATCH * E1 + i * D:B * PATCH * E1 + (i + 1) * D] for i in range(2)]

        def in_pairs(engine, emit):
            for b in range(2):
                emit(b, b)
            with engine.Fori(1, B // 2) as i:
                for k in range(2):
                    emit(2 * i + k, k)

        def l1_sp(sp):
            m = L1
            F0.events.wait(sp, "pre_split", 2)
            sp.dma_start(brow[:, 0:3 * E1 + P], ins["L1_w"]).then_inc(m["w_landed"], 16)
            sp.dma_start(bv1, ins["L1_bv"].partition_broadcast(P)).then_inc(m["w_landed"], 16)
            F0.events.wait(sp, "split", 3 * F0.chunks)

            def mask_row(b):
                return ins["mask1"][bass.ds(b, 1)].rearrange("a n -> (a n)").partition_broadcast(P)

            def batch(b, k):
                wait(sp, m["v_full"], b - 1)
                sp.dma_start(ring[:, k, :], ins["ctx_tok"][bass.ds(b, 1)].rearrange("a p n -> (a p) n"))\
                  .then_inc(m["ctx_landed", k], 16)
                wait(sp, m["k_made"], 2 * b - 2)
                sp.dma_start(ring[:, 2 + k, :], mask_row(b)).then_inc(m["mask_landed", k], 16)

            in_pairs(sp, batch)
            for b in range(B):
                if b < 2:
                    sp.wait_ge(m["k_made"], 2 * (B - 1 + b))
                else:
                    sp.wait_ge(m["out_biased"], b - 1)
                sp.dma_start(ring[:, 2 + b % 2, :], mask_row(b)).then_inc(m["mask_landed", b % 2], 16)

        def l1_pool(pool):
            m = L1

            def batch(b, k):
                pool.wait_ge(m["k_made"], 2 * b + 2)
                for n in range(PATCH):
                    pn = PATCH * b + n
                    wait(pool, m["sfull"], 2 * (pn - 1))
                    pool.tensor_tensor(kblock[0:E1 + 1, n % 2, :, :],
                                       k1[0:E1 + 1, n * P:(n + 1) * P].unsqueeze(1).broadcast_to([E1 + 1, H1, P]),
                                       consts[0:E1 + 1, C_HEADS:C_HEADS + H1].unsqueeze(2).broadcast_to([E1 + 1, H1, P]),
                                       ALU.mult).then_inc(m["blocked"], 1)

            in_pairs(pool, batch)

        def l1_pe(pe):
            m = L1
            pe.wait_ge(m["w_landed"], 32)
            pe.wait_ge(m["ones"], 3)

            def turn_and_sum(b, k, n):
                pn = PATCH * b + n
                for s in range(2):
                    u = 2 * pn + s
                    wait(pe, m["tfree"], u)
                    pe.wait_ge(m["exps"], u + 1)
                    for h in range(4):
                        mm = pe.transpose(turn[:, h * P:(h + 1) * P], pbuf[:, s, h * P:(h + 1) * P], ident)
                    mm.then_inc(m["tfull"], 1)
                    pe.wait_ge(m["tfree"], u + 1)
                    if s == 0:
                        wait(pe, m["onorm"], pn)
                        pe.wait_ge(m["v_made"], b + 1)
                    for h in range(4):
                        hh = 4 * s + h
                        mm = pe.matmul(heado[:, hh * 9:hh * 9 + 9], ptbuf[:, s, h * P:(h + 1) * P], v1[k][:, n, hh, :],
                                       start=True, stop=True)
                mm.then_inc(m["av"], 1)

            def batch(b, k):
                pe.wait_ge(m["normed"], b + 1)
                wait(pe, m["k_biased"], b)
                wait(pe, m["q_made"], b)
                pe.matmul(proj[0][0:E1, :], wq1, xn1[k], start=True, stop=True)
                pe.matmul(proj[1][0:E1, :], wk1, xn1[k], start=True, stop=True).then_inc(m["qk_full"], 1)
                pe.wait_ge(m["ctx_landed", k], 16 * (b // 2 + 1) if isinstance(b, int) else 8 * (b - k) + 16)
                wait(pe, m["v_made"], b)
                for n in range(PATCH):
                    mm = pe.matmul(outp[1][:, n * E1:(n + 1) * E1], ring[:, k, n * P:(n + 1) * P], wv1, start=True, stop=True)
                mm.then_inc(m["v_full"], 1)
                pe.wait_ge(m["q_made"], b + 1)
                for n in range(PATCH):
                    pn = PATCH * b + n
                    pe.wait_ge(m["blocked"], pn + 1)
                    for s in range(2):
                        wait(pe, m["shifted"], 2 * pn + s - 1)
                        pe.matmul(score[s][:, :], q1[0:E1 + 1, n * P:(n + 1) * P],
                                  kblock[0:E1 + 1, n % 2, 4 * s:4 * s + 4, :].rearrange("p h j -> p (h j)"),
                                  start=True, stop=True).then_inc(m["sfull"], 1)
                    if n:
                        turn_and_sum(b, k, n - 1)
                turn_and_sum(b, k, PATCH - 1)

            in_pairs(pe, batch)

            def turn_outputs(b):
                wait(pe, m["oturned"], b - 1)
                for n in range(PATCH):
                    mm = pe.transpose(proj[b % 2][0:E1, n * P:(n + 1) * P], o1[:, (PATCH * b + n) * E1:(PATCH * b + n + 1) * E1],
                                      ident)
                mm.then_inc(m["osum"], 1)

            def out_product(b):
                if b + 1 < B:
                    turn_outputs(b + 1)
                pe.wait_ge(m["oturned"], b + 1)
                wait(pe, m["out_biased"], b - 1)
                pe.matmul(outp[b % 2][:, :], wo1, og[b % 2], start=True, stop=True).then_inc(m["out_full"], 1)

            pe.wait_ge(m["gelu"], 1)
            turn_outputs(0)
            pe_tail(pe, 3, out_product)

        def l1_act(act):
            m = L1

            def exponentials(pn, s):
                u = 2 * pn + s
                act.wait_ge(m["shifted"], u + 1)
                wait(act, m["tfull"], u - 1)
                act.activation(pbuf[:, s, :], tbuf[:, s, :], ACT.Exp).then_inc(m["exps"], 1)

            def take_turned(pn, s):
                act.wait_ge(m["tfull"], 2 * pn + s + 1)
                act.activation(ptbuf[:, s, :], turn[:, :], ACT.Copy).then_inc(m["tfree"], 1)

            def batch(b, k):
                for n in range(PATCH):
                    for s in range(2):
                        exponentials(PATCH * b + n, s)
                        if n:
                            take_turned(PATCH * b + n - 1, s)
                for s in range(2):
                    take_turned(PATCH * b + PATCH - 1, s)

            in_pairs(act, batch)
            act.wait_ge(m["onorm"], B * PATCH)
            act.activation(o1, o1, ACT.Gelu).then_inc(m["gelu"], 1)
            for b in range(B):
                act.wait_ge(m["osum"], b + 1)
                wait(act, m["out_full"], b - 1)
                act.activation(og[b % 2], proj[b % 2][0:E1, :], ACT.Copy).then_inc(m["oturned"], 1)
            act_tail(act, 3)

        def l1_dve(dve):
            m = L1
            F0.events.wait(dve, "split", 3 * F0.chunks)
            for i in range(2):
                dve.memset(v1[i][:, :, :, DH1:DH1 + 1], 1.0).then_inc(m["ones"], 1)
            dve.memset(q1[E1:E1 + 1, :], 1.0).then_inc(m["ones"], 1)
            dve.wait_ge(ln_newton, 9 * LN_CALLS_AT_L1)
            dve.wait_ge(m["w_landed"], 32)

            def softmax(pn, s):
                u = 2 * pn + s
                blocks = lambda ap: ap.rearrange("p (h j) -> p h j", h=4)
                dve.wait_ge(m["sfull"], u + 1)
                dve.tensor_reduce(rowmax[:, s, 0:4], blocks(score[s][:, :]), AX.X, ALU.max).then_inc(m["rowmax"], 1)
                dve.wait_ge(m["rowmax"], u + 1)
                wait(dve, m["exps"], u - 1)
                dve.tensor_tensor(blocks(tbuf[:, s, :]), blocks(score[s][:, :]),
                                  rowmax[:, s, 0:4].unsqueeze(2).broadcast_to([P, 4, P]), ALU.subtract).then_inc(m["shifted"], 1)

            def normalise(pn):
                dve.wait_ge(m["av"], pn + 1)
                o = heado[:, 0:H1 * 9].rearrange("p (h d) -> p h d", h=H1)
                dve.reciprocal(rinv[:, 0, :], o[:, :, DH1]).then_inc(m["v_inv"], 1)
                dve.wait_ge(m["v_inv"], pn + 1)
                dve.tensor_tensor(o1[:, bass.ds(pn * E1, E1)].rearrange("p (h d) -> p h d", h=H1), o[:, :, 0:DH1],
                                  rinv[:, 0, :].unsqueeze(2).broadcast_to([P, H1, DH1]), ALU.mult).then_inc(m["onorm"], 1)

            def batch(b, k):
                wait(dve, m["qk_full"], b - 1)
                dve.tensor_scalar(xn1[k], x[:, bass.ds(b, 1), :].rearrange("p a n -> p (a n)"),
                                  moments[:, bass.ds(b, 1), 0], rstd[:, bass.ds(b, 1)], ALU.subtract, ALU.mult)\
                   .then_inc(m["normed"], 1)
                dve.wait_ge(m["qk_full"], b + 1)
                wait(dve, m["sfull"], 2 * PATCH * b)
                dve.tensor_scalar(q1[0:E1, :], proj[0][0:E1, :], vecs[0:E1, V_BQ1:V_BQ1 + 1], float(DH1) ** -0.5,
                                  ALU.add, ALU.mult).then_inc(m["q_made"], 1)
                wait(dve, m["blocked"], PATCH * b)
                dve.tensor_scalar(k1[0:E1, :], proj[1][0:E1, :], vecs[0:E1, V_BK1:V_BK1 + 1], None, ALU.add)\
                   .then_inc(m["k_biased"], 1)
                dve.wait_ge(m["k_biased"], b + 1)
                dve.wait_ge(m["mask_landed", k], 16 * (b // 2 + 1) if isinstance(b, int) else 8 * (b - k) + 16)
                mask = ring[:, 2 + k, :]
                dve.scalar_tensor_tensor(k1[0:E1, :], mask[0:E1, :], 0.0, k1[0:E1, :], ALU.is_gt, ALU.mult)\
                   .then_inc(m["k_made"], 1)
                dve.tensor_scalar(k1[E1:E1 + 1, :], mask[E1:E1 + 1, :], 0.0, -1e9, ALU.is_le, ALU.mult).then_inc(m["k_made"], 1)
                dve.wait_ge(m["v_full"], b + 1)
                wait(dve, m["av"], PATCH * (b - 1))
                dve.tensor_tensor(v1[k][:, :, :, 0:DH1],
                                  outp[1][:, 0:PATCH * E1].rearrange("p (n h d) -> p n h d", n=PATCH, h=H1),
                                  bv1.rearrange("p (h d) -> p h d", h=H1).unsqueeze(1).broadcast_to([P, PATCH, H1, DH1]),
                                  ALU.add).then_inc(m["v_made"], 1)
                for n in range(PATCH):
                    for s in range(2):
                        softmax(PATCH * b + n, s)
                    if n:
                        normalise(PATCH * b + n - 1)
                normalise(PATCH * b + PATCH - 1)

            in_pairs(dve, batch)

            def add(b):
                dve.wait_ge(m["out_full"], b + 1)
                dve.wait_ge(m["mask_landed", b % 2], 16 * (B // 2 + b // 2 + 1))
                wait(dve, m["added"], b - 1)
                dve.scalar_tensor_tensor(ptbuf[:, b % 2, :], outp[b % 2][:, :], vecs[:, V_BO1:V_BO1 + 1],
                                         ring[:, 2 + b % 2, :], ALU.add, ALU.mult).then_inc(m["out_biased"], 1)
                dve.wait_ge(m["out_biased"], b + 1)
                dve.tensor_tensor(x[:, b, :], x[:, b, :], ptbuf[:, b % 2, :], ALU.add).then_inc(m["added"], 1)
                dve.wait_ge(m["added"], b + 1)

            dve_tail(dve, 3, add)

        EXPERTS, RANK = 8, 16
        ER = EXPERTS * RANK
        HL = ER + EXPERTS
        hl = flat[:, 0:B * HL].rearrange("p (b n) -> p b n", b=B)
        rt = [flat[:, 2048 + 64 * i:2048 + 64 * (i + 1)].rearrange("p (b e) -> p b e", b=B) for i in range(6)]

        def m2_sp(sp):
            m = M2
            LA[2].events.wait(sp, "split", LA[2].tiles * NG)
            sp.dma_start(ring[:, 0:4, 0:HL], ins["M2_a"]).then_inc(m["a_landed"], 16)
            sp.dma_start(ring[:, 5, :], ins["M2_b"]).then_inc(m["b_landed"], 16)
            row_sp(sp, 0, "M2_bias")
            sp.wait_ge(m["a_split"], 1)
            sp.dma_start(ring[:, 0:4, :], ins["M2_w"]).then_inc(m["w_landed"], 16)

        def m2_pool(pool):
            m = M2
            LA[2].events.wait(pool, "outfull", B * NPAIR)
            pool.wait_ge(m["a_landed"], 16)
            raw = ring[:, 0:4, 0:HL]
            pool.tensor_tensor(w_out[:, :, 0, 0:HL], raw, consts[:, C_ZERO:C_ZERO + 1].unsqueeze(2).broadcast_to([P, 4, HL]),
                               ALU.add).then_inc(m["a_high"], 1)
            pool.wait_ge(m["a_high"], 1)
            pool.tensor_tensor(w_out[:, :, 1, 0:HL], raw, w_out[:, :, 0, 0:HL].bitcast(F32), ALU.subtract)\
                .then_inc(m["a_split"], 1)
            pool.wait_ge(m["w_landed"], 16)
            for i, w in enumerate((w_in, w_kv)):
                raw = ring[:, 2 * i:2 * i + 2, :]
                pool.tensor_tensor(w[:, :, 0, :], raw, consts[:, C_ZERO:C_ZERO + 1].unsqueeze(2).broadcast_to([P, 2, D]),
                                   ALU.add).then_inc(m["w_high"], 1)
                pool.wait_ge(m["w_high"], i + 1)
                pool.tensor_tensor(w[:, :, 1, :], raw, w[:, :, 0, :].bitcast(F32), ALU.subtract).then_inc(m["w_split"], 1)

        def m2_pe(pe):
            m = M2
            pe.wait_ge(m["a_split"], 1)
            for b in range(B):
                pe.wait_ge(ln_low, 8 * ln_no(5) + b + 1)
                wait(pe, m["copied"], b - 1)
                mm = pe_matmuls(pe, score[b % 2][:, 0:HL], lambda a, c: xnT[:, a, c, b * S:(b + 1) * S],
                                lambda a, c: w_out[:, c, a, 0:HL])
                mm.then_inc(m["full"], 1)
            pe.wait_ge(m["w_split"], 2)

            def base(b):
                wait(pe, m["added"], b - 1)
                pe_matmuls(pe, outp[b % 2][:, :], lambda a, c: xnT[:, a, c, b * S:(b + 1) * S],
                           lambda a, c: (w_in if c < 2 else w_kv)[:, c % 2, a, :], last=False)

            def turn_weighted(b):
                wait(pe, m["high"], b - 1)
                pe.transpose(proj[b % 2][:, 0:P], hl[:, b, 0:ER], ident).then_inc(m["turned"], 1)

            def product(b):
                if b >= 2:
                    base(b)
                if b + 1 < B:
                    turn_weighted(b + 1)
                pe.wait_ge(m["high"], b + 1)
                pe.matmul(outp[b % 2][:, :], ptbuf[:, b % 2, 0:P], ring[:, 5, :], start=False, stop=True)\
                  .then_inc(m["outfull"], 1)

            base(0)
            base(1)
            pe.wait_ge(m["b_landed"], 16)
            pe.wait_ge(m["weighted"], 1)
            turn_weighted(0)
            pe_tail(pe, 6, product)

        def m2_act(act):
            m = M2
            act.wait_ge(m["route"], 6)
            act.activation(rt[1], rt[1], ACT.Exp).then_inc(m["expd"], 1)
            for b in range(B):
                act.wait_ge(m["turned"], b + 1)
                wait(act, m["outfull"], b - 1)
                act.activation(ptbuf[:, b % 2, 0:P], proj[b % 2][:, 0:P], ACT.Copy).then_inc(m["high"], 1)
            act_tail(act, 6)

        def m2_dve(dve):
            m = M2
            add_row(dve, 0)
            for b in range(B):
                dve.wait_ge(m["full"], b + 1)
                dve.tensor_copy(hl[:, b, :], score[b % 2][:, 0:HL]).then_inc(m["copied"], 1)
            dve.wait_ge(m["copied"], B)
            logits = hl[:, :, ER:HL]
            wide = [t.rearrange("p (b e f) -> p b e f", b=B, e=EXPERTS) for t in (tbuf[:, 0, :], tbuf[:, 1, :])]
            mine = logits.unsqueeze(3).broadcast_to([P, B, EXPERTS, EXPERTS])
            other = logits.unsqueeze(2).broadcast_to([P, B, EXPERTS, EXPERTS])
            dve.tensor_tensor(wide[0], other, mine, ALU.is_gt).then_inc(m["route"], 1)
            dve.tensor_tensor(wide[1], other, mine, ALU.is_equal).then_inc(m["route"], 1)
            dve.wait_ge(m["route"], 2)
            less = consts[:, C_LESS:C_LESS + 64].unsqueeze(1).broadcast_to([P, B, 64])
            dve.tensor_tensor(tbuf[:, 1, :].rearrange("p (b n) -> p b n", b=B), tbuf[:, 1, :].rearrange("p (b n) -> p b n", b=B),
                              less, ALU.mult).then_inc(m["route"], 1)
            dve.wait_ge(m["route"], 3)
            dve.tensor_tensor(tbuf[:, 0, :], tbuf[:, 0, :], tbuf[:, 1, :], ALU.add).then_inc(m["route"], 1)
            dve.tensor_reduce(rowmax[:, 0, :], logits, AX.X, ALU.max).then_inc(m["route"], 1)
            dve.wait_ge(m["route"], 5)
            dve.tensor_tensor(rt[1], logits, rowmax[:, 0, :].unsqueeze(2).broadcast_to([P, B, EXPERTS]), ALU.subtract)\
               .then_inc(m["route"], 1)
            dve.tensor_reduce(rt[0], wide[0], AX.X, ALU.add).then_inc(m["route"], 1)
            dve.wait_ge(m["route"], 7)
            dve.wait_ge(m["expd"], 1)
            dve.scalar_tensor_tensor(rt[2], rt[0], 1.5, rt[1], ALU.is_lt, ALU.mult).then_inc(m["routed"], 1)
            dve.wait_ge(m["routed"], 1)
            dve.tensor_reduce(rowmax[:, 1, :], rt[2], AX.X, ALU.add).then_inc(m["routed"], 1)
            dve.wait_ge(m["routed"], 2)
            dve.reciprocal(rinv[:, 0, :], rowmax[:, 1, :]).then_inc(m["routed"], 1)
            dve.wait_ge(m["routed"], 3)
            dve.scalar_tensor_tensor(rt[3], rt[2], 2.0, rinv[:, 0, :].unsqueeze(2).broadcast_to([P, B, EXPERTS]),
                                     ALU.mult, ALU.mult).then_inc(m["routed"], 1)
            dve.wait_ge(m["routed"], 4)
            act_hl = hl[:, :, 0:ER].rearrange("p b (e r) -> p b e r", e=EXPERTS)
            dve.tensor_tensor(act_hl, act_hl, rt[3].unsqueeze(3).broadcast_to([P, B, EXPERTS, RANK]), ALU.mult)\
               .then_inc(m["weighted"], 1)

            def add(b):
                dve.wait_ge(m["outfull"], b + 1)
                dve.tensor_tensor(x[:, b, :], x[:, b, :], outp[b % 2][:, :], ALU.add).then_inc(m["added"], 1)
                dve.wait_ge(m["added"], b + 1)

            dve_tail(dve, 6, add)

        def start_sp(sp):
            sp.dma_start(consts[:, :], ins["consts"]).then_inc(consts_landed, 16)
            sp.dma_start(vecs[:, :], ins["vecs"]).then_inc(consts_landed, 16)
            for b in range(0, B, 4):
                sp.dma_start(x[:, b:b + 4, :], ins["x"][:, b:b + 4, :]).then_inc(x_landed, 16)
            for n in range(8):
                if n == 4:
                    sp.dma_start(mask_bytes[:, :], ins["mask0"]).then_inc(mask_landed, 16)
                if n >= 4:
                    sp.wait_ge(ctx_split, n - 3)
                sp.dma_start(ring[:, n % 4, :], ins["ctxT"][:, n // 2, (n % 2) * HALF:(n % 2 + 1) * HALF])\
                  .then_inc(ctx_landed[n % 4], 16)
            sp.wait_ge(ctx_split, 8)

        def start_pool(pool):
            pool.wait_ge(consts_landed, 32)
            for n in range(8):
                cols = slice((n % 2) * HALF, (n % 2 + 1) * HALF)
                pool.wait_ge(ctx_landed[n % 4], 16 * (n // 4 + 1))
                pool.tensor_tensor(ctxT[:, 0, n // 2, cols], ring[:, n % 4, :], zeros512, ALU.add).then_inc(ctx_high, 1)
                pool.wait_ge(ctx_high, n + 1)
                pool.tensor_tensor(ctxT[:, 1, n // 2, cols], ring[:, n % 4, :],
                                   ctxT[:, 0, n // 2, cols].bitcast(F32), ALU.subtract).then_inc(ctx_split, 1)

        def start_dve(dve):
            dve.wait_ge(consts_landed, 32)
            dve.tensor_tensor(kqn[:, :], vecs[:, V_QN:V_QN + 1], vecs[:, V_KN:V_KN + 1], ALU.mult).then_inc(kqn_made, 1)
            dve.wait_ge(x_landed, 32)
            dve_tail(dve, 0, None)
            dve.wait_ge(mask_landed, 16)
            dve.tensor_scalar(maskadd[:, :, :].rearrange("p b n -> p (b n)"), mask_bytes[:, :].bitcast(U8), -1.0, MASKED, ALU.add, ALU.mult).then_inc(mask_made, 1)
            dve.wait_ge(mask_made, 1)
            dve.tensor_reduce(live[:, :], maskadd[:, :, :], AX.X, ALU.max).then_inc(mask_made, 1)
            dve.wait_ge(mask_made, 2)
            dve.tensor_scalar(live[:, :], live[:, :], -1.0, None, ALU.is_gt).then_inc(mask_made, 1)
            dve.wait_ge(mask_made, 3)

        def finish_sp(sp):
            for b in range(B):
                F3.events.wait(sp, "added", B * (F3.chunks // 2 - 1) + b + 1)
                sp.dma_start(out[:, b, :], x[:, b, :]).then_inc(out_landed, 16)
            sp.wait_ge(out_landed, 16 * B)

        block = ctx.enter_context(nc.Block())

        @block.sync
        def _(sp):
            start_sp(sp)
            attention_sp(sp, LA[0])
            LA[0].events.wait(sp, "split", LA[0].tiles * NG)
            LA[0].events.wait(sp, "pv", 2 * NH)
            ffn_sp(sp, F0)
            l1_sp(sp)
            sp.wait_ge(L1["out_full"], B)
            sp.wait_ge(L1["out_biased"], B)
            ffn_sp(sp, F1)
            F1.events.wait(sp, "split", 2 * F1.chunks)
            sp.dma_start(maskadd[:, 0, :], ins["mask2"]).then_inc(mask_landed, 16)
            attention_sp(sp, LA[2])
            m2_sp(sp)
            row_sp(sp, 1, "L3_bo")
            sp.wait_ge(M2["w_split"], 2)
            sp.wait_ge(M2["outfull"], B)
            attention_sp(sp, LA[3])
            row_sp(sp, 2, "F3_bias")
            LA[3].events.wait(sp, "split", LA[3].tiles * NG)
            ffn_sp(sp, F3)
            finish_sp(sp)

        @block.gpsimd
        def _(pool):
            start_pool(pool)
            attention_pool(pool, LA[0])
            ffn_pool(pool, F0)
            l1_pool(pool)
            ffn_pool(pool, F1)
            attention_pool(pool, LA[2])
            m2_pool(pool)
            attention_pool(pool, LA[3])
            ffn_pool(pool, F3)

        @block.tensor
        def _(pe):
            pe.wait_ge(consts_landed, 32)
            pe_tail(pe, 0, None)
            pe.wait_ge(ctx_split, 8)
            attention_pe(pe, LA[0])
            ffn_pe(pe, F0)
            l1_pe(pe)
            ffn_pe(pe, F1)
            attention_pe(pe, LA[2])
            m2_pe(pe)
            attention_pe(pe, LA[3])
            ffn_pe(pe, F3)

        @block.scalar
        def _(act):
            act.wait_ge(consts_landed, 32)
            act_tail(act, 0)
            attention_act(act, LA[0])
            ffn_act(act, F0)
            l1_act(act)
            ffn_act(act, F1)
            attention_act(act, LA[2])
            m2_act(act)
            attention_act(act, LA[3])
            ffn_act(act, F3)

        @block.vector
        def _(dve):
            start_dve(dve)
            attention_dve(dve, LA[0])
            ffn_dve(dve, F0)
            l1_dve(dve)
            ffn_dve(dve, F1)
            dve.wait_ge(mask_landed, 32)
            attention_dve(dve, LA[2])
            m2_dve(dve)
            attention_dve(dve, LA[3])
            ffn_dve(dve, F3)


def constants():
    c = np.zeros((P, C_COUNT), np.float32)
    c[:, C_IDENT:C_IDENT + P] = np.eye(P)
    c[:, C_ONES:C_ONES + P] = 1
    for e in range(64):
        c[e, C_HEADS + e // 8] = 1
    c[64, C_HEADS:C_HEADS + 8] = 1
    c[:, C_MEAN] = 1 / P
    c[:, C_FIRST:C_FIRST + 32] = np.arange(32, 0, -1)
    c[:, C_LESS:C_LESS + 64] = np.tril(np.ones((8, 8)), -1).reshape(64)
    return c


def tiles(w):
    n = w.shape[0] // P
    return w.reshape(n, P, -1, P).transpose(0, 3, 2, 1).reshape(n, P, -1)


def pad_rows(w, rows):
    return np.concatenate([w, np.zeros((rows - w.shape[0], w.shape[1]), w.dtype)])


def layout(inputs):
    i = {k: np.asarray(a) for k, a in inputs.items()}
    a = {"consts": constants()}
    a["x"] = i["x"].transpose(1, 0, 2)
    a["ctxT"] = i["ctx_4096"].reshape(T, DC, P).transpose(2, 1, 0)
    a["mask0"] = i["mask_BxSxS2_bk0"].transpose(1, 0, 2).reshape(S, T).view(np.int32)
    a["position_bias"] = i["L0_xattn_position_bias"]
    vecs = np.zeros((P, V_COUNT), np.float32)
    vecs[:, V_LNW:V_LNW + 4] = i["L0_xattn_ln_weight"].reshape(DC, P).T
    vecs[:, V_BQ3:V_BQ3 + 32] = i["L3_xattn_bq"].reshape(NH, P).T
    vecs[:, V_BK3:V_BK3 + 16] = i["L3_xattn_bkv"].reshape(16, P).T
    vecs[:, V_QN] = i["L2_xattn_q_norm_w"]
    vecs[:, V_KN] = i["L2_xattn_k_norm_w"]
    vecs[:64, V_BQ1] = i["L1_xattn_bq"]
    vecs[:64, V_BK1] = i["L1_xattn_bk"]
    vecs[:, V_BO1] = i["L1_xattn_bo"]
    vecs[:, V_BI:V_BI + 16] = i["L3_ffn_inter_b"].reshape(16, P).T
    vecs[:, V_BI + 16:V_BI + 32] = vecs[:, V_BI:V_BI + 16]
    a["vecs"] = vecs
    a["L0_wq"], a["L0_wk"], a["L0_wv"] = (tiles(i[f"L0_xattn_w_{n}"]) for n in "qkv")
    a["L0_wo"] = i["L0_xattn_w_out"].T.reshape(NH, P, D)
    a["L2_wq"], a["L2_wk"], a["L2_wv"] = (tiles(i[f"L2_xattn_W{n}"]) for n in "qkv")
    a["L2_wo"] = i["L2_xattn_Wo"].T.reshape(NH, P, D)
    a["L3_wq"] = tiles(i["L3_xattn_Wq"].T)
    a["L3_wk"] = tiles(i["L3_xattn_Wkv"][:, :1024].T)
    a["L3_wv"] = tiles(i["L3_xattn_Wkv"][:, 1024:].T)
    a["L3_wo"] = i["L3_xattn_Wo"].reshape(NH, P, D)
    hid0 = 11 * P
    w1, w3, b1, b3 = (pad_rows(i[f"L0_ffn_{n}"], hid0) for n in ("w1", "w3", "lora_B1", "lora_B3"))
    a["F0_in"], a["F0_in2"] = tiles(w1), tiles(w3)
    a["F0_out"] = pad_rows(i["L0_ffn_w2"].T, hid0).reshape(11, P, D)
    pre = np.zeros((P, D), np.float32)
    pre[0:16], pre[32:48] = i["L0_ffn_lora_A1"], i["L0_ffn_lora_A3"]
    a["F0_pre"] = tiles(pre)[0]
    a["F0_b1"], a["F0_b3"], a["F0_b2"] = b1.T, b3.T, i["L0_ffn_lora_B2"].T
    a["F0_a2"] = pad_rows(i["L0_ffn_lora_A2"].T, hid0).reshape(11, P, 16).transpose(1, 0, 2).reshape(P, -1)
    a["L1_w"] = np.concatenate([i["L1_xattn_Wq"].T, i["L1_xattn_Wk"].T, i["L1_xattn_Wv"].T,
                                pad_rows(i["L1_xattn_Wo"].T, P)], axis=1)
    a["L1_bv"] = i["L1_xattn_bv"]
    a["ctx_tok"] = i["ctx_4096"]
    a["mask1"] = i["mask_Bx1x4096_ff1"].reshape(B, D)
    a["F1_pre"] = tiles(pad_rows(i["L1_ffn_c1_w"], P))[0]
    a["F1_c2"] = i["L1_ffn_c2_w"].T
    a["F1_in"] = tiles(i["L1_ffn_w1"])
    a["F1_out"] = i["L1_ffn_w2t"].reshape(14, P, D)
    a["mask2"] = i["mask_1x1xSxS2_ff0"].reshape(S, S)
    experts = np.concatenate([i["L2_ffn_A"].reshape(P, D), i["L2_ffn_W_router"]])
    a["M2_a"] = experts.T.reshape(DC, P, -1).transpose(1, 0, 2)
    a["M2_w"] = i["L2_ffn_W_base"].T.reshape(DC, P, D).transpose(1, 0, 2)
    a["M2_b"] = i["L2_ffn_B"].transpose(0, 2, 1).reshape(P, D)
    a["M2_bias"], a["L3_bo"], a["F3_bias"] = i["L2_ffn_b_base"], i["L3_xattn_bo"], i["L3_ffn_output_b"]
    a["F3_in"] = tiles(i["L3_ffn_inter_w"].T)
    a["F3_out"] = i["L3_ffn_output_w"].reshape(16, P, D)
    return {k: np.ascontiguousarray(n) for k, n in a.items()}


def kernel(**inputs):
    from concourse import bacc
    from concourse.bass_utils import run_bass_kernel_spmd

    arrays = layout(inputs)
    nc = bacc.Bacc("TRN2", target_bir_lowering=False, num_devices=1)
    ins = {k: nc.dram_tensor(f"in_{k}", a.shape, mybir.dt.from_np(a.dtype), kind="ExternalInput").ap()
           for k, a in arrays.items()}
    out = nc.dram_tensor("out", (P, B, D), F32, kind="ExternalOutput").ap()
    build(nc, ins, out)
    r = run_bass_kernel_spmd(nc, [{f"in_{k}": a for k, a in arrays.items()}], core_ids=[0])
    return np.ascontiguousarray(np.asarray(r.results[0]["out"]).transpose(1, 0, 2))
```

```python
from contextlib import ExitStack

import numpy as np

import concourse.bass as bass
from concourse import mybir

F32 = mybir.dt.float32
F32R = mybir.dt.float32r
I32 = mybir.dt.int32
U8 = mybir.dt.uint8
ALU = mybir.AluOpType
ACT = mybir.ActivationFunctionType
AX = mybir.AxisListType

P = 128
B = 8
S = 128
D = 512
DC = D // P
T = B * S
HALF = T // 2
BH = B // 2
NH = 32
GH = 4
NG = NH // GH
NPAIR = NH // 2
EPS = 1e-5
MASKED = 1e30
RSQRT_MAGIC = 0x5F3759DF
RSQRT_OPS = 11
PASSES = ((0, 0), (0, 1), (1, 0))

C_IDENT = 0
C_ONES = 128
C_HEADS = 256
C_ZERO = 264
C_MEAN = 265
C_FIRST = 266
C_LESS = 298
C_COUNT = 362

V_LNW, V_BQ3, V_BK3, V_BV3, V_QN, V_KN, V_BQ1, V_BK1, V_BO1, V_BI = 0, 4, 36, 44, 52, 53, 54, 55, 56, 57
V_COUNT = 89


def wait(engine, semaphore, value):
    if isinstance(value, int) and value <= 0:
        return
    engine.wait_ge(semaphore, value)


class Events:

    def __init__(self, semaphores, before, totals):
        self.semaphores = semaphores
        self.before = before
        self.after = dict(before)
        for name, n in totals.items():
            self.after[name] = before.get(name, 0) + n

    def __getitem__(self, name):
        return self.semaphores[name]

    def wait(self, engine, name, n):
        if isinstance(n, int) and n <= 0:
            return
        engine.wait_ge(self.semaphores[name], n + self.before.get(name, 0))


class Attention:

    def __init__(self, layer, stage, semaphores, before):
        self.layer = layer
        self.scale = float(P) ** -0.5
        self.stage = stage
        self.own_kv = layer == 0
        self.normed = layer == 2
        kv = GH if self.own_kv else 1
        self.tiles = 2 * kv + 2 * GH
        self.ring = 4 if self.own_kv else 5
        self.projections = 2 * kv + GH
        self.turns = 16 if self.own_kv else 17 if self.normed else 10
        self.turns_first = 6 if self.normed else 2
        units, heads = 2 * NH, NH
        turns = self.turns_first + self.turns * NG - (6 if self.normed else 2)
        calls = heads + NG if self.normed else 0
        totals = dict(split=self.tiles * NG, high_w=self.tiles * NG, sfull=units, rowmax=units, negmax=units,
                      exps=units, rinv=units, pready=units, tfull=turns, tfree=turns, pv=units, high=units,
                      low=units, outfull=B * NPAIR, added=B * NPAIR, sfree=units if layer != 3 else 0,
                      masked=units if layer == 0 else 0, rlive=units if layer == 0 else 0,
                      squared=calls, shifted=2 * calls, newton=9 * calls,
                      rsq=heads if self.normed else 0, diag=NG if self.normed else 0)
        for i in range(2):
            totals["pfull", i] = totals["pfree", i] = self.projections * NG
            totals["bias_landed", i] = 16 * NPAIR if layer == 0 else 0
        for i in range(self.ring):
            totals["landed", i] = 16 * self.tiles // self.ring * NG
        self.events = Events(semaphores, before, totals)

    NAMES = ("split high_w sfull sfree masked rowmax negmax exps rinv rlive pready tfull tfree pv high low "
             "outfull added squared shifted newton rsq diag").split() + [
                 (n, i) for n in ("pfull", "pfree", "bias_landed") for i in range(2)] + [("landed", i) for i in range(5)]

    def new_kv(self, j):
        return self.own_kv or j == 0

    def tile(self, g, j, what):
        if self.own_kv:
            return self.tiles * g + 4 * j + "kvqo".index(what)
        return self.tiles * g + self.SHARED_TILES.index((what, j if what in "qo" else 0))

    SHARED_TILES = [("k", 0), ("v", 0), ("q", 0), ("q", 1), ("o", 0), ("q", 2), ("o", 1), ("q", 3), ("o", 2), ("o", 3)]

    def projection(self, g, j, what):
        if self.own_kv:
            return self.projections * g + 3 * j + "kvq".index(what)
        return self.projections * g + ("kv".index(what) if what in "kv" else 2 + j)

    def turn(self, g, j, what):
        if self.own_kv:
            order = ["T0", "T1", "V0", "V1"]
            at = 4 * j
        elif self.normed:
            order = [["T0", "T1", "Q"], ["T0", "T1", "Q"], ["T0", "T1", "Q", "K"],
                     ["B0", "B1", "T0", "T1", "V0", "V1", "Q"]][j]
            at = (0, 3, 6, 10)[j]
            if isinstance(g, int) and g < 0:
                return ["K", "B0", "B1", "V0", "V1", "Q"].index(what)
            if isinstance(g, int) and g == NG - 1 and j == GH - 1:
                order, at = ["T0", "T1"], 9
        else:
            order = ["T0", "T1", "V0", "V1"]
            at = 2 * j
        if isinstance(g, int) and g < 0:
            return [x for x in order if x[0] != "T"].index(what)
        return self.turns_first + self.turns * g + at + order.index(what)


class FeedForward:

    def __init__(self, name, stage, kind, chunks, semaphores, before, small=(), row=None):
        self.name, self.stage, self.kind, self.chunks, self.row = name, stage, kind, chunks, row
        self.low_rank = kind != "gelu"
        self.what = ["in", "in2", "out"] if kind == "silu" else ["in", "out"]
        self.ring = 2 * len(self.what)
        n, halves, pre = chunks, 2 * chunks, int(self.low_rank)
        nt = len(self.what) * chunks
        silu, pick = halves * (kind == "silu"), halves * (kind == "pick")
        outs = B * ((chunks + 1) // 2)
        totals = dict(split=nt, high_w=nt, pre_landed=16 * pre, pre_split=2 * pre, small_landed=16 * len(small),
                      sfull=silu + pick, tfull=pick, made=halves, high=halves, low=halves, outfull=outs, added=outs,
                      lowfull=silu, low2=2 * (kind == "silu"), bmax=pick, equal=pick, weighed=pick, fmax=pick,
                      picked=pick)
        for i in range(2):
            totals["pfull", i] = n + pre
            totals["pfree", i] = (n + pre) * (kind != "gelu")
        for i in range(self.ring):
            totals["landed", i] = 16 * len(range(i, nt, self.ring))
        self.small = small
        self.events = Events(semaphores, before, totals)

    NAMES = ("split high_w pre_landed pre_split small_landed sfull tfull made high low outfull added lowfull low2 "
             "bmax equal weighed fmax picked").split() + [
                 (n, i) for n in ("pfull", "pfree") for i in range(2)] + [("landed", i) for i in range(6)]

    def tile(self, g, j, k):
        return len(self.what) * (GH * g + j) + k

    def out_tile(self, pair, slots):
        return len(self.what) * (2 * pair + len(slots))


def small_attention(sem):
    names = ("w_landed ones normed qk_full q_made k_biased k_made v_full v_made blocked sfull rowmax shifted exps "
             "tfull tfree av osum onorm v_inv oturned gelu out_full out_biased added").split()
    found = {n: sem(f"L1_{n}") for n in names}
    for n in ("ctx_landed", "mask_landed"):
        for i in range(2):
            found[n, i] = sem(f"L1_{n}{i}")
    return found


def mixture(sem):
    names = ("a_landed w_landed b_landed a_split w_split a_high w_high full copied route routed expd weighted "
             "turned high outfull added").split()
    return {n: sem(f"M2_{n}") for n in names}


def build(nc, ins, out):
    with ExitStack() as ctx:
        def sb(name, shape, dt=F32):
            return ctx.enter_context(nc.sbuf_tensor(name, shape, dt))

        def bank(name):
            return ctx.enter_context(nc.psum_tensor(name, [P, 512], F32))

        def sem(name):
            return ctx.enter_context(nc.semaphore(name))

        x = sb("x", [P, B, D])
        ctxT = sb("ctxT", [P, 2, DC, T], F32R)
        xnT = sb("xnT", [P, 2, DC, T], F32R)
        acts = sb("acts", [P, 4, 2, T], F32R)
        w_in = sb("w_in", [P, 2, 2, D], F32R)
        w_kv = sb("w_kv", [P, 2, 2, D], F32R)
        w_out = sb("w_out", [P, 4, 2, D], F32R)
        sq = sb("sq", [P, T])
        ring = sb("ring", [P, 6, D])
        big = sb("big", [P, 4, T])
        qT, kT, vT, v = (big[:, i, :] for i in range(4))
        tbuf = sb("tbuf", [P, 2, 512])
        pbuf = sb("pbuf", [P, 2, 512])
        ptbuf = sb("ptbuf", [P, 2, 512])
        mask_bytes = sb("mask_bytes", [P, T // 4], I32)
        maskadd = sb("maskadd", [P, B, S])
        biasbuf = sb("biasbuf", [P, 2, S])
        brow = sb("brow", [P, D])
        consts = sb("consts", [P, C_COUNT])
        vecs = sb("vecs", [P, V_COUNT])
        kqn = sb("kqn", [P, 1])
        live = sb("live", [P, B])
        stats = sb("stats", [P, B, 6])
        moments = sb("moments", [P, B, 2])
        rstd = sb("rstd", [P, B])
        rrms = sb("rrms", [P, B])
        nw_v = sb("nw_v", [P, B])
        nw_t = sb("nw_t", [P, B])
        rq = sb("rq", [P, B])
        rk = sb("rk", [P, B])
        rowmax = sb("rowmax", [P, 2, 8])
        blockmax = sb("blockmax", [P, 2, 16])
        firstmax = sb("firstmax", [P, 2, 16])
        negmax = sb("negmax", [P, 2, 8])
        rowsum = sb("rowsum", [P, 2, 8])
        rinv = sb("rinv", [P, 2, 8])
        with nc.sbuf_tensor("w_kv2", [P, 2, 2, D], F32R) as w_kv2:
            pass
        spare = sb("spare", [P, 2 * T])
        kblock = spare[:, :].rearrange("p (a h n) -> p a h n", a=2, h=8)
        kraw, diagonals = spare[:, 0:T], spare[:, T:2 * T]
        ksq = diagonals
        ident = consts[:, C_IDENT:C_IDENT + P]
        ones = consts[:, C_ONES:C_ONES + P]
        zeros512 = consts[:, C_ZERO:C_ZERO + 1].broadcast_to([P, 512])

        proj = [bank(f"proj{i}") for i in range(2)]
        score = [bank(f"score{i}") for i in range(2)]
        turn = bank("turn")
        heado = bank("heado")
        outp = [bank(f"outp{i}") for i in range(2)]

        x_landed = sem("x_landed")
        consts_landed = sem("consts_landed")
        mask_landed = sem("mask_landed")
        ctx_landed = [sem(f"ctx_landed{i}") for i in range(4)]
        ctx_high = sem("ctx_high")
        ctx_split = sem("ctx_split")
        mask_made = sem("mask_made")
        kqn_made = sem("kqn_made")
        ln_stats, ln_moments, ln_shifted, ln_newton, ln_rstd, ln_normed, ln_full, ln_high, ln_low, ln_rms, ln_kept = (
            sem(f"ln_{n}") for n in "stats moments shifted newton rstd normed full high low rms kept".split())
        out_landed = sem("out_landed")
        row_landed = sem("row_landed")
        row_added = sem("row_added")
        flat = big[:, :, :].rearrange("p a n -> p (a n)")
        attention_sems = {n: sem("A_" + n if isinstance(n, str) else f"A_{n[0]}{n[1]}") for n in Attention.NAMES}
        ffn_sems = {n: sem("F_" + n if isinstance(n, str) else f"F_{n[0]}{n[1]}") for n in FeedForward.NAMES}
        LA = {0: Attention(0, 0, attention_sems, {})}
        LA[2] = Attention(2, 4, attention_sems, LA[0].events.after)
        LA[3] = Attention(3, 6, attention_sems, LA[2].events.after)
        a2 = flat[:, T + 11 * P + D:T + 11 * P + D + 11 * 16]
        b2 = flat[0:16, T + 11 * P:T + 11 * P + D]
        F0 = FeedForward("F0", 1, "silu", 11, ffn_sems, {}, small=[
            (flat[0:16, T:T + 11 * P], ins["F0_b1"]), (flat[32:48, T:T + 11 * P], ins["F0_b3"]),
            (b2, ins["F0_b2"]), (a2, ins["F0_a2"])])
        F1 = FeedForward("F1", 3, "pick", 14, ffn_sems, F0.events.after,
                         small=[(flat[0:16, T:T + 14 * P], ins["F1_c2"])])
        F3 = FeedForward("F3", 7, "gelu", 16, ffn_sems, F1.events.after, row=2)
        L1 = small_attention(sem)
        M2 = mixture(sem)
        def last_uses(A):
            n = A.chunks + A.low_rank if A in (F0, F1, F3) else A.projections * NG
            outs = B * ((A.chunks + 1) // 2 if A in (F0, F1, F3) else NPAIR)
            return [(A.events, ("pfull", 1), n), (A.events, "sfull", 2 * A.chunks if A is F0 else 0),
                    (A.events, "outfull", outs)]

        LA[0].before = LA[3].before = None
        F0.before, F1.before, LA[2].before, F3.before = (last_uses(A) for A in (LA[0], F0, F1, LA[3]))

        def wait_before(engine, A, out):
            for events, name, n in (A.before or [])[2:] if out else (A.before or [])[:2]:
                events.wait(engine, name, n)

        def pe_matmuls(pe, bank_ap, w_ap, rhs, chunks=DC, first=True, last=True):
            for c in range(chunks):
                for n, (a, b) in enumerate(PASSES):
                    mm = pe.matmul(bank_ap, w_ap(a, c), rhs(b, c), start=first and c == 0 and n == 0,
                                   stop=last and c == chunks - 1 and n == len(PASSES) - 1)
            return mm

        def pe_project(pe, w, slot, actT, half):
            return pe_matmuls(pe, proj[half][:, :], lambda a, c: w[:, slot, a, c * P:(c + 1) * P],
                              lambda b, c: actT[:, b, c, half * HALF:(half + 1) * HALF])

        def pe_out(pe, b, slots, last=True):
            for n, s in enumerate(slots):
                mm = pe_matmuls(pe, outp[b % 2][:, :], lambda a, c: acts[:, s, a, b * S:(b + 1) * S],
                                lambda a, c: w_out[:, s, a, :], chunks=1, first=n == 0,
                                last=last and n == len(slots) - 1)
            return mm

        def dve_rsqrt(dve, y, arg, tmp, shifted, newton, calls):
            base = calls * 9
            dve.tensor_scalar(tmp.bitcast(I32), arg.bitcast(I32), 1, None, ALU.logical_shift_right).then_inc(shifted, 1)
            dve.wait_ge(shifted, calls * 2 + 1)
            dve.tensor_scalar(y.bitcast(I32), tmp.bitcast(I32), -1.0, float(RSQRT_MAGIC), ALU.mult,
                              ALU.add).then_inc(shifted, 1)
            dve.wait_ge(shifted, calls * 2 + 2)
            for n in range(3):
                dve.scalar_tensor_tensor(tmp, y, -0.5, y, ALU.mult, ALU.mult).then_inc(newton, 1)
                dve.wait_ge(newton, base + (3 * n + 1))
                dve.tensor_tensor(tmp, tmp, arg, ALU.mult).then_inc(newton, 1)
                dve.wait_ge(newton, base + (3 * n + 2))
                dve.scalar_tensor_tensor(y, tmp, 1.5, y, ALU.add, ALU.mult).then_inc(newton, 1)
                dve.wait_ge(newton, base + (3 * n + 3))

        normed = [tbuf[:, 0, :], tbuf[:, 1, :], pbuf[:, 0, :], pbuf[:, 1, :]]
        ln_banks = [turn, heado]
        ln_calls = [0]
        LN_CALLS_AT_L1 = 4 + 2 + 2
        LN_STAGES = [0, 1, 3, 4, 5, 6, 7]

        def ln_no(n):
            return LN_STAGES.index(n)

        def dve_ln_stats(dve, n, b):
            dve.bn_stats(stats[:, b, :], x[:, b, :]).then_inc(ln_stats, 1)
            dve.wait_ge(ln_stats, 8 * n + b + 1)
            dve.bn_aggr(moments[:, b, :], stats[:, b, :]).then_inc(ln_moments, 1)

        def dve_ln_rstd(dve, n, half):
            cols = slice(half * BH, half * BH + BH)
            dve.wait_ge(ln_moments, 8 * n + half * BH + BH)
            dve.tensor_scalar(nw_v[:, cols], moments[:, cols, 1], EPS, None, ALU.add).then_inc(ln_rstd, 1)
            dve.wait_ge(ln_rstd, 2 * n + half + 1)
            dve_rsqrt(dve, rstd[:, cols], nw_v[:, cols], nw_t[:, cols], ln_shifted, ln_newton, ln_calls[0])
            ln_calls[0] += 1
            if n == 0:
                dve.scalar_tensor_tensor(rrms[:, cols], rstd[:, cols], 1.0, rstd[:, cols], ALU.mult,
                                         ALU.mult).then_inc(ln_rms, 1)
                dve.wait_ge(ln_rms, 3 * half + 1)
                dve.tensor_tensor(rrms[:, cols], rrms[:, cols], moments[:, cols, 1], ALU.mult).then_inc(ln_rms, 1)
                dve.wait_ge(ln_rms, 3 * half + 2)
                dve.tensor_scalar(nw_v[:, cols], rrms[:, cols], EPS, None, ALU.add).then_inc(ln_rms, 1)
                dve.wait_ge(ln_rms, 3 * half + 3)
                dve_rsqrt(dve, rrms[:, cols], nw_v[:, cols], nw_t[:, cols], ln_shifted, ln_newton, ln_calls[0])
                ln_calls[0] += 1

        def dve_ln_norm(dve, n, b):
            m = ln_no(n)
            out_ap = normed[b % 4]
            if b >= 4:
                dve.wait_ge(ln_full, 8 * m + b - 3)
            norm = dve.tensor_scalar(out_ap, x[:, b, :], moments[:, b, 0:1], rstd[:, b:b + 1], ALU.subtract, ALU.mult)
            if n == 0:
                norm.then_inc(ln_kept, 1)
                dve.wait_ge(ln_kept, 2 * b + 1)
                dve.tensor_tensor(x[:, b, :], x[:, b, :], out_ap, ALU.add).then_inc(ln_kept, 1)
                dve.wait_ge(ln_kept, 2 * b + 2)
                dve.tensor_scalar(out_ap, out_ap, rrms[:, b:b + 1], None, ALU.mult).then_inc(ln_normed, 1)
            else:
                norm.then_inc(ln_normed, 1)

        def pe_ln_turn(pe, n, b):
            m = ln_no(n)
            pe.wait_ge(ln_normed, 8 * m + b + 1)
            if b >= 2:
                pe.wait_ge(ln_low, 8 * m + b - 1)
            for c in range(DC):
                mm = pe.transpose(ln_banks[b % 2][:, c * P:(c + 1) * P], normed[b % 4][:, c * P:(c + 1) * P], ident)
            mm.then_inc(ln_full, 1)

        def act_ln_high(act, n, b):
            m = ln_no(n)
            act.wait_ge(ln_full, 8 * m + b + 1)
            src = ln_banks[b % 2][:, :].rearrange("p (c t) -> p c t", c=DC)
            if n == 0:
                for c in range(DC):
                    a = act.activation(xnT[:, 0, c, b * S:(b + 1) * S], src[:, c, :], ACT.Copy,
                                       scale=vecs[:, V_LNW + c:V_LNW + c + 1])
            else:
                a = act.activation(xnT[:, 0, :, b * S:(b + 1) * S], src, ACT.Copy)
            a.then_inc(ln_high, 1)

        def dve_ln_low(dve, n, b):
            m = ln_no(n)
            dve.wait_ge(ln_high, 8 * m + b + 1)
            src = ln_banks[b % 2][:, :].rearrange("p (c t) -> p c t", c=DC)
            if n == 0:
                for c in range(DC):
                    a = dve.scalar_tensor_tensor(xnT[:, 1, c, b * S:(b + 1) * S], src[:, c, :],
                                                 vecs[:, V_LNW + c:V_LNW + c + 1],
                                                 xnT[:, 0, c, b * S:(b + 1) * S].bitcast(F32), ALU.mult, ALU.subtract)
            else:
                a = dve.tensor_tensor(xnT[:, 1, :, b * S:(b + 1) * S], src, xnT[:, 0, :, b * S:(b + 1) * S].bitcast(F32),
                                      ALU.subtract)
            a.then_inc(ln_low, 1)

        def pe_tail(pe, n, out_of):
            for b in range(B):
                if out_of:
                    out_of(b)
                if n in LN_STAGES and b >= 4:
                    pe_ln_turn(pe, n, b - 4)
            if n in LN_STAGES:
                for b in range(4, B):
                    pe_ln_turn(pe, n, b)

        def act_tail(act, n):
            if n in LN_STAGES:
                for b in range(B):
                    act_ln_high(act, n, b)

        def dve_tail(dve, n, add_of):
            for b in range(B):
                if add_of:
                    add_of(b)
                if n > 7:
                    continue
                dve_ln_stats(dve, n, b)
                if b == BH - 1:
                    dve_ln_rstd(dve, n, 0)
                    if n in LN_STAGES:
                        for k in range(4):
                            dve_ln_norm(dve, n, k)
                elif b >= BH and n in LN_STAGES:
                    dve_ln_low(dve, n, b - BH)
            if n > 7:
                return
            dve_ln_rstd(dve, n, 1)
            if n in LN_STAGES:
                for b in range(4, B):
                    dve_ln_norm(dve, n, b)
                for b in range(4, B):
                    dve_ln_low(dve, n, b)

        def attention_sp(sp, A):
            m = A.events
            wk, wv, wq, wo = (ins[f"L{A.layer}_{k}"] for k in ("wk", "wv", "wq", "wo"))

            def load(g, j, what, source):
                n = A.tile(g, j, what)
                slot = A.tile(0, j, what) % A.ring
                m.wait(sp, "split", n - (A.ring - 1))
                sp.dma_start(ring[:, slot, :], source).then_inc(m["landed", slot], 16)

            def group(g):
                if not A.own_kv:
                    for what, j in A.SHARED_TILES:
                        n = g if what in "kv" else GH * g + j
                        load(g, j, what, {"k": wk, "v": wv, "q": wq, "o": wo}[what][bass.ds(n, 1)].rearrange("a p n -> (a p) n"))
                    return
                for j in range(GH):
                    h = GH * g + j
                    m.wait(sp, "masked", 2 * h - 2)
                    sp.dma_start(biasbuf[:, j % 2, :], ins["position_bias"][bass.ds(h, 1)].rearrange("a p n -> (a p) n"))\
                      .then_inc(m["bias_landed", j % 2], 16)
                    for what, w in (("k", wk), ("v", wv), ("q", wq), ("o", wo)):
                        load(g, j, what, w[bass.ds(h, 1)].rearrange("a p n -> (a p) n"))

            group(0)
            with sp.Fori(1, NG) as g:
                group(g)

        def attention_pool(pool, A):
            m = A.events

            def split(g, j, what, dst, slot):
                n = A.tile(g, j, what)
                pos = A.tile(0, j, what)
                r = pos % A.ring
                m.wait(pool, ("landed", r), 16 * ((A.tiles // A.ring) * g + (pos // A.ring + 1)))
                pool.tensor_tensor(dst[:, slot, 0, :], ring[:, r, :], zeros512, ALU.add).then_inc(m["high_w"], 1)
                m.wait(pool, "high_w", n + 1)
                pool.tensor_tensor(dst[:, slot, 1, :], ring[:, r, :], dst[:, slot, 0, :].bitcast(F32),
                                   ALU.subtract).then_inc(m["split"], 1)

            def split_q(g, j):
                if not (isinstance(g, int) and g == 0 and j < 2):
                    before = (g, j - 2) if j >= 2 else (g - 1, j + 2)
                    m.wait(pool, ("pfull", 1), A.projection(*before, "q") + 1)
                split(g, j, "q", w_in, j % 2)

            def split_o(g, j):
                if not (isinstance(g, int) and g == 0):
                    m.wait(pool, "outfull", B * (2 * g + (j // 2 - 1)))
                elif j == 0:
                    wait_before(pool, A, out=True)
                split(g, j, "o", w_out, j)

            def split_kv(g, what):
                if not (isinstance(g, int) and g == 0):
                    m.wait(pool, ("pfull", 1), A.projection(g - 1, 0, what) + 1)
                split(g, 0, what, w_kv, "kv".index(what))

            def square_q(g, j):
                for half in range(2):
                    m.wait(pool, ("pfree", half), A.projection(g, j, "q") + 1)
                if not (isinstance(g, int) and g == 0 and j == 0):
                    m.wait(pool, "tfull", A.turn(*((g, j - 2) if j >= 2 else (g - 1, j + 2)), "Q") + 1)
                pool.tensor_tensor(sq[:, :], qT, qT, ALU.mult).then_inc(m["squared"], 1)

            def square_k(g):
                for half in range(2):
                    m.wait(pool, ("pfree", half), A.projection(g, 0, "k") + 1)
                if not (isinstance(g, int) and g == 0):
                    m.wait(pool, "tfull", A.turn(g - 2, 3, "B1") + 1)
                pool.tensor_tensor(ksq, kraw, kraw, ALU.mult).then_inc(m["squared"], 1)

            def own_group(g):
                for j in range(GH):
                    for n, what in enumerate("kv"):
                        if not (isinstance(g, int) and g == 0 and j < 2):
                            before = (g, j - 2) if j >= 2 else (g - 1, j + 2)
                            m.wait(pool, ("pfull", 1), A.projection(*before, what) + 1)
                        split(g, j, what, (w_kv, w_kv2)[j % 2], n)
                    split_q(g, j)
                    split_o(g, j)

            def shared_group(g, last=False):
                split_o(g, 0)
                split_q(g, 2)
                split_o(g, 1)
                if A.normed:
                    square_q(g, 1)
                split_q(g, 3)
                if A.normed:
                    square_q(g, 2)
                split_o(g, 2)
                split_o(g, 3)
                if not last:
                    split_kv(g + 1, "k")
                    split_kv(g + 1, "v")
                    split_q(g + 1, 0)
                if A.normed:
                    square_q(g, 3)
                if not last:
                    if A.normed:
                        square_k(g + 1)
                    split_q(g + 1, 1)
                    if A.normed:
                        square_q(g + 1, 0)

            wait_before(pool, A, out=False)
            if A.layer == 3:
                pool.wait_ge(M2["outfull"], B)
            if A.own_kv:
                own_group(0)
                with pool.Fori(1, NG) as g:
                    own_group(g)
                return
            split_kv(0, "k")
            split_kv(0, "v")
            split_q(0, 0)
            if A.normed:
                square_k(0)
            split_q(0, 1)
            if A.normed:
                square_q(0, 0)
            shared_group(0)
            with pool.Fori(1, NG - 1) as g:
                shared_group(g)
            shared_group(NG - 1, last=True)

        def after(g, j):
            return (g, j + 1) if j < GH - 1 else (g + 1, 0)

        def needed_next(A, g, j):
            last = isinstance(g, int) and g == NG - 1
            if A.own_kv:
                return [] if last and j == GH - 1 else [(*after(g, j), what) for what in "kvq"]
            if A.normed and j == GH - 2:
                return [(g, j + 1, "q")] + ([] if last else [(g + 1, 0, "k")])
            if j < GH - 1:
                return [(g, j + 1, "q")]
            return [] if last else [(g + 1, 0, what) for what in ("vq" if A.normed else "kvq")]

        def new_values(A, g, j):
            return A.new_kv((j + 1) % GH) and not (isinstance(g, int) and g == NG - 1 and j == GH - 1)

        def pending(g, j):
            if isinstance(g, int) and g == 0 and j < 2:
                return g, 0, [[]] * 5
            at = (g, 0) if j >= 2 else (g - 1, 1)
            return (*at, [[0], [1], [2], [3], [4]] if j % 2 == 0 else [[5], [6], [7], [], []])

        def attention_pe(pe, A):
            m = A.events
            unit = lambda g, j, half: 2 * (GH * g + j) + half

            def project(g, j, what):
                n = A.projection(g, j, what)
                w, slot, act = {"k": (w_kv, 0, ctxT), "v": (w_kv, 1, ctxT), "q": (w_in, j % 2, xnT)}[what]
                if A.own_kv and what != "q" and j % 2:
                    w = w_kv2
                m.wait(pe, "split", A.tile(g, j, what) + 1)
                for half in range(2):
                    m.wait(pe, ("pfree", half), n)
                    if what == "q" and isinstance(g, int) and g == 0 and j == 0:
                        pe.wait_ge(ln_low, 8 * ln_no(A.stage) + BH * (half + 1))
                    pe_project(pe, w, slot, act, half).then_inc(m["pfull", half], 1)

            def use_turn(n):
                m.wait(pe, "tfree", n)

            def turn_values(g, j, half):
                use_turn(A.turn(g, j, f"V{half}"))
                if half == 0:
                    k = A.projection(*after(g, j), "v") if not (isinstance(g, int) and g < 0) else 1
                    for i in range(2):
                        m.wait(pe, ("pfree", i), k + 1)
                for b in range(BH):
                    mm = pe.transpose(turn[:, b * P:(b + 1) * P], vT[:, (half * BH + b) * S:(half * BH + b + 1) * S], ident)
                mm.then_inc(m["tfull"], 1)

            def sum_squares(g, j, what, g2, j2):
                use_turn(A.turn(g, j, what))
                m.wait(pe, "squared", 5 * g2 + (1 if what == "K" else 2 + j2))
                src = ksq if what == "K" else sq
                for b in range(B):
                    mm = pe.matmul(turn[:, b:b + 1], src[:, b * S:(b + 1) * S], consts[:, C_MEAN:C_MEAN + 1],
                                   start=True, stop=True)
                mm.then_inc(m["tfull"], 1)

            def spread(g, j, g2, half):
                use_turn(A.turn(g, j, f"B{half}"))
                if half == 0:
                    m.wait(pe, "diag", g2 + 1)
                for b in range(half * BH, (half + 1) * BH):
                    mm = pe.matmul(turn[:, (b % BH) * P:(b % BH + 1) * P], ones, diagonals[:, b * P:(b + 1) * P],
                                   start=True, stop=True)
                mm.then_inc(m["tfull"], 1)

            def out_product(g, pair, bs):
                p = 2 * g + pair
                if bs[0] == 0:
                    m.wait(pe, "low", 4 * (p + 1))
                    m.wait(pe, "split", A.tile(g, 2 * pair + 1, "o") + 1)
                for b in bs:
                    m.wait(pe, "added", B * p + (b - 1))
                    pe_out(pe, b, (2 * pair, 2 * pair + 1)).then_inc(m["outfull"], 1)

            def step(g, j):
                out_g, pair, at_place = pending(g, j)

                def out_at(place):
                    if at_place[place]:
                        out_product(out_g, pair, at_place[place])

                for half in range(2):
                    u = unit(g, j, half)
                    if half == 0:
                        for i in range(2):
                            m.wait(pe, ("pfree", i), A.projection(g, j, "q") + 1)
                        if A.normed and j == 0:
                            m.wait(pe, "tfree", A.turn(g - 1, 3, "B1") + 1)
                    m.wait(pe, "exps" if A.layer == 3 else "sfree", u - 1)
                    for b in range(BH):
                        t = slice((half * BH + b) * S, (half * BH + b + 1) * S)
                        mm = pe.matmul(score[half][:, b * P:(b + 1) * P], qT[:, t], kT[:, t], start=True, stop=True)
                    mm.then_inc(m["sfull"], 1)
                for n, new in enumerate(needed_next(A, g, j)):
                    project(*new)
                    if A.normed and j == GH - 1:
                        spread(g, j, g + 1, n)
                out_at(0)
                for half in range(2):
                    n = A.turn(g, j, f"T{half}")
                    use_turn(n)
                    m.wait(pe, "pready", unit(g, j, half) + 1)
                    for b in range(BH):
                        mm = pe.transpose(turn[:, b * P:(b + 1) * P], pbuf[:, half, b * P:(b + 1) * P], ident)
                    mm.then_inc(m["tfull"], 1)
                    out_at(1 + half)
                    m.wait(pe, "tfree", n + 1)
                    m.wait(pe, "low", unit(g, j, half))
                    for b in range(BH):
                        mm = pe.matmul(heado[:, b * P:(b + 1) * P], v[:, (half * BH + b) * S:(half * BH + b + 1) * S],
                                       ptbuf[:, half, b * P:(b + 1) * P], start=True, stop=True)
                    mm.then_inc(m["pv"], 1)
                if new_values(A, g, j):
                    turn_values(g, j, 0)
                out_at(3)
                if new_values(A, g, j):
                    turn_values(g, j, 1)
                out_at(4)
                if A.normed:
                    for g2, j2, what in needed_next(A, g, j):
                        if what != "v":
                            sum_squares(g, j, what.upper(), g2, j2)

            def group(g):
                for j in range(GH):
                    step(g, j)

            project(0, 0, "k")
            project(0, 0, "v")
            if A.normed:
                sum_squares(-1, 3, "K", 0, 0)
            project(0, 0, "q")
            for half in range(2):
                if A.normed:
                    spread(-1, 3, 0, half)
            for half in range(2):
                turn_values(-1, 3, half)
            if A.normed:
                sum_squares(-1, 3, "Q", 0, 0)
            group(0)
            with pe.Fori(1, NG - 1) as g:
                group(g)
            group(NG - 1)
            pe_tail(pe, A.stage + 1, lambda b: out_product(NG - 1, 1, [b]))

        def copy_projection(engine, on_act, dst, src, bias):
            if on_act:
                if bias is None:
                    return engine.activation(dst, src, ACT.Copy)
                return engine.activation(dst, src, ACT.Identity, bias=bias)
            if bias is None:
                return engine.tensor_copy(dst, src)
            return engine.tensor_scalar(dst, src, bias, None, ALU.add)

        def take_projection(engine, on_act, A, g, j, what):
            m = A.events
            half = 0 if on_act else 1
            m.wait(engine, ("pfull", half), A.projection(g, j, what) + 1)
            dst = {"k": kraw if A.normed else kT, "v": vT, "q": qT}[what][:, half * HALF:(half + 1) * HALF]
            bias = None
            if A.layer == 3:
                base, n = {"k": (V_BK3, g), "v": (V_BV3, g), "q": (V_BQ3, GH * g + j)}[what]
                bias = vecs[:, bass.ds(base + n, 1)]
            copy_projection(engine, on_act, dst, proj[half][:, :], bias).then_inc(m["pfree", half], 1)

        def take_values(engine, on_act, A, g, j):
            m = A.events
            half = 0 if on_act else 1
            m.wait(engine, "tfull", A.turn(g, j, f"V{half}") + 1)
            dst = v[:, half * HALF:(half + 1) * HALF]
            copy_projection(engine, on_act, dst, turn[:, :], None).then_inc(m["tfree"], 1)

        def attention_act(act, A):
            m = A.events

            def step(g, j):
                for half in range(2):
                    u = 2 * (GH * g + j) + half
                    src = score[half] if A.layer == 3 else tbuf[:, half, :]
                    scale = A.scale if A.layer == 3 else 1.0
                    m.wait(act, "negmax", u + 1)
                    for b in range(BH):
                        a = act.activation(pbuf[:, half, b * P:(b + 1) * P], src[:, b * P:(b + 1) * P], ACT.Exp,
                                           bias=negmax[:, half, b:b + 1], scale=scale,
                                           accum_out=rowsum[:, half, b:b + 1])
                    a.then_inc(m["exps"], 1)
                for new in needed_next(A, g, j):
                    take_projection(act, True, A, *new)
                for half in range(2):
                    u = 2 * (GH * g + j) + half
                    m.wait(act, "tfull", A.turn(g, j, f"T{half}") + 1)
                    act.activation(ptbuf[:, half, :], turn[:, :], ACT.Copy).then_inc(m["tfree"], 1)
                    m.wait(act, "pv", u + 1)
                    act.activation(acts[:, j, 0, half * HALF:(half + 1) * HALF], heado[:, :], ACT.Copy)\
                       .then_inc(m["high"], 1)
                if new_values(A, g, j):
                    take_values(act, True, A, g, j)

            def group(g):
                for j in range(GH):
                    step(g, j)

            for what in "kv":
                take_projection(act, True, A, 0, 0, what)
            take_projection(act, True, A, 0, 0, "q")
            take_values(act, True, A, -1, 3)
            group(0)
            with act.Fori(1, NG - 1) as g:
                group(g)
            group(NG - 1)
            act_tail(act, A.stage + 1)

        def attention_dve(dve, A):
            m = A.events

            def scores(g, j, half):
                h = GH * g + j
                u = 2 * h + half
                blocks = lambda ap: ap.rearrange("p (b k) -> p b k", b=BH)
                m.wait(dve, "sfull", u + 1)
                src = blocks(score[half][:, :])
                if A.layer == 0:
                    if half == 0:
                        m.wait(dve, ("bias_landed", j % 2), 16 * (2 * g + (j // 2 + 1)))
                    t = blocks(tbuf[:, half, :])
                    dve.tensor_tensor(t, src, biasbuf[:, j % 2:j % 2 + 1, :].broadcast_to([P, BH, S]), ALU.add)\
                       .then_inc(m["sfree"], 1)
                    m.wait(dve, "sfree", u + 1)
                    dve.tensor_tensor(t, t, maskadd[:, half * BH:(half + 1) * BH, :], ALU.add).then_inc(m["masked"], 1)
                    m.wait(dve, "masked", u + 1)
                    src = t
                elif A.layer == 2:
                    for b in range(BH):
                        n = half * BH + b
                        a = dve.scalar_tensor_tensor(tbuf[:, half, b * P:(b + 1) * P], score[half][:, b * P:(b + 1) * P],
                                                     rq[:, n:n + 1], maskadd[:, 0, :], ALU.mult, ALU.add)
                    a.then_inc(m["sfree"], 1)
                    m.wait(dve, "sfree", u + 1)
                    src = blocks(tbuf[:, half, :])
                dve.tensor_reduce(rowmax[:, half, 0:BH], src, AX.X, ALU.max).then_inc(m["rowmax"], 1)
                m.wait(dve, "rowmax", u + 1)
                dve.tensor_scalar(negmax[:, half, 0:BH], rowmax[:, half, 0:BH], -A.scale if A.layer == 3 else -1.0,
                                  None, ALU.mult).then_inc(m["negmax"], 1)

            def normalise(g, j, half):
                u = 2 * (GH * g + j) + half
                m.wait(dve, "exps", u + 1)
                dve.reciprocal(rinv[:, half, 0:BH], rowsum[:, half, 0:BH]).then_inc(m["rinv"], 1)
                m.wait(dve, "rinv", u + 1)
                if A.layer == 0:
                    dve.tensor_tensor(rinv[:, half, 0:BH], rinv[:, half, 0:BH], live[:, half * BH:(half + 1) * BH],
                                      ALU.mult).then_inc(m["rlive"], 1)
                    m.wait(dve, "rlive", u + 1)
                pb = pbuf[:, half, :].rearrange("p (b k) -> p b k", b=BH)
                dve.tensor_tensor(pb, pb, rinv[:, half, 0:BH].unsqueeze(2).broadcast_to([P, BH, S]), ALU.mult)\
                   .then_inc(m["pready"], 1)

            def rms(g, j, what):
                order = {"K": 3, "Q": 4 if j == 3 else j}[what]
                calls = ({"K": 0, "Q": 1}[what]) if isinstance(g, int) and g < 0 else 2 + 5 * g + order
                dst = rk if what == "K" else rq
                m.wait(dve, "tfull", A.turn(g, j, what) + 1)
                dve.tensor_scalar(nw_v[:, :], turn[:, 0:B], EPS, None, ALU.add).then_inc(m["tfree"], 1)
                m.wait(dve, "tfree", A.turn(g, j, what) + 1)
                dve_rsqrt(dve, dst[:, :], nw_v[:, :], nw_t[:, :], m["shifted"], m["newton"], calls)
                if what == "Q":
                    dve.tensor_scalar(rq[:, :], rq[:, :], A.scale, None, ALU.mult).then_inc(m["rsq"], 1)
                    m.wait(dve, "rsq", (0 if isinstance(g, int) and g < 0 else GH * g + (j + 1)) + 1)

            def make_diagonals():
                for b in range(B):
                    a = dve.tensor_scalar(diagonals[:, b * P:(b + 1) * P], ident, rk[:, b:b + 1], None, ALU.mult)
                a.then_inc(m["diag"], 1)

            def norm_keys(g, j, g2, half):
                cols = slice(half * HALF, (half + 1) * HALF)
                m.wait(dve, "tfull", A.turn(g, j, f"B{half}") + 1)
                m.wait(dve, ("pfree", half), A.projection(g2, 0, "k") + 1)
                dve.scalar_tensor_tensor(kT[:, cols], kraw[:, cols], kqn[:, 0:1], turn[:, :], ALU.mult, ALU.mult)\
                   .then_inc(m["tfree"], 1)

            def add(p, b):
                m.wait(dve, "added", B * p + (b - B + 1))
                m.wait(dve, "outfull", B * p + (b + 1))
                dve.tensor_tensor(x[:, b, :], x[:, b, :], outp[b % 2][:, :], ALU.add).then_inc(m["added"], 1)

            def step(g, j):
                out_g, pair, at_place = pending(g, j)

                def add_at(place):
                    for b in at_place[place]:
                        add(2 * out_g + pair, b)

                new = needed_next(A, g, j)
                spreads = A.normed and j == GH - 1 and new
                for half in range(2):
                    scores(g, j, half)
                normalise(g, j, 0)
                if spreads:
                    norm_keys(g, j, g + 1, 0)
                normalise(g, j, 1)
                for n in new:
                    take_projection(dve, False, A, *n)
                if spreads:
                    norm_keys(g, j, g + 1, 1)
                add_at(0)
                for half in range(2):
                    add_at(1 + half)
                    u = 2 * (GH * g + j) + half
                    m.wait(dve, "high", u + 1)
                    cols = slice(half * HALF, (half + 1) * HALF)
                    dve.tensor_tensor(acts[:, j, 1, cols], heado[:, :], acts[:, j, 0, cols].bitcast(F32), ALU.subtract)\
                       .then_inc(m["low"], 1)
                add_at(3)
                if new_values(A, g, j):
                    take_values(dve, False, A, g, j)
                add_at(4)
                if A.normed:
                    for g2, j2, what in new:
                        if what == "q":
                            rms(g, j, "Q")
                        elif what == "k":
                            rms(g, j, "K")
                            make_diagonals()

            def group(g):
                for j in range(GH):
                    step(g, j)

            if A.layer == 3:
                add_row(dve, 1)
            for what in "kv":
                take_projection(dve, False, A, 0, 0, what)
            if A.normed:
                rms(-1, 3, "K")
                make_diagonals()
            take_projection(dve, False, A, 0, 0, "q")
            for half in range(2):
                if A.normed:
                    norm_keys(-1, 3, 0, half)
            take_values(dve, False, A, -1, 3)
            if A.normed:
                rms(-1, 3, "Q")
            group(0)
            with dve.Fori(1, NG - 1) as g:
                group(g)
            group(NG - 1)

            def last_add(b):
                add(NPAIR - 1, b)
                m.wait(dve, "added", B * (NPAIR - 1) + b + 1)

            dve_tail(dve, A.stage + 1, last_add)

        def ffn_run(engine, A, emit):
            last = (A.chunks - 1) // GH
            emit(0, range(GH))
            if last > 2:
                with engine.Fori(1, last) as g:
                    emit(g, range(GH))
            else:
                emit(1, range(GH))
            emit(last, range(A.chunks - GH * last))

        def ffn_sp(sp, A):
            m = A.events
            if A.low_rank:
                sp.dma_start(brow[:, :], ins[f"{A.name}_pre"]).then_inc(m["pre_landed"], 16)
                for dst, src in A.small:
                    sp.dma_start(dst, src).then_inc(m["small_landed"], 16)

            def chunks(g, js):
                for j in js:
                    c = GH * g + j
                    for k, what in enumerate(A.what):
                        n = A.tile(g, j, k)
                        slot = (len(A.what) * j + k) % A.ring
                        m.wait(sp, "split", n - (A.ring - 1))
                        sp.dma_start(ring[:, slot, :], ins[f"{A.name}_{what}"][bass.ds(c, 1)].rearrange("a p n -> (a p) n"))\
                          .then_inc(m["landed", slot], 16)

            ffn_run(sp, A, chunks)

        def ffn_pool(pool, A):
            m = A.events

            def tiles_of(g, j):
                for k, what in enumerate(A.what):
                    r = (len(A.what) * j + k) % A.ring
                    n = A.tile(g, j, k)
                    early = isinstance(g, int) and g == 0
                    if what == "in":
                        dst = w_in[:, j % 2]
                        if not (early and j < 2):
                            m.wait(pool, ("pfull", 1), GH * g + (j - 2 + A.low_rank + 1))
                    elif what == "in2":
                        dst = w_kv[:, j % 2]
                        if not (early and j < 2):
                            m.wait(pool, "sfull", 2 * (GH * g + (j - 2)) + 2)
                        elif j == 1 and A.low_rank:
                            m.wait(pool, ("pfull", 1), 1)
                    else:
                        dst = w_out[:, j]
                        if early and j == 0:
                            wait_before(pool, A, out=True)
                        if not early:
                            m.wait(pool, "outfull", B * (2 * g + (j // 2 - 1)))
                    m.wait(pool, ("landed", r), 16 * ((GH * len(A.what) // A.ring) * g + ((len(A.what) * j + k) // A.ring + 1)))
                    pool.tensor_tensor(dst[:, 0, :], ring[:, r, :], zeros512, ALU.add).then_inc(m["high_w"], 1)
                    m.wait(pool, "high_w", n + 1)
                    pool.tensor_tensor(dst[:, 1, :], ring[:, r, :], dst[:, 0, :].bitcast(F32), ALU.subtract)\
                        .then_inc(m["split"], 1)

            def chunks(g, js):
                for j in js:
                    c = GH * g + j
                    if not (isinstance(c, int) and c == A.chunks - 1):
                        tiles_of(*after(g, j))
                    for half in range(2):
                        if A.kind == "pick":
                            u = 2 * c + half
                            m.wait(pool, "equal", u + 1)
                            e = ptbuf[:, half, :].rearrange("p (k i) -> p k i", i=32)
                            pool.tensor_tensor(e, e, consts[:, C_FIRST:C_FIRST + 32].unsqueeze(1).broadcast_to([P, 16, 32]),
                                               ALU.mult).then_inc(m["weighed"], 1)
                    for half in range(2):
                        u = 2 * c + half
                        m.wait(pool, "made", u + 1)
                        if not (isinstance(g, int) and g == 0):
                            m.wait(pool, "outfull", B * (2 * g + (j // 2 - 1)))
                        pool.tensor_tensor(acts[:, j, 0, half * HALF:(half + 1) * HALF], pbuf[:, half, :], zeros512,
                                           ALU.add).then_inc(m["high"], 1)

            wait_before(pool, A, out=False)
            if A.low_rank:
                m.wait(pool, "pre_landed", 16)
                pool.tensor_tensor(w_kv[:, 1, 0, :], brow[:, :], zeros512, ALU.add).then_inc(m["pre_split"], 1)
                m.wait(pool, "pre_split", 1)
                pool.tensor_tensor(w_kv[:, 1, 1, :], brow[:, :], w_kv[:, 1, 0, :].bitcast(F32), ALU.subtract)\
                    .then_inc(m["pre_split"], 1)
            tiles_of(0, 0)
            ffn_run(pool, A, chunks)

        def ffn_pe(pe, A):
            m = A.events
            pre = int(A.low_rank)
            low = big[0:48, 0, :]

            def second_low(g, j):
                c = GH * g + j
                for half in range(2):
                    m.wait(pe, "made", 2 * c + half + 1)
                    mm = pe.matmul(ln_banks[half][0:16, :], a2[:, c * 16:(c + 1) * 16], pbuf[:, half, :], start=isinstance(c, int) and c == 0,
                                   stop=isinstance(c, int) and c == A.chunks - 1)
                    mm.then_inc(m["lowfull"], 1)

            def out_product(p, slots, bs, last):
                if bs[0] == 0:
                    m.wait(pe, "low", 4 * p + 2 * len(slots))
                    m.wait(pe, "split", A.out_tile(p, slots))
                for b in bs:
                    m.wait(pe, "added", B * p + (b - 1))
                    more = last and A.kind == "silu"
                    mm = pe_out(pe, b, slots, last=not more)
                    if more:
                        if b == 0:
                            m.wait(pe, "low2", 2)
                        mm = pe.matmul(outp[b % 2][:, :], sq[0:16, b * S:(b + 1) * S], b2, start=False, stop=True)
                    mm.then_inc(m["outfull"], 1)

            def chunks(g, js):
                for j in js:
                    c = GH * g + j
                    first = isinstance(c, int) and c == 0
                    if A.kind == "pick":
                        for half in range(2):
                            if half == 0:
                                m.wait(pe, "equal", 2 * c)
                            for b in range(BH):
                                t = half * BH + b
                                mm = pe.matmul(score[half][:, b * P:(b + 1) * P], low[0:16, t * S:(t + 1) * S],
                                               flat[0:16, bass.ds(T + P * c, P)], start=True, stop=True)
                            mm.then_inc(m["sfull"], 1)
                    m.wait(pe, "split", A.tile(g, j, 0) + 1)
                    for half in range(2):
                        if A.kind == "gelu":
                            m.wait(pe, "made", 2 * c + half - 1)
                        else:
                            m.wait(pe, ("pfree", half), c + pre)
                        mm = pe_matmuls(pe, proj[half][:, :], lambda a, k: w_in[:, j % 2, a, k * P:(k + 1) * P],
                                        lambda b, k: xnT[:, b, k, half * HALF:(half + 1) * HALF], last=A.kind != "silu")
                        if A.kind == "silu":
                            mm = pe.matmul(proj[half][:, :], flat[0:16, T + c * P:T + (c + 1) * P], big[0:16, 0, half * HALF:(half + 1) * HALF],
                                           start=False, stop=True)
                        mm.then_inc(m["pfull", half], 1)
                    if A.kind == "silu":
                        if not first:
                            second_low(*((g, j - 1) if j else (g - 1, GH - 1)))
                        m.wait(pe, "split", A.tile(g, j, 1) + 1)
                        for half in range(2):
                            m.wait(pe, "made", 2 * c + half - 1)
                            pe_matmuls(pe, score[half][:, :], lambda a, k: w_kv[:, j % 2, a, k * P:(k + 1) * P],
                                       lambda b, k: xnT[:, b, k, half * HALF:(half + 1) * HALF], last=False)
                            pe.matmul(score[half][:, :], flat[32:48, T + c * P:T + (c + 1) * P], big[32:48, 0, half * HALF:(half + 1) * HALF],
                                      start=False, stop=True).then_inc(m["sfull"], 1)
                    if j % 2 == 0 and not first:
                        out_product(2 * g + (0 if j else -1), (0, 1) if j else (2, 3), range(B), False)
                    if A.kind == "pick":
                        for half in range(2):
                            m.wait(pe, "made", 2 * c + half - 1)
                            m.wait(pe, "picked", 2 * c + half + 1)
                            for b in range(BH):
                                mm = pe.transpose(ln_banks[half][:, b * P:(b + 1) * P], ptbuf[:, half, b * P:(b + 1) * P],
                                                  ident)
                            mm.then_inc(m["tfull"], 1)

            if A.kind == "pick":
                m.wait(pe, "small_landed", 16)
            if A.low_rank:
                m.wait(pe, "pre_split", 2)
                m.wait(pe, "small_landed", 16 * len(A.small))
                for half in range(2):
                    pe.wait_ge(ln_low, 8 * ln_no(A.stage) + BH * (half + 1))
                    pe_project(pe, w_kv, 1, xnT, half).then_inc(m["pfull", half], 1)
                for half in range(2):
                    m.wait(pe, ("pfree", half), 1)
            else:
                pe.wait_ge(ln_low, 8 * ln_no(A.stage) + B)
            ffn_run(pe, A, chunks)
            if A.kind == "silu":
                second_low(*divmod(A.chunks - 1, GH))
            p = (A.chunks - 1) // 2
            s = 2 * (p % 2)
            slots = (s, s + 1) if A.chunks % 2 == 0 else (s,)
            pe_tail(pe, A.stage + 1, lambda b: out_product(p, slots, [b], True))

        def ffn_act(act, A):
            m = A.events
            pre = int(A.low_rank)

            def chunks(g, js):
                for j in js:
                    c = GH * g + j
                    for half in range(2):
                        m.wait(act, ("pfull", half), c + pre + 1)
                        if A.kind == "gelu":
                            m.wait(act, "low", 2 * c + half - 1)
                            a = act.activation(pbuf[:, half, :], proj[half][:, :], ACT.Gelu_apprx_tanh,
                                               bias=vecs[:, bass.ds(V_BI + 16 * half + c, 1)])
                            a.then_inc(m["made"], 1)
                            continue
                        m.wait(act, "made", 2 * c + half - 1)
                        act.activation(tbuf[:, half, :], proj[half][:, :], ACT.Silu if A.kind == "silu" else ACT.Relu)\
                           .then_inc(m["pfree", half], 1)

            if A.low_rank:
                for half in range(2):
                    m.wait(act, ("pfull", half), 1)
                    act.activation(big[0:48, 0, half * HALF:(half + 1) * HALF], proj[half][0:48, :], ACT.Copy,
                                   scale=2.0 if A.kind == "silu" else 1.0).then_inc(m["pfree", half], 1)
            ffn_run(act, A, chunks)
            if A.kind == "silu":
                m.wait(act, "lowfull", 2 * A.chunks)
                for half in range(2):
                    act.activation(sq[0:16, half * HALF:(half + 1) * HALF], ln_banks[half][0:16, :], ACT.Copy, scale=2.0)\
                       .then_inc(m["low2"], 1)
            act_tail(act, A.stage + 1)

        def ffn_dve(dve, A):
            m = A.events

            def add(p, b):
                m.wait(dve, "added", B * p + (b - B + 1))
                m.wait(dve, "outfull", B * p + (b + 1))
                dve.tensor_tensor(x[:, b, :], x[:, b, :], outp[b % 2][:, :], ALU.add).then_inc(m["added"], 1)

            def low_part(c, j, half):
                m.wait(dve, "high", 2 * c + half + 1)
                cols = slice(half * HALF, (half + 1) * HALF)
                dve.tensor_tensor(acts[:, j, 1, cols], pbuf[:, half, :], acts[:, j, 0, cols].bitcast(F32), ALU.subtract)\
                   .then_inc(m["low"], 1)

            def pick(c):
                blocks = lambda ap: ap.rearrange("p (k i) -> p k i", i=32)
                spread = lambda ap: ap.unsqueeze(2).broadcast_to([P, 16, 32])
                for half in range(2):
                    u = 2 * c + half
                    m.wait(dve, "sfull", u + 1)
                    dve.tensor_reduce(blockmax[:, half, :], blocks(score[half][:, :]), AX.X, ALU.max).then_inc(m["bmax"], 1)
                    m.wait(dve, "bmax", u + 1)
                    m.wait(dve, "tfull", u - 1)
                    dve.tensor_tensor(blocks(ptbuf[:, half, :]), blocks(score[half][:, :]), spread(blockmax[:, half, :]),
                                      ALU.is_equal).then_inc(m["equal"], 1)
                for half in range(2):
                    u = 2 * c + half
                    m.wait(dve, "weighed", u + 1)
                    dve.tensor_reduce(firstmax[:, half, :], blocks(ptbuf[:, half, :]), AX.X, ALU.max).then_inc(m["fmax"], 1)
                    m.wait(dve, "fmax", u + 1)
                    dve.tensor_tensor(blocks(ptbuf[:, half, :]), blocks(ptbuf[:, half, :]), spread(firstmax[:, half, :]),
                                      ALU.is_equal).then_inc(m["picked"], 1)

            def chunks(g, js):
                for j in js:
                    c = GH * g + j
                    first = isinstance(c, int) and c == 0
                    adds = [] if j % 2 or first else range(B)
                    p = 2 * g + (0 if j else -1)
                    if A.kind == "silu":
                        for half in range(2):
                            u = 2 * c + half
                            m.wait(dve, "sfull", u + 1)
                            m.wait(dve, ("pfree", half), c + 2)
                            m.wait(dve, "lowfull", u - 1)
                            m.wait(dve, "low", u - 1)
                            dve.tensor_tensor(pbuf[:, half, :], score[half][:, :], tbuf[:, half, :], ALU.mult)\
                               .then_inc(m["made"], 1)
                    if A.kind == "pick":
                        pick(c)
                        for b in adds:
                            add(p, b)
                        for half in range(2):
                            u = 2 * c + half
                            m.wait(dve, "tfull", u + 1)
                            m.wait(dve, ("pfree", half), c + 2)
                            m.wait(dve, "low", u - 1)
                            dve.tensor_tensor(pbuf[:, half, :], ln_banks[half][:, :], tbuf[:, half, :], ALU.mult)\
                               .then_inc(m["made"], 1)
                        adds = []
                    for b in list(adds)[:BH]:
                        add(p, b)
                    for half in range(2):
                        low_part(c, j, half)
                    for b in list(adds)[BH:]:
                        add(p, b)

            if A.row is not None:
                add_row(dve, A.row)
            ffn_run(dve, A, chunks)
            p = (A.chunks - 1) // 2

            def last_add(b):
                add(p, b)
                m.wait(dve, "added", B * p + b + 1)

            dve_tail(dve, A.stage + 1, last_add)

        def row_sp(sp, n, name):
            wait(sp, row_added, B * n)
            if n == 0:
                sp.wait_ge(L1["v_made"], B)
                sp.wait_ge(L1["out_full"], B)
            sp.dma_start(brow[:, :], ins[name].partition_broadcast(P)).then_inc(row_landed, 16)

        def add_row(dve, n):
            dve.wait_ge(row_landed, 16 * (n + 1))
            for b in range(B):
                dve.tensor_tensor(x[:, b, :], x[:, b, :], brow[:, :], ALU.add).then_inc(row_added, 1)
            dve.wait_ge(row_added, B * (n + 1))

        PATCH = D // P
        H1, DH1 = 8, 8
        E1 = H1 * DH1
        xn1 = [sq[:, i * D:(i + 1) * D] for i in range(2)]
        wq1, wk1, wv1 = (brow[:, i * E1:(i + 1) * E1] for i in range(3))
        wo1 = brow[0:E1, 3 * E1:3 * E1 + P]
        bv1 = brow[:, 3 * E1 + P:4 * E1 + P]
        q1, k1 = ([maskadd[:, j * BH:(j + 1) * BH, :].rearrange("p a n -> p (a n)"),
                   flat[:, 3 * T + j * D:3 * T + (j + 1) * D]] for j in range(2))
        bq1 = rrms[0:E1, 0:1]
        turn1 = [turn, outp[0]]
        sum1 = [heado, outp[1]]
        v1 = [ring[:, 4 + i, 0:PATCH * H1 * (DH1 + 1)].rearrange("p (n h d) -> p n h d", n=PATCH, h=H1)
              for i in range(2)]
        o1 = flat[:, 0:B * PATCH * E1]
        og = [flat[0:E1, B * PATCH * E1 + i * D:B * PATCH * E1 + (i + 1) * D] for i in range(2)]

        UNITS = 2 * PATCH

        def in_pairs(engine, emit):
            for b in range(2):
                emit(b, b)
            with engine.Fori(1, B // 2 - 1) as i:
                for k in range(2):
                    emit(2 * i + k, k)
            for b in range(2):
                emit(B - 2 + b, b)

        def is_last(b):
            return isinstance(b, int) and b == B - 1

        def l1_sp(sp):
            m = L1
            F0.events.wait(sp, "pre_split", 2)
            sp.dma_start(brow[:, 0:3 * E1 + P], ins["L1_w"]).then_inc(m["w_landed"], 16)
            sp.dma_start(bv1, ins["L1_bv"].partition_broadcast(P)).then_inc(m["w_landed"], 16)
            F0.events.wait(sp, "split", 3 * F0.chunks)

            def mask_row(b):
                return ins["mask1"][bass.ds(b, 1)].rearrange("a n -> (a n)").partition_broadcast(P)

            def batch(b, k):
                wait(sp, m["v_full"], b - 1)
                sp.dma_start(ring[:, k, :], ins["ctx_tok"][bass.ds(b, 1)].rearrange("a p n -> (a p) n"))\
                  .then_inc(m["ctx_landed", k], 16)
                wait(sp, m["k_made"], 2 * b - 2)
                sp.dma_start(ring[:, 2 + k, :], mask_row(b)).then_inc(m["mask_landed", k], 16)

            in_pairs(sp, batch)
            for b in range(B):
                if b < 2:
                    sp.wait_ge(m["k_made"], 2 * (B - 1 + b))
                else:
                    sp.wait_ge(m["out_biased"], b - 1)
                sp.dma_start(ring[:, 2 + b % 2, :], mask_row(b)).then_inc(m["mask_landed", b % 2], 16)

        def l1_pool(pool):
            m = L1

            def batch(b, k):
                pool.wait_ge(m["k_made"], 2 * b + 2)
                for n in range(PATCH):
                    pn = PATCH * b + n
                    wait(pool, m["sfull"], 2 * (pn - 1))
                    pool.tensor_tensor(kblock[0:E1 + 1, n % 2, :, :],
                                       k1[k][0:E1 + 1, n * P:(n + 1) * P].unsqueeze(1).broadcast_to([E1 + 1, H1, P]),
                                       consts[0:E1 + 1, C_HEADS:C_HEADS + H1].unsqueeze(2).broadcast_to([E1 + 1, H1, P]),
                                       ALU.mult).then_inc(m["blocked"], 1)

            in_pairs(pool, batch)

        def l1_pe(pe):
            m = L1
            pe.wait_ge(m["w_landed"], 32)
            pe.wait_ge(m["ones"], 5)

            def project_qk(b, k):
                pe.wait_ge(m["normed"], b + 1)
                wait(pe, m["k_biased"], b)
                wait(pe, m["v_made"], b)
                pe.matmul(proj[0][0:E1, :], wq1, xn1[k], start=True, stop=True)
                pe.matmul(proj[1][0:E1, :], wk1, xn1[k], start=True, stop=True).then_inc(m["qk_full"], 1)

            def project_v(b, k):
                pe.wait_ge(m["ctx_landed", k], 16 * (b // 2 + 1) if isinstance(b, int) else 8 * (b - k) + 16)
                pe.wait_ge(m["q_made"], b + 1)
                for n in range(PATCH):
                    mm = pe.matmul(proj[0][:, n * E1:(n + 1) * E1], ring[:, k, n * P:(n + 1) * P], wv1, start=True, stop=True)
                mm.then_inc(m["v_full"], 1)

            def turn_probs(u, s):
                wait(pe, m["tfree"], u - 1)
                pe.wait_ge(m["exps"], u + 1)
                for h in range(4):
                    mm = pe.transpose(turn1[s][:, h * P:(h + 1) * P], pbuf[:, s, h * P:(h + 1) * P], ident)
                mm.then_inc(m["tfull"], 1)

            def sum_values(b, u, k, n, s):
                pe.wait_ge(m["tfree"], u + 1)
                if s == 0:
                    wait(pe, m["onorm"], PATCH * b + (n - 1))
                    pe.wait_ge(m["v_made"], b + 1)
                for h in range(4):
                    at = (4 * s + h) * 9
                    mm = pe.matmul(sum1[n % 2][:, at:at + 9], ptbuf[:, s, h * P:(h + 1) * P], v1[k][:, n, 4 * s + h, :],
                                   start=True, stop=True)
                mm.then_inc(m["av"], 1)

            def back(b, k, n, s, steps):
                at = 2 * n + s - steps
                if at < 0:
                    b, k, at = b - 1, 1 - k, at + UNITS
                if isinstance(b, int) and b < 0:
                    return None
                return b, UNITS * b + at, k, at // 2, at % 2

            def batch(b, k):
                pe.wait_ge(m["q_made"], b + 1)
                for n in range(PATCH):
                    pn = PATCH * b + n
                    for s in range(2):
                        u = UNITS * b + (2 * n + s)
                        if s == 0:
                            pe.wait_ge(m["blocked"], pn + 1)
                        wait(pe, m["shifted"], u - 1)
                        pe.matmul(score[s][:, :], q1[k][0:E1 + 1, n * P:(n + 1) * P],
                                  kblock[0:E1 + 1, n % 2, 4 * s:4 * s + 4, :].rearrange("p h j -> p (h j)"),
                                  start=True, stop=True).then_inc(m["sfull"], 1)
                        if (n, s) == (1, 0) and not is_last(b):
                            project_qk(b + 1, 1 - k)
                        if (n, s) == (2, 0) and not is_last(b):
                            project_v(b + 1, 1 - k)
                        two = back(b, k, n, s, 2)
                        if two:
                            turn_probs(two[1], s)
                        three = back(b, k, n, s, 3)
                        if three:
                            sum_values(*three)

            project_qk(0, 0)
            project_v(0, 0)
            in_pairs(pe, batch)
            u = UNITS * B
            turn_probs(u - 2, 0)
            sum_values(B - 1, u - 3, 1, PATCH - 2, 1)
            turn_probs(u - 1, 1)
            sum_values(B - 1, u - 2, 1, PATCH - 1, 0)
            sum_values(B - 1, u - 1, 1, PATCH - 1, 1)

            def turn_outputs(b):
                wait(pe, m["oturned"], b - 1)
                for n in range(PATCH):
                    mm = pe.transpose(proj[b % 2][0:E1, n * P:(n + 1) * P], o1[:, (PATCH * b + n) * E1:(PATCH * b + n + 1) * E1],
                                      ident)
                mm.then_inc(m["osum"], 1)

            def out_product(b):
                if b + 1 < B:
                    turn_outputs(b + 1)
                pe.wait_ge(m["oturned"], b + 1)
                wait(pe, m["out_biased"], b - 1)
                pe.matmul(outp[b % 2][:, :], wo1, og[b % 2], start=True, stop=True).then_inc(m["out_full"], 1)

            pe.wait_ge(m["gelu"], 1)
            turn_outputs(0)
            pe_tail(pe, 3, out_product)

        def l1_act(act):
            m = L1

            def take_turned(u, s):
                act.wait_ge(m["tfull"], u + 1)
                wait(act, m["av"], u - 1)
                act.activation(ptbuf[:, s, :], turn1[s][:, :], ACT.Copy).then_inc(m["tfree"], 1)

            def take_qk(b, k):
                act.wait_ge(m["qk_full"], b + 1)
                wait(act, m["sfull"], UNITS * (b - 1))
                act.activation(q1[k][0:E1, :], proj[0][0:E1, :], ACT.Identity, bias=bq1, scale=float(DH1) ** -0.5)\
                   .then_inc(m["q_made"], 1)
                wait(act, m["blocked"], PATCH * (b - 1))
                act.activation(k1[k][0:E1, :], proj[1][0:E1, :], ACT.Identity, bias=vecs[0:E1, V_BK1:V_BK1 + 1])\
                   .then_inc(m["k_biased"], 1)

            def batch(b, k):
                for n in range(PATCH):
                    for s in range(2):
                        u = UNITS * b + (2 * n + s)
                        act.wait_ge(m["shifted"], u + 1)
                        wait(act, m["tfull"], u - 1)
                        act.activation(pbuf[:, s, :], tbuf[:, s, :], ACT.Exp).then_inc(m["exps"], 1)
                        if (n, s) == (1, 0) and not is_last(b):
                            take_qk(b + 1, 1 - k)
                        if not (isinstance(u, int) and u < 2):
                            take_turned(u - 2, s)

            act.wait_ge(m["ones"], 5)
            take_qk(0, 0)
            in_pairs(act, batch)
            for s in range(2):
                take_turned(UNITS * B - 2 + s, s)
            act.wait_ge(m["onorm"], B * PATCH)
            act.activation(o1, o1, ACT.Gelu).then_inc(m["gelu"], 1)
            for b in range(B):
                act.wait_ge(m["osum"], b + 1)
                wait(act, m["out_full"], b - 1)
                act.activation(og[b % 2], proj[b % 2][0:E1, :], ACT.Copy).then_inc(m["oturned"], 1)
            act_tail(act, 3)

        def l1_dve(dve):
            m = L1
            F0.events.wait(dve, "split", 3 * F0.chunks)
            for i in range(2):
                dve.memset(v1[i][:, :, :, DH1:DH1 + 1], 1.0).then_inc(m["ones"], 1)
            for i in range(2):
                dve.memset(q1[i][E1:E1 + 1, :], 1.0).then_inc(m["ones"], 1)
            dve.tensor_scalar(bq1, vecs[0:E1, V_BQ1:V_BQ1 + 1], float(DH1) ** -0.5, None, ALU.mult).then_inc(m["ones"], 1)
            dve.wait_ge(ln_newton, 9 * LN_CALLS_AT_L1)
            dve.wait_ge(m["w_landed"], 32)

            def softmax(u, s):
                blocks = lambda ap: ap.rearrange("p (h j) -> p h j", h=4)
                dve.wait_ge(m["sfull"], u + 1)
                dve.tensor_reduce(rowmax[:, s, 0:4], blocks(score[s][:, :]), AX.X, ALU.max).then_inc(m["rowmax"], 1)
                dve.wait_ge(m["rowmax"], u + 1)
                wait(dve, m["exps"], u - 1)
                dve.tensor_tensor(blocks(tbuf[:, s, :]), blocks(score[s][:, :]),
                                  rowmax[:, s, 0:4].unsqueeze(2).broadcast_to([P, 4, P]), ALU.subtract).then_inc(m["shifted"], 1)

            def normalise(pn, n):
                dve.wait_ge(m["av"], 2 * pn + 2)
                o = sum1[n % 2][:, 0:H1 * 9].rearrange("p (h d) -> p h d", h=H1)
                dve.reciprocal(rinv[:, n % 2, :], o[:, :, DH1]).then_inc(m["v_inv"], 1)
                dve.wait_ge(m["v_inv"], pn + 1)
                dve.tensor_tensor(o1[:, bass.ds(pn * E1, E1)].rearrange("p (h d) -> p h d", h=H1), o[:, :, 0:DH1],
                                  rinv[:, n % 2, :].unsqueeze(2).broadcast_to([P, H1, DH1]), ALU.mult).then_inc(m["onorm"], 1)

            def norm(b, k):
                wait(dve, m["qk_full"], b - 1)
                dve.tensor_scalar(xn1[k], x[:, bass.ds(b, 1), :].rearrange("p a n -> p (a n)"),
                                  moments[:, bass.ds(b, 1), 0], rstd[:, bass.ds(b, 1)], ALU.subtract, ALU.mult)\
                   .then_inc(m["normed"], 1)

            def mask_keys(b, k):
                dve.wait_ge(m["k_biased"], b + 1)
                dve.wait_ge(m["mask_landed", k], 16 * (b // 2 + 1) if isinstance(b, int) else 8 * (b - k) + 16)
                mask = ring[:, 2 + k, :]
                dve.scalar_tensor_tensor(k1[k][0:E1, :], mask[0:E1, :], 0.0, k1[k][0:E1, :], ALU.is_gt, ALU.mult)\
                   .then_inc(m["k_made"], 1)
                dve.tensor_scalar(k1[k][E1:E1 + 1, :], mask[E1:E1 + 1, :], 0.0, -1e9, ALU.is_le, ALU.mult)\
                   .then_inc(m["k_made"], 1)

            def take_values(b, k):
                dve.wait_ge(m["v_full"], b + 1)
                wait(dve, m["av"], UNITS * (b - 1))
                dve.tensor_tensor(v1[k][:, :, :, 0:DH1],
                                  proj[0][:, 0:PATCH * E1].rearrange("p (n h d) -> p n h d", n=PATCH, h=H1),
                                  bv1.rearrange("p (h d) -> p h d", h=H1).unsqueeze(1).broadcast_to([P, PATCH, H1, DH1]),
                                  ALU.add).then_inc(m["v_made"], 1)

            def batch(b, k):
                for n in range(PATCH):
                    pn = PATCH * b + n
                    for s in range(2):
                        softmax(UNITS * b + (2 * n + s), s)
                        if s == 0 and n == 1 and not is_last(b):
                            mask_keys(b + 1, 1 - k)
                    if n == 0 and not is_last(b):
                        norm(b + 1, 1 - k)
                    if n == 2 and not is_last(b):
                        take_values(b + 1, 1 - k)
                    if not (isinstance(pn, int) and pn < 2):
                        normalise(pn - 2, n % 2)

            norm(0, 0)
            mask_keys(0, 0)
            take_values(0, 0)
            in_pairs(dve, batch)
            for n in range(2):
                normalise(PATCH * B - 2 + n, n)

            def add(b):
                dve.wait_ge(m["out_full"], b + 1)
                dve.wait_ge(m["mask_landed", b % 2], 16 * (B // 2 + b // 2 + 1))
                wait(dve, m["added"], b - 1)
                dve.scalar_tensor_tensor(ptbuf[:, b % 2, :], outp[b % 2][:, :], vecs[:, V_BO1:V_BO1 + 1],
                                         ring[:, 2 + b % 2, :], ALU.add, ALU.mult).then_inc(m["out_biased"], 1)
                dve.wait_ge(m["out_biased"], b + 1)
                dve.tensor_tensor(x[:, b, :], x[:, b, :], ptbuf[:, b % 2, :], ALU.add).then_inc(m["added"], 1)
                dve.wait_ge(m["added"], b + 1)

            dve_tail(dve, 3, add)

        EXPERTS, RANK = 8, 16
        ER = EXPERTS * RANK
        HL = ER + EXPERTS
        hl = flat[:, 0:B * HL].rearrange("p (b n) -> p b n", b=B)
        rt = [flat[:, 2048 + 64 * i:2048 + 64 * (i + 1)].rearrange("p (b e) -> p b e", b=B) for i in range(6)]

        def m2_sp(sp):
            m = M2
            LA[2].events.wait(sp, "split", LA[2].tiles * NG)
            sp.dma_start(ring[:, 0:4, 0:HL], ins["M2_a"]).then_inc(m["a_landed"], 16)
            sp.dma_start(ring[:, 5, :], ins["M2_b"]).then_inc(m["b_landed"], 16)
            row_sp(sp, 0, "M2_bias")
            sp.wait_ge(m["a_split"], 1)
            sp.dma_start(ring[:, 0:4, :], ins["M2_w"]).then_inc(m["w_landed"], 16)

        def m2_pool(pool):
            m = M2
            LA[2].events.wait(pool, "outfull", B * NPAIR)
            pool.wait_ge(m["a_landed"], 16)
            raw = ring[:, 0:4, 0:HL]
            pool.tensor_tensor(w_out[:, :, 0, 0:HL], raw, consts[:, C_ZERO:C_ZERO + 1].unsqueeze(2).broadcast_to([P, 4, HL]),
                               ALU.add).then_inc(m["a_high"], 1)
            pool.wait_ge(m["a_high"], 1)
            pool.tensor_tensor(w_out[:, :, 1, 0:HL], raw, w_out[:, :, 0, 0:HL].bitcast(F32), ALU.subtract)\
                .then_inc(m["a_split"], 1)
            pool.wait_ge(m["w_landed"], 16)
            for i, w in enumerate((w_in, w_kv)):
                raw = ring[:, 2 * i:2 * i + 2, :]
                pool.tensor_tensor(w[:, 0:2, 0, :], raw, consts[:, C_ZERO:C_ZERO + 1].unsqueeze(2).broadcast_to([P, 2, D]),
                                   ALU.add).then_inc(m["w_high"], 1)
                pool.wait_ge(m["w_high"], i + 1)
                pool.tensor_tensor(w[:, 0:2, 1, :], raw, w[:, 0:2, 0, :].bitcast(F32), ALU.subtract).then_inc(m["w_split"], 1)

        def m2_pe(pe):
            m = M2
            pe.wait_ge(m["a_split"], 1)
            for b in range(B):
                pe.wait_ge(ln_low, 8 * ln_no(5) + b + 1)
                wait(pe, m["copied"], b - 1)
                mm = pe_matmuls(pe, score[b % 2][:, 0:HL], lambda a, c: xnT[:, a, c, b * S:(b + 1) * S],
                                lambda a, c: w_out[:, c, a, 0:HL])
                mm.then_inc(m["full"], 1)
            pe.wait_ge(m["w_split"], 2)

            def base(b):
                wait(pe, m["added"], b - 1)
                pe_matmuls(pe, outp[b % 2][:, :], lambda a, c: xnT[:, a, c, b * S:(b + 1) * S],
                           lambda a, c: (w_in if c < 2 else w_kv)[:, c % 2, a, :], last=False)

            def turn_weighted(b):
                wait(pe, m["high"], b - 1)
                pe.transpose(proj[b % 2][:, 0:P], hl[:, b, 0:ER], ident).then_inc(m["turned"], 1)

            def product(b):
                if b >= 2:
                    base(b)
                if b + 1 < B:
                    turn_weighted(b + 1)
                pe.wait_ge(m["high"], b + 1)
                pe.matmul(outp[b % 2][:, :], ptbuf[:, b % 2, 0:P], ring[:, 5, :], start=False, stop=True)\
                  .then_inc(m["outfull"], 1)

            base(0)
            base(1)
            pe.wait_ge(m["b_landed"], 16)
            pe.wait_ge(m["weighted"], 1)
            turn_weighted(0)
            pe_tail(pe, 6, product)

        def m2_act(act):
            m = M2
            act.wait_ge(m["route"], 6)
            act.activation(rt[1], rt[1], ACT.Exp).then_inc(m["expd"], 1)
            for b in range(B):
                act.wait_ge(m["turned"], b + 1)
                wait(act, m["outfull"], b - 1)
                act.activation(ptbuf[:, b % 2, 0:P], proj[b % 2][:, 0:P], ACT.Copy).then_inc(m["high"], 1)
            act_tail(act, 6)

        def m2_dve(dve):
            m = M2
            add_row(dve, 0)
            for b in range(B):
                dve.wait_ge(m["full"], b + 1)
                dve.tensor_copy(hl[:, b, :], score[b % 2][:, 0:HL]).then_inc(m["copied"], 1)
            dve.wait_ge(m["copied"], B)
            logits = hl[:, :, ER:HL]
            wide = [t.rearrange("p (b e f) -> p b e f", b=B, e=EXPERTS) for t in (tbuf[:, 0, :], tbuf[:, 1, :])]
            mine = logits.unsqueeze(3).broadcast_to([P, B, EXPERTS, EXPERTS])
            other = logits.unsqueeze(2).broadcast_to([P, B, EXPERTS, EXPERTS])
            dve.tensor_tensor(wide[0], other, mine, ALU.is_gt).then_inc(m["route"], 1)
            dve.tensor_tensor(wide[1], other, mine, ALU.is_equal).then_inc(m["route"], 1)
            dve.wait_ge(m["route"], 2)
            less = consts[:, C_LESS:C_LESS + 64].unsqueeze(1).broadcast_to([P, B, 64])
            dve.tensor_tensor(tbuf[:, 1, :].rearrange("p (b n) -> p b n", b=B), tbuf[:, 1, :].rearrange("p (b n) -> p b n", b=B),
                              less, ALU.mult).then_inc(m["route"], 1)
            dve.wait_ge(m["route"], 3)
            dve.tensor_tensor(tbuf[:, 0, :], tbuf[:, 0, :], tbuf[:, 1, :], ALU.add).then_inc(m["route"], 1)
            dve.tensor_reduce(rowmax[:, 0, :], logits, AX.X, ALU.max).then_inc(m["route"], 1)
            dve.wait_ge(m["route"], 5)
            dve.tensor_tensor(rt[1], logits, rowmax[:, 0, :].unsqueeze(2).broadcast_to([P, B, EXPERTS]), ALU.subtract)\
               .then_inc(m["route"], 1)
            dve.tensor_reduce(rt[0], wide[0], AX.X, ALU.add).then_inc(m["route"], 1)
            dve.wait_ge(m["route"], 7)
            dve.wait_ge(m["expd"], 1)
            dve.scalar_tensor_tensor(rt[2], rt[0], 1.5, rt[1], ALU.is_lt, ALU.mult).then_inc(m["routed"], 1)
            dve.wait_ge(m["routed"], 1)
            dve.tensor_reduce(rowmax[:, 1, :], rt[2], AX.X, ALU.add).then_inc(m["routed"], 1)
            dve.wait_ge(m["routed"], 2)
            dve.reciprocal(rinv[:, 0, :], rowmax[:, 1, :]).then_inc(m["routed"], 1)
            dve.wait_ge(m["routed"], 3)
            dve.scalar_tensor_tensor(rt[3], rt[2], 2.0, rinv[:, 0, :].unsqueeze(2).broadcast_to([P, B, EXPERTS]),
                                     ALU.mult, ALU.mult).then_inc(m["routed"], 1)
            dve.wait_ge(m["routed"], 4)
            act_hl = hl[:, :, 0:ER].rearrange("p b (e r) -> p b e r", e=EXPERTS)
            dve.tensor_tensor(act_hl, act_hl, rt[3].unsqueeze(3).broadcast_to([P, B, EXPERTS, RANK]), ALU.mult)\
               .then_inc(m["weighted"], 1)

            def add(b):
                dve.wait_ge(m["outfull"], b + 1)
                dve.tensor_tensor(x[:, b, :], x[:, b, :], outp[b % 2][:, :], ALU.add).then_inc(m["added"], 1)
                dve.wait_ge(m["added"], b + 1)

            dve_tail(dve, 6, add)

        def start_sp(sp):
            sp.dma_start(consts[:, :], ins["consts"]).then_inc(consts_landed, 16)
            sp.dma_start(vecs[:, :], ins["vecs"]).then_inc(consts_landed, 16)
            for b in range(0, B, 4):
                sp.dma_start(x[:, b:b + 4, :], ins["x"][:, b:b + 4, :]).then_inc(x_landed, 16)
            for n in range(8):
                if n == 4:
                    sp.dma_start(mask_bytes[:, :], ins["mask0"]).then_inc(mask_landed, 16)
                if n >= 4:
                    sp.wait_ge(ctx_split, n - 3)
                sp.dma_start(ring[:, n % 4, :], ins["ctxT"][:, n // 2, (n % 2) * HALF:(n % 2 + 1) * HALF])\
                  .then_inc(ctx_landed[n % 4], 16)
            sp.wait_ge(ctx_split, 8)

        def start_pool(pool):
            pool.wait_ge(consts_landed, 32)
            for n in range(8):
                cols = slice((n % 2) * HALF, (n % 2 + 1) * HALF)
                pool.wait_ge(ctx_landed[n % 4], 16 * (n // 4 + 1))
                pool.tensor_tensor(ctxT[:, 0, n // 2, cols], ring[:, n % 4, :], zeros512, ALU.add).then_inc(ctx_high, 1)
                pool.wait_ge(ctx_high, n + 1)
                pool.tensor_tensor(ctxT[:, 1, n // 2, cols], ring[:, n % 4, :],
                                   ctxT[:, 0, n // 2, cols].bitcast(F32), ALU.subtract).then_inc(ctx_split, 1)

        def start_dve(dve):
            dve.wait_ge(consts_landed, 32)
            dve.tensor_tensor(kqn[:, :], vecs[:, V_QN:V_QN + 1], vecs[:, V_KN:V_KN + 1], ALU.mult).then_inc(kqn_made, 1)
            dve.wait_ge(x_landed, 32)
            dve_tail(dve, 0, None)
            dve.wait_ge(mask_landed, 16)
            dve.tensor_scalar(maskadd[:, :, :].rearrange("p b n -> p (b n)"), mask_bytes[:, :].bitcast(U8), -1.0, MASKED, ALU.add, ALU.mult).then_inc(mask_made, 1)
            dve.wait_ge(mask_made, 1)
            dve.tensor_reduce(live[:, :], maskadd[:, :, :], AX.X, ALU.max).then_inc(mask_made, 1)
            dve.wait_ge(mask_made, 2)
            dve.tensor_scalar(live[:, :], live[:, :], -1.0, None, ALU.is_gt).then_inc(mask_made, 1)
            dve.wait_ge(mask_made, 3)

        def finish_sp(sp):
            for b in range(B):
                F3.events.wait(sp, "added", B * (F3.chunks // 2 - 1) + b + 1)
                sp.dma_start(out[:, b, :], x[:, b, :]).then_inc(out_landed, 16)
            sp.wait_ge(out_landed, 16 * B)

        block = ctx.enter_context(nc.Block())

        @block.sync
        def _(sp):
            start_sp(sp)
            attention_sp(sp, LA[0])
            LA[0].events.wait(sp, "split", LA[0].tiles * NG)
            LA[0].events.wait(sp, "pv", 2 * NH)
            ffn_sp(sp, F0)
            l1_sp(sp)
            sp.wait_ge(L1["out_full"], B)
            sp.wait_ge(L1["out_biased"], B)
            ffn_sp(sp, F1)
            F1.events.wait(sp, "split", 2 * F1.chunks)
            sp.dma_start(maskadd[:, 0, :], ins["mask2"]).then_inc(mask_landed, 16)
            attention_sp(sp, LA[2])
            m2_sp(sp)
            row_sp(sp, 1, "L3_bo")
            sp.wait_ge(M2["w_split"], 2)
            sp.wait_ge(M2["outfull"], B)
            attention_sp(sp, LA[3])
            row_sp(sp, 2, "F3_bias")
            LA[3].events.wait(sp, "split", LA[3].tiles * NG)
            ffn_sp(sp, F3)
            finish_sp(sp)

        @block.gpsimd
        def _(pool):
            start_pool(pool)
            attention_pool(pool, LA[0])
            ffn_pool(pool, F0)
            l1_pool(pool)
            ffn_pool(pool, F1)
            attention_pool(pool, LA[2])
            m2_pool(pool)
            attention_pool(pool, LA[3])
            ffn_pool(pool, F3)

        @block.tensor
        def _(pe):
            pe.wait_ge(consts_landed, 32)
            pe_tail(pe, 0, None)
            pe.wait_ge(ctx_split, 8)
            attention_pe(pe, LA[0])
            ffn_pe(pe, F0)
            l1_pe(pe)
            ffn_pe(pe, F1)
            attention_pe(pe, LA[2])
            m2_pe(pe)
            attention_pe(pe, LA[3])
            ffn_pe(pe, F3)

        @block.scalar
        def _(act):
            act.wait_ge(consts_landed, 32)
            act_tail(act, 0)
            attention_act(act, LA[0])
            ffn_act(act, F0)
            l1_act(act)
            ffn_act(act, F1)
            attention_act(act, LA[2])
            m2_act(act)
            attention_act(act, LA[3])
            ffn_act(act, F3)

        @block.vector
        def _(dve):
            start_dve(dve)
            attention_dve(dve, LA[0])
            ffn_dve(dve, F0)
            l1_dve(dve)
            ffn_dve(dve, F1)
            dve.wait_ge(mask_landed, 32)
            attention_dve(dve, LA[2])
            m2_dve(dve)
            attention_dve(dve, LA[3])
            ffn_dve(dve, F3)


def constants():
    c = np.zeros((P, C_COUNT), np.float32)
    c[:, C_IDENT:C_IDENT + P] = np.eye(P)
    c[:, C_ONES:C_ONES + P] = 1
    for e in range(64):
        c[e, C_HEADS + e // 8] = 1
    c[64, C_HEADS:C_HEADS + 8] = 1
    c[:, C_MEAN] = 1 / P
    c[:, C_FIRST:C_FIRST + 32] = np.arange(32, 0, -1)
    c[:, C_LESS:C_LESS + 64] = np.tril(np.ones((8, 8)), -1).reshape(64)
    return c


def tiles(w):
    n = w.shape[0] // P
    return w.reshape(n, P, -1, P).transpose(0, 3, 2, 1).reshape(n, P, -1)


def pad_rows(w, rows):
    return np.concatenate([w, np.zeros((rows - w.shape[0], w.shape[1]), w.dtype)])


def layout(inputs):
    i = {k: np.asarray(a) for k, a in inputs.items()}
    a = {"consts": constants()}
    a["x"] = i["x"].transpose(1, 0, 2)
    a["ctxT"] = i["ctx_4096"].reshape(T, DC, P).transpose(2, 1, 0)
    a["mask0"] = i["mask_BxSxS2_bk0"].transpose(1, 0, 2).reshape(S, T).view(np.int32)
    a["position_bias"] = i["L0_xattn_position_bias"]
    vecs = np.zeros((P, V_COUNT), np.float32)
    vecs[:, V_LNW:V_LNW + 4] = i["L0_xattn_ln_weight"].reshape(DC, P).T
    vecs[:, V_BQ3:V_BQ3 + 32] = i["L3_xattn_bq"].reshape(NH, P).T
    vecs[:, V_BK3:V_BK3 + 16] = i["L3_xattn_bkv"].reshape(16, P).T
    vecs[:, V_QN] = i["L2_xattn_q_norm_w"]
    vecs[:, V_KN] = i["L2_xattn_k_norm_w"]
    vecs[:64, V_BQ1] = i["L1_xattn_bq"]
    vecs[:64, V_BK1] = i["L1_xattn_bk"]
    vecs[:, V_BO1] = i["L1_xattn_bo"]
    vecs[:, V_BI:V_BI + 16] = i["L3_ffn_inter_b"].reshape(16, P).T
    vecs[:, V_BI + 16:V_BI + 32] = vecs[:, V_BI:V_BI + 16]
    a["vecs"] = vecs
    a["L0_wq"], a["L0_wk"], a["L0_wv"] = (tiles(i[f"L0_xattn_w_{n}"]) for n in "qkv")
    a["L0_wo"] = i["L0_xattn_w_out"].T.reshape(NH, P, D)
    a["L2_wq"], a["L2_wk"], a["L2_wv"] = (tiles(i[f"L2_xattn_W{n}"]) for n in "qkv")
    a["L2_wo"] = i["L2_xattn_Wo"].T.reshape(NH, P, D)
    a["L3_wq"] = tiles(i["L3_xattn_Wq"].T)
    a["L3_wk"] = tiles(i["L3_xattn_Wkv"][:, :1024].T)
    a["L3_wv"] = tiles(i["L3_xattn_Wkv"][:, 1024:].T)
    a["L3_wo"] = i["L3_xattn_Wo"].reshape(NH, P, D)
    hid0 = 11 * P
    w1, w3, b1, b3 = (pad_rows(i[f"L0_ffn_{n}"], hid0) for n in ("w1", "w3", "lora_B1", "lora_B3"))
    a["F0_in"], a["F0_in2"] = tiles(w1), tiles(w3)
    a["F0_out"] = pad_rows(i["L0_ffn_w2"].T, hid0).reshape(11, P, D)
    pre = np.zeros((P, D), np.float32)
    pre[0:16], pre[32:48] = i["L0_ffn_lora_A1"], i["L0_ffn_lora_A3"]
    a["F0_pre"] = tiles(pre)[0]
    a["F0_b1"], a["F0_b3"], a["F0_b2"] = b1.T, b3.T, i["L0_ffn_lora_B2"].T
    a["F0_a2"] = pad_rows(i["L0_ffn_lora_A2"].T, hid0).reshape(11, P, 16).transpose(1, 0, 2).reshape(P, -1)
    a["L1_w"] = np.concatenate([i["L1_xattn_Wq"].T, i["L1_xattn_Wk"].T, i["L1_xattn_Wv"].T,
                                pad_rows(i["L1_xattn_Wo"].T, P)], axis=1)
    a["L1_bv"] = i["L1_xattn_bv"]
    a["ctx_tok"] = i["ctx_4096"]
    a["mask1"] = i["mask_Bx1x4096_ff1"].reshape(B, D)
    a["F1_pre"] = tiles(pad_rows(i["L1_ffn_c1_w"], P))[0]
    a["F1_c2"] = i["L1_ffn_c2_w"].T
    a["F1_in"] = tiles(i["L1_ffn_w1"])
    a["F1_out"] = i["L1_ffn_w2t"].reshape(14, P, D)
    a["mask2"] = i["mask_1x1xSxS2_ff0"].reshape(S, S)
    experts = np.concatenate([i["L2_ffn_A"].reshape(P, D), i["L2_ffn_W_router"]])
    a["M2_a"] = experts.T.reshape(DC, P, -1).transpose(1, 0, 2)
    a["M2_w"] = i["L2_ffn_W_base"].T.reshape(DC, P, D).transpose(1, 0, 2)
    a["M2_b"] = i["L2_ffn_B"].transpose(0, 2, 1).reshape(P, D)
    a["M2_bias"], a["L3_bo"], a["F3_bias"] = i["L2_ffn_b_base"], i["L3_xattn_bo"], i["L3_ffn_output_b"]
    a["F3_in"] = tiles(i["L3_ffn_inter_w"].T)
    a["F3_out"] = i["L3_ffn_output_w"].reshape(16, P, D)
    return {k: np.ascontiguousarray(n) for k, n in a.items()}


def kernel(**inputs):
    from concourse import bacc
    from concourse.bass_utils import run_bass_kernel_spmd

    arrays = layout(inputs)
    nc = bacc.Bacc("TRN2", target_bir_lowering=False, num_devices=1)
    ins = {k: nc.dram_tensor(f"in_{k}", a.shape, mybir.dt.from_np(a.dtype), kind="ExternalInput").ap()
           for k, a in arrays.items()}
    out = nc.dram_tensor("out", (P, B, D), F32, kind="ExternalOutput").ap()
    build(nc, ins, out)
    r = run_bass_kernel_spmd(nc, [{f"in_{k}": a for k, a in arrays.items()}], core_ids=[0])
    return np.ascontiguousarray(np.asarray(r.results[0]["out"]).transpose(1, 0, 2))
```

```python
from contextlib import ExitStack

import numpy as np

import concourse.bass as bass
from concourse import mybir

F32 = mybir.dt.float32
F32R = mybir.dt.float32r
I32 = mybir.dt.int32
U8 = mybir.dt.uint8
ALU = mybir.AluOpType
ACT = mybir.ActivationFunctionType
AX = mybir.AxisListType

P = 128
B = 8
S = 128
D = 512
DC = D // P
T = B * S
HALF = T // 2
BH = B // 2
NH = 32
GH = 4
NG = NH // GH
NPAIR = NH // 2
EPS = 1e-5
MASKED = 1e30
RSQRT_MAGIC = 0x5F3759DF
RSQRT_OPS = 11
PASSES = ((0, 0), (0, 1), (1, 0))

C_IDENT = 0
C_ONES = 128
C_HEADS = 256
C_ZERO = 264
C_FIRST = 266
C_LESS = 298
C_COUNT = 362

V_LNW, V_BQ3, V_BK3, V_BV3, V_QN, V_KN, V_BQ1, V_BK1, V_BO1, V_BI = 0, 4, 36, 44, 52, 53, 54, 55, 56, 57
V_COUNT = 89


def wait(engine, semaphore, value):
    if isinstance(value, int) and value <= 0:
        return
    engine.wait_ge(semaphore, value)


class Events:

    def __init__(self, semaphores, before, totals):
        self.semaphores = semaphores
        self.before = before
        self.after = dict(before)
        for name, n in totals.items():
            self.after[name] = before.get(name, 0) + n

    def __getitem__(self, name):
        return self.semaphores[name]

    def wait(self, engine, name, n):
        if isinstance(n, int) and n <= 0:
            return
        engine.wait_ge(self.semaphores[name], n + self.before.get(name, 0))


class Attention:

    def __init__(self, layer, stage, semaphores, before):
        self.layer = layer
        self.scale = float(P) ** -0.5
        self.stage = stage
        self.own_kv = layer == 0
        self.normed = layer == 2
        self.order = self.OWN_TILES if self.own_kv else self.SHARED_TILES
        kv = GH if self.own_kv else 1
        self.tiles = 2 * kv + 2 * GH
        self.ring = 4 if self.own_kv else 5
        self.projections = 2 * kv + GH
        self.turns = 16 if self.own_kv else 12 if self.normed else 10
        self.turns_first = 4 if self.normed else 2
        units, heads = 2 * NH, NH
        turns = self.turns_first + self.turns * NG - (4 if self.normed else 2)
        calls = heads + NG if self.normed else 0
        totals = dict(split=self.tiles * NG, high_w=self.tiles * NG, sfull=units, rowmax=units, negmax=units,
                      exps=units, rinv=units, pready=units, tfull=turns, tfree=turns, pv=units, high=units,
                      low=units, outfull=B * NPAIR, added=B * NPAIR, sfree=units if layer != 3 else 0,
                      masked=units if layer == 0 else 0, rlive=units if layer == 0 else 0,
                      squared=2 * calls, qturned=2 * calls, meaned=calls, shifted=2 * calls, newton=9 * calls,
                      diag=NG if self.normed else 0)
        for i in range(2):
            totals["pfull", i] = totals["pfree", i] = self.projections * NG
            totals["bias_landed", i] = 16 * NPAIR if layer == 0 else 0
        for i in range(self.ring):
            totals["landed", i] = 16 * self.tiles // self.ring * NG
        self.events = Events(semaphores, before, totals)

    NAMES = ("split high_w sfull sfree masked rowmax negmax exps rinv rlive pready tfull tfree pv high low "
             "outfull added squared qturned meaned shifted newton diag").split() + [
                 (n, i) for n in ("pfull", "pfree", "bias_landed") for i in range(2)] + [("landed", i) for i in range(5)]

    def new_kv(self, j):
        return self.own_kv or j == 0

    def tile(self, g, j, what):
        return self.tiles * g + self.order.index((what, j))

    OWN_TILES = [(what, j) for what, j in zip("kvqkvqokvqokvqoo", (0, 0, 0, 1, 1, 1, 0, 2, 2, 2, 1, 3, 3, 3, 2, 3))]
    SHARED_TILES = [("k", 0), ("v", 0), ("q", 0), ("q", 1), ("o", 0), ("q", 2), ("o", 1), ("q", 3), ("o", 2), ("o", 3)]

    def projection(self, g, j, what):
        if self.own_kv:
            return self.projections * g + 3 * j + "kvq".index(what)
        return self.projections * g + ("kv".index(what) if what in "kv" else 2 + j)

    def turn(self, g, j, what):
        if self.own_kv:
            order = ["T0", "T1", "V0", "V1"]
            at = 4 * j
        elif self.normed:
            order = ["T0", "T1"] if j < GH - 1 or isinstance(g, int) and g == NG - 1 else \
                    ["B0", "B1", "T0", "T1", "V0", "V1"]
            at = 2 * j
        else:
            order = ["T0", "T1", "V0", "V1"]
            at = 2 * j
        if isinstance(g, int) and g < 0:
            return [x for x in order if x[0] != "T"].index(what)
        return self.turns_first + self.turns * g + at + order.index(what)


class FeedForward:

    def __init__(self, name, stage, kind, chunks, semaphores, before, small=(), row=None):
        self.name, self.stage, self.kind, self.chunks, self.row = name, stage, kind, chunks, row
        self.low_rank = kind != "gelu"
        self.what = ["in", "in2", "out"] if kind == "silu" else ["in", "out"]
        self.ring = 2 * len(self.what)
        n, halves, pre = chunks, 2 * chunks, int(self.low_rank)
        nt = len(self.what) * chunks
        silu, pick = halves * (kind == "silu"), halves * (kind == "pick")
        outs = B * ((chunks + 1) // 2)
        totals = dict(split=nt, high_w=nt, pre_landed=16 * pre, pre_split=2 * pre, small_landed=16 * len(small),
                      sfull=silu + pick, tfull=pick, made=halves, high=halves, low=halves, outfull=outs, added=outs,
                      lowfull=silu, low2=2 * (kind == "silu"), bmax=pick, equal=pick, weighed=pick, fmax=pick,
                      picked=pick)
        for i in range(2):
            totals["pfull", i] = n + pre
            totals["pfree", i] = (n + pre) * (kind != "gelu")
        for i in range(self.ring):
            totals["landed", i] = 16 * len(range(i, nt, self.ring))
        self.small = small
        self.events = Events(semaphores, before, totals)

    NAMES = ("split high_w pre_landed pre_split small_landed sfull tfull made high low outfull added lowfull low2 "
             "bmax equal weighed fmax picked").split() + [
                 (n, i) for n in ("pfull", "pfree") for i in range(2)] + [("landed", i) for i in range(6)]

    def tile(self, g, j, k):
        return len(self.what) * (GH * g + j) + k

    def out_batches(self, g, j):
        if isinstance(g, int) and g == 0 and j < 2:
            return []
        if self.kind == "pick":
            return list(range(BH)) if j % 2 == 0 else list(range(BH, B))
        return list(range(B)) if j % 2 == 0 else []

    def out_tile(self, pair, slots):
        return len(self.what) * (2 * pair + len(slots))


def small_attention(sem):
    names = ("w_landed ones normed qk_full q_made k_biased k_made v_full v_made blocked sfull rowmax shifted exps "
             "tfull tfree av osums sturned osum onorm v_inv oturned gelu out_full out_biased added").split()
    found = {n: sem(f"L1_{n}") for n in names}
    for n in ("ctx_landed", "mask_landed"):
        for i in range(2):
            found[n, i] = sem(f"L1_{n}{i}")
    return found


def mixture(sem):
    names = ("a_landed w_landed b_landed a_split w_split a_high w_high full copied route routed expd weighted "
             "turned high outfull added").split()
    return {n: sem(f"M2_{n}") for n in names}


def build(nc, ins, out):
    with ExitStack() as ctx:
        def sb(name, shape, dt=F32):
            return ctx.enter_context(nc.sbuf_tensor(name, shape, dt))

        def bank(name):
            return ctx.enter_context(nc.psum_tensor(name, [P, 512], F32))

        def sem(name):
            return ctx.enter_context(nc.semaphore(name))

        x = sb("x", [P, B, D])
        ctxT = sb("ctxT", [P, 2, DC, T], F32R)
        xnT = sb("xnT", [P, 2, DC, T], F32R)
        acts = sb("acts", [P, 4, 2, T], F32R)
        w_in = sb("w_in", [P, 2, 2, D], F32R)
        w_kv = sb("w_kv", [P, 2, 2, D], F32R)
        w_out = sb("w_out", [P, 4, 2, D], F32R)
        sq = sb("sq", [P, T])
        ring = sb("ring", [P, 6, D])
        big = sb("big", [P, 4, T])
        qT, kT, vT, v = (big[:, i, :] for i in range(4))
        tbuf = sb("tbuf", [P, 2, 512])
        pbuf = sb("pbuf", [P, 2, 512])
        ptbuf = sb("ptbuf", [P, 2, 512])
        mask_bytes = sb("mask_bytes", [P, T // 4], I32)
        maskadd = sb("maskadd", [P, B, S])
        biasbuf = sb("biasbuf", [P, 2, S])
        brow = sb("brow", [P, D])
        consts = sb("consts", [P, C_COUNT])
        vecs = sb("vecs", [P, V_COUNT])
        kqn = sb("kqn", [P, 1])
        live = sb("live", [P, B])
        stats = sb("stats", [P, B, 6])
        moments = sb("moments", [P, B, 2])
        rstd = sb("rstd", [P, B])
        rrms = sb("rrms", [P, B])
        nw_v = sb("nw_v", [P, B])
        nw_t = sb("nw_t", [P, B])
        rq = sb("rq", [P, B])
        rk = sb("rk", [P, B])
        sumsq = sb("sumsq", [P, B])
        rowmax = sb("rowmax", [P, 2, 8])
        blockmax = sb("blockmax", [P, 2, 16])
        firstmax = sb("firstmax", [P, 2, 16])
        negmax = sb("negmax", [P, 2, 8])
        rowsum = sb("rowsum", [P, 2, 8])
        rinv = sb("rinv", [P, 2, 8])
        with nc.sbuf_tensor("w_kv2", [P, 2, 2, D], F32R) as w_kv2:
            pass
        spare = sb("spare", [P, 2 * T])
        kblock = spare[:, :].rearrange("p (a h n) -> p a h n", a=2, h=8)
        kraw, diagonals = spare[:, 0:T], spare[:, T:2 * T]
        ident = consts[:, C_IDENT:C_IDENT + P]
        ones = consts[:, C_ONES:C_ONES + P]
        zeros512 = consts[:, C_ZERO:C_ZERO + 1].broadcast_to([P, 512])

        proj = [bank(f"proj{i}") for i in range(2)]
        score = [bank(f"score{i}") for i in range(2)]
        turn = bank("turn")
        heado = bank("heado")
        outp = [bank(f"outp{i}") for i in range(2)]

        x_landed = [sem(f"x_landed{i}") for i in range(2)]
        consts_landed = sem("consts_landed")
        mask_landed = sem("mask_landed")
        ctx_landed = [sem(f"ctx_landed{i}") for i in range(4)]
        ctx_high = sem("ctx_high")
        ctx_split = sem("ctx_split")
        mask_made = sem("mask_made")
        kqn_made = sem("kqn_made")
        ln_stats, ln_moments, ln_shifted, ln_newton, ln_rstd, ln_normed, ln_full, ln_high, ln_low, ln_rms, ln_kept = (
            sem(f"ln_{n}") for n in "stats moments shifted newton rstd normed full high low rms kept".split())
        out_landed = sem("out_landed")
        row_landed = sem("row_landed")
        row_added = sem("row_added")
        flat = big[:, :, :].rearrange("p a n -> p (a n)")
        attention_sems = {n: sem("A_" + n if isinstance(n, str) else f"A_{n[0]}{n[1]}") for n in Attention.NAMES}
        ffn_sems = {n: sem("F_" + n if isinstance(n, str) else f"F_{n[0]}{n[1]}") for n in FeedForward.NAMES}
        LA = {0: Attention(0, 0, attention_sems, {})}
        LA[2] = Attention(2, 4, attention_sems, LA[0].events.after)
        LA[3] = Attention(3, 6, attention_sems, LA[2].events.after)
        a2 = flat[:, T + 11 * P + D:T + 11 * P + D + 11 * 16]
        b2 = flat[0:16, T + 11 * P:T + 11 * P + D]
        F0 = FeedForward("F0", 1, "silu", 11, ffn_sems, {}, small=[
            (flat[0:16, T:T + 11 * P], ins["F0_b1"]), (flat[32:48, T:T + 11 * P], ins["F0_b3"]),
            (b2, ins["F0_b2"]), (a2, ins["F0_a2"])])
        F1 = FeedForward("F1", 3, "pick", 14, ffn_sems, F0.events.after,
                         small=[(flat[0:16, T:T + 14 * P], ins["F1_c2"])])
        F3 = FeedForward("F3", 7, "gelu", 16, ffn_sems, F1.events.after, row=2)
        L1 = small_attention(sem)
        M2 = mixture(sem)
        def last_uses(A):
            n = A.chunks + A.low_rank if A in (F0, F1, F3) else A.projections * NG
            outs = B * ((A.chunks + 1) // 2 if A in (F0, F1, F3) else NPAIR)
            return [(A.events, ("pfull", 1), n), (A.events, "sfull", 2 * A.chunks if A is F0 else 0),
                    (A.events, "outfull", outs)]

        LA[0].before = LA[3].before = None
        F0.before, F1.before, LA[2].before, F3.before = (last_uses(A) for A in (LA[0], F0, F1, LA[3]))

        def wait_before(engine, A, out):
            for events, name, n in (A.before or [])[2:] if out else (A.before or [])[:2]:
                events.wait(engine, name, n)

        def pe_matmuls(pe, bank_ap, w_ap, rhs, chunks=DC, first=True, last=True):
            for c in range(chunks):
                for n, (a, b) in enumerate(PASSES):
                    mm = pe.matmul(bank_ap, w_ap(a, c), rhs(b, c), start=first and c == 0 and n == 0,
                                   stop=last and c == chunks - 1 and n == len(PASSES) - 1)
            return mm

        def pe_project(pe, w, slot, actT, half):
            return pe_matmuls(pe, proj[half][:, :], lambda a, c: w[:, slot, a, c * P:(c + 1) * P],
                              lambda b, c: actT[:, b, c, half * HALF:(half + 1) * HALF])

        def pe_out(pe, b, slots, last=True):
            for n, s in enumerate(slots):
                mm = pe_matmuls(pe, outp[b % 2][:, :], lambda a, c: acts[:, s, a, b * S:(b + 1) * S],
                                lambda a, c: w_out[:, s, a, :], chunks=1, first=n == 0,
                                last=last and n == len(slots) - 1)
            return mm

        def dve_rsqrt(dve, y, arg, tmp, shifted, newton, calls):
            base = calls * 9
            dve.tensor_scalar(tmp.bitcast(I32), arg.bitcast(I32), 1, None, ALU.logical_shift_right).then_inc(shifted, 1)
            dve.wait_ge(shifted, calls * 2 + 1)
            dve.tensor_scalar(y.bitcast(I32), tmp.bitcast(I32), -1.0, float(RSQRT_MAGIC), ALU.mult,
                              ALU.add).then_inc(shifted, 1)
            dve.wait_ge(shifted, calls * 2 + 2)
            for n in range(3):
                dve.scalar_tensor_tensor(tmp, y, -0.5, y, ALU.mult, ALU.mult).then_inc(newton, 1)
                dve.wait_ge(newton, base + (3 * n + 1))
                dve.tensor_tensor(tmp, tmp, arg, ALU.mult).then_inc(newton, 1)
                dve.wait_ge(newton, base + (3 * n + 2))
                dve.scalar_tensor_tensor(y, tmp, 1.5, y, ALU.add, ALU.mult).then_inc(newton, 1)
                dve.wait_ge(newton, base + (3 * n + 3))

        normed = [tbuf[:, 0, :], tbuf[:, 1, :], pbuf[:, 0, :], pbuf[:, 1, :]]
        ln_banks = [turn, heado] + score
        ln_calls = [0]
        LN_CALLS_AT_L1 = 4 + 2 + 2
        LN_STAGES = [0, 1, 3, 4, 5, 6, 7]

        def ln_no(n):
            return LN_STAGES.index(n)

        def dve_ln_stats(dve, n, b):
            if n == 0 and b % BH == 0:
                dve.wait_ge(x_landed[b // BH], 16)
            dve.bn_stats(stats[:, b, :], x[:, b, :]).then_inc(ln_stats, 1)
            dve.wait_ge(ln_stats, 8 * n + b + 1)
            dve.bn_aggr(moments[:, b, :], stats[:, b, :]).then_inc(ln_moments, 1)

        def dve_ln_rstd(dve, n, half):
            cols = slice(half * BH, half * BH + BH)
            dve.wait_ge(ln_moments, 8 * n + half * BH + BH)
            dve.tensor_scalar(nw_v[:, cols], moments[:, cols, 1], EPS, None, ALU.add).then_inc(ln_rstd, 1)
            dve.wait_ge(ln_rstd, 2 * n + half + 1)
            dve_rsqrt(dve, rstd[:, cols], nw_v[:, cols], nw_t[:, cols], ln_shifted, ln_newton, ln_calls[0])
            ln_calls[0] += 1
            if n == 0:
                dve.scalar_tensor_tensor(rrms[:, cols], rstd[:, cols], 1.0, rstd[:, cols], ALU.mult,
                                         ALU.mult).then_inc(ln_rms, 1)
                dve.wait_ge(ln_rms, 3 * half + 1)
                dve.tensor_tensor(rrms[:, cols], rrms[:, cols], moments[:, cols, 1], ALU.mult).then_inc(ln_rms, 1)
                dve.wait_ge(ln_rms, 3 * half + 2)
                dve.tensor_scalar(nw_v[:, cols], rrms[:, cols], EPS, None, ALU.add).then_inc(ln_rms, 1)
                dve.wait_ge(ln_rms, 3 * half + 3)
                dve_rsqrt(dve, rrms[:, cols], nw_v[:, cols], nw_t[:, cols], ln_shifted, ln_newton, ln_calls[0])
                ln_calls[0] += 1

        def dve_ln_norm(dve, n, b):
            m = ln_no(n)
            out_ap = normed[b % 4]
            if b >= 4:
                dve.wait_ge(ln_full, 8 * m + b - 3)
            norm = dve.tensor_scalar(out_ap, x[:, b, :], moments[:, b, 0:1], rstd[:, b:b + 1], ALU.subtract, ALU.mult)
            if n == 0:
                norm.then_inc(ln_kept, 1)
                dve.wait_ge(ln_kept, 2 * b + 1)
                dve.tensor_tensor(x[:, b, :], x[:, b, :], out_ap, ALU.add).then_inc(ln_kept, 1)
                dve.wait_ge(ln_kept, 2 * b + 2)
                dve.tensor_scalar(out_ap, out_ap, rrms[:, b:b + 1], None, ALU.mult).then_inc(ln_normed, 1)
            else:
                norm.then_inc(ln_normed, 1)

        def pe_ln_turn(pe, n, b):
            m = ln_no(n)
            pe.wait_ge(ln_normed, 8 * m + b + 1)
            if b >= 4:
                pe.wait_ge(ln_low, 8 * m + b - 3)
            for c in range(DC):
                mm = pe.transpose(ln_banks[b % 4][:, c * P:(c + 1) * P], normed[b % 4][:, c * P:(c + 1) * P], ident)
            mm.then_inc(ln_full, 1)

        def act_ln_high(act, n, b):
            m = ln_no(n)
            act.wait_ge(ln_full, 8 * m + b + 1)
            src = ln_banks[b % 4][:, :].rearrange("p (c t) -> p c t", c=DC)
            if n == 0:
                for c in range(DC):
                    a = act.activation(xnT[:, 0, c, b * S:(b + 1) * S], src[:, c, :], ACT.Copy,
                                       scale=vecs[:, V_LNW + c:V_LNW + c + 1])
            else:
                a = act.activation(xnT[:, 0, :, b * S:(b + 1) * S], src, ACT.Copy)
            a.then_inc(ln_high, 1)

        def dve_ln_low(dve, n, b):
            m = ln_no(n)
            dve.wait_ge(ln_high, 8 * m + b + 1)
            src = ln_banks[b % 4][:, :].rearrange("p (c t) -> p c t", c=DC)
            if n == 0:
                for c in range(DC):
                    a = dve.scalar_tensor_tensor(xnT[:, 1, c, b * S:(b + 1) * S], src[:, c, :],
                                                 vecs[:, V_LNW + c:V_LNW + c + 1],
                                                 xnT[:, 0, c, b * S:(b + 1) * S].bitcast(F32), ALU.mult, ALU.subtract)
            else:
                a = dve.tensor_tensor(xnT[:, 1, :, b * S:(b + 1) * S], src, xnT[:, 0, :, b * S:(b + 1) * S].bitcast(F32),
                                      ALU.subtract)
            a.then_inc(ln_low, 1)

        def low_rank_product(pe, A, half):
            if half == 0:
                A.events.wait(pe, "pre_split", 2)
            pe.wait_ge(ln_low, 8 * ln_no(A.stage) + BH * (half + 1))
            pe_project(pe, w_kv, 1, xnT, half).then_inc(A.events["pfull", half], 1)

        def take_low_rank(act, A, half):
            A.events.wait(act, ("pfull", half), 1)
            act.activation(big[0:48, 0, half * HALF:(half + 1) * HALF], proj[half][0:48, :], ACT.Copy,
                           scale=2.0 if A.kind == "silu" else 1.0).then_inc(A.events["pfree", half], 1)

        def pe_tail(pe, n, out_of):
            for b in range(B):
                if out_of:
                    out_of(b)
                if n in LN_STAGES and b >= B - 2:
                    for k in range(2):
                        pe_ln_turn(pe, n, 2 * (b - (B - 2)) + k)
            for F in (F0, F1):
                if F.stage == n:
                    low_rank_product(pe, F, 0)
            for A in LA.values():
                if A.stage == n:
                    if n == 0:
                        pe.wait_ge(ctx_split, 8)
                    for what in "kv":
                        project_head(pe, A, 0, 0, what)
            if n in LN_STAGES:
                for b in range(4, B):
                    pe_ln_turn(pe, n, b)

        def first_take(engine, on_act, n, what):
            for A in LA.values():
                if A.stage == n:
                    take_projection(engine, on_act, A, 0, 0, what)

        def act_tail(act, n):
            if n not in LN_STAGES:
                return
            for b in range(BH):
                act_ln_high(act, n, b)
            for what in "kv":
                first_take(act, True, n, what)
            for F in (F0, F1):
                if F.stage == n:
                    take_low_rank(act, F, 0)
            for b in range(BH, B):
                act_ln_high(act, n, b)

        def dve_tail(dve, n, add_of):
            turned = n in LN_STAGES
            early = BH if add_of else BH - 1
            for b in range(B):
                if add_of:
                    add_of(b)
                if n > 7:
                    continue
                dve_ln_stats(dve, n, b)
                if b == early:
                    dve_ln_rstd(dve, n, 0)
                    if turned:
                        dve_ln_norm(dve, n, 0)
                        dve_ln_norm(dve, n, 1)
                elif b == early + 1 and turned:
                    dve_ln_norm(dve, n, 2)
                    dve_ln_norm(dve, n, 3)
                elif b >= B - 2 and turned:
                    dve_ln_low(dve, n, b - (B - 2))
            if n > 7:
                return
            for b in range(2, BH if turned else 2):
                dve_ln_low(dve, n, b)
            dve_ln_rstd(dve, n, 1)
            if turned:
                for what, b in (("k", 4), ("v", 6)):
                    dve_ln_norm(dve, n, b)
                    dve_ln_norm(dve, n, b + 1)
                    first_take(dve, False, n, what)
                for b in range(4, B):
                    dve_ln_low(dve, n, b)

        def attention_sp(sp, A):
            m = A.events
            wk, wv, wq, wo = (ins[f"L{A.layer}_{k}"] for k in ("wk", "wv", "wq", "wo"))

            def load(g, j, what, source):
                n = A.tile(g, j, what)
                slot = A.tile(0, j, what) % A.ring
                m.wait(sp, "split", n - (A.ring - 1))
                sp.dma_start(ring[:, slot, :], source).then_inc(m["landed", slot], 16)

            def group(g):
                for what, j in A.order:
                    h = GH * g + j
                    n = g if what in "kv" and not A.own_kv else h
                    if A.layer == 0 and what == "k":
                        m.wait(sp, "masked", 2 * h - 2)
                        sp.dma_start(biasbuf[:, j % 2, :],
                                     ins["position_bias"][bass.ds(h, 1)].rearrange("a p n -> (a p) n"))\
                          .then_inc(m["bias_landed", j % 2], 16)
                    load(g, j, what, {"k": wk, "v": wv, "q": wq, "o": wo}[what][bass.ds(n, 1)].rearrange("a p n -> (a p) n"))

            group(0)
            with sp.Fori(1, NG) as g:
                group(g)

        def attention_pool(pool, A):
            m = A.events

            def split(g, j, what, dst, slot):
                n = A.tile(g, j, what)
                pos = A.tile(0, j, what)
                r = pos % A.ring
                m.wait(pool, ("landed", r), 16 * ((A.tiles // A.ring) * g + (pos // A.ring + 1)))
                pool.tensor_tensor(dst[:, slot, 0, :], ring[:, r, :], zeros512, ALU.add).then_inc(m["high_w"], 1)
                m.wait(pool, "high_w", n + 1)
                pool.tensor_tensor(dst[:, slot, 1, :], ring[:, r, :], dst[:, slot, 0, :].bitcast(F32),
                                   ALU.subtract).then_inc(m["split"], 1)

            def split_q(g, j):
                if A.layer == 3 and isinstance(g, int) and g == 0 and j == 0:
                    pool.wait_ge(M2["full"], B)
                if not (isinstance(g, int) and g == 0 and j < 2):
                    before = (g, j - 2) if j >= 2 else (g - 1, j + 2)
                    m.wait(pool, ("pfull", 1), A.projection(*before, "q") + 1)
                split(g, j, "q", w_in, j % 2)

            def split_o(g, j):
                if not (isinstance(g, int) and g == 0):
                    m.wait(pool, "outfull", B * (2 * g + (j // 2 - 1)))
                elif j == 0:
                    wait_before(pool, A, out=True)
                    if A.layer == 3:
                        LA[2].events.wait(pool, "outfull", B * NPAIR)
                split(g, j, "o", w_out, j)

            def split_kv(g, what):
                if not (isinstance(g, int) and g == 0):
                    m.wait(pool, ("pfull", 1), A.projection(g - 1, 0, what) + 1)
                split(g, 0, what, w_kv, "kv".index(what))

            def own_group(g):
                for what, j in A.order:
                    if what == "q":
                        split_q(g, j)
                    elif what == "o":
                        split_o(g, j)
                    else:
                        if not (isinstance(g, int) and g == 0 and j < 2):
                            before = (g, j - 2) if j >= 2 else (g - 1, j + 2)
                            m.wait(pool, ("pfull", 1), A.projection(*before, what) + 1)
                        split(g, j, what, (w_kv, w_kv2)[j % 2], "kv".index(what))

            def shared_group(g, last=False):
                split_o(g, 0)
                split_q(g, 2)
                split_o(g, 1)
                split_q(g, 3)
                split_o(g, 2)
                split_o(g, 3)
                if not last:
                    split_kv(g + 1, "k")
                    split_kv(g + 1, "v")
                    split_q(g + 1, 0)
                    split_q(g + 1, 1)

            wait_before(pool, A, out=False)
            if A.layer == 3:
                LA[2].events.wait(pool, ("pfull", 1), LA[2].projections * NG)
            if A.own_kv:
                own_group(0)
                with pool.Fori(1, NG) as g:
                    own_group(g)
                return
            split_kv(0, "k")
            split_kv(0, "v")
            split_q(0, 0)
            split_q(0, 1)
            shared_group(0)
            with pool.Fori(1, NG - 1) as g:
                shared_group(g)
            shared_group(NG - 1, last=True)

        def after(g, j):
            return (g, j + 1) if j < GH - 1 else (g + 1, 0)

        def needed_next(A, g, j):
            last = isinstance(g, int) and g == NG - 1
            if A.own_kv:
                return [] if last and j == GH - 1 else [(*after(g, j), what) for what in "kvq"]
            if A.normed and j == GH - 2:
                return [(g, j + 1, "q")] + ([] if last else [(g + 1, 0, "k")])
            if j < GH - 1:
                return [(g, j + 1, "q")]
            return [] if last else [(g + 1, 0, what) for what in ("vq" if A.normed else "kvq")]

        def new_values(A, g, j):
            return A.new_kv((j + 1) % GH) and not (isinstance(g, int) and g == NG - 1 and j == GH - 1)

        def pending(A, g, j):
            if isinstance(g, int) and g == 0 and j < 2:
                return g, 0, [[]] * 5
            at = (g, 0) if j >= 2 else (g - 1, 1)
            if j % 2 == 0:
                return (*at, [[0], [1], [2], [3], [4]] if A.own_kv else [[0, 1], [2], [3], [4], []])
            return (*at, [[], [5], [6], [7], []] if A.new_kv((j + 1) % GH) else [[5], [6], [7], [], []])

        def rms_call(g, j, what):
            return 5 * g + (0 if what == "k" else j + 1)

        def project_head(pe, A, g, j, what, squares=None):
            m = A.events
            n = A.projection(g, j, what)
            w, slot, act = {"k": (w_kv, 0, ctxT), "v": (w_kv, 1, ctxT), "q": (w_in, j % 2, xnT)}[what]
            if A.own_kv and what != "q" and j % 2:
                w = w_kv2
            m.wait(pe, "split", A.tile(g, j, what) + 1)
            for half in range(2):
                m.wait(pe, ("pfree", half), n)
                if A.normed and squares is not None:
                    m.wait(pe, "squared", 2 * squares + (half + 1))
                if what == "q" and isinstance(g, int) and g == 0 and j == 0:
                    pe.wait_ge(ln_low, 8 * ln_no(A.stage) + BH * (half + 1))
                pe_project(pe, w, slot, act, half).then_inc(m["pfull", half], 1)

        def attention_pe(pe, A):
            m = A.events
            unit = lambda g, j, half: 2 * (GH * g + j) + half
            project = lambda g, j, what, squares=None: project_head(pe, A, g, j, what, squares)

            def use_turn(n):
                m.wait(pe, "tfree", n)

            def turn_values(g, j, half):
                use_turn(A.turn(g, j, f"V{half}"))
                if half == 0:
                    k = A.projection(*after(g, j), "v") if not (isinstance(g, int) and g < 0) else 1
                    for i in range(2):
                        m.wait(pe, ("pfree", i), k + 1)
                for b in range(BH):
                    mm = pe.transpose(turn[:, b * P:(b + 1) * P], vT[:, (half * BH + b) * S:(half * BH + b + 1) * S], ident)
                mm.then_inc(m["tfull"], 1)

            def turn_for_sums(g, j, what):
                c = rms_call(g, j, what)
                src = kraw if what == "k" else qT
                for half in range(2):
                    if half == 0:
                        n = A.projection(g, j, what)
                        if what == "q" and j == GH - 1 and not (isinstance(g, int) and g == NG - 1):
                            n = n + 1
                        if what == "k" and isinstance(g, int) and g == 0:
                            n = n + 1
                        for i in range(2):
                            m.wait(pe, ("pfree", i), n + 1)
                    m.wait(pe, "squared", 2 * c + (half - 1))
                    for b in range(BH):
                        t = slice((half * BH + b) * S, (half * BH + b + 1) * S)
                        mm = pe.transpose(proj[half][:, b * P:(b + 1) * P], src[:, t], ident)
                    mm.then_inc(m["qturned"], 1)

            def spread(g, j, g2, half):
                use_turn(A.turn(g, j, f"B{half}"))
                if half == 0:
                    m.wait(pe, "diag", g2 + 1)
                for b in range(half * BH, (half + 1) * BH):
                    mm = pe.matmul(turn[:, (b % BH) * P:(b % BH + 1) * P], ones, diagonals[:, b * P:(b + 1) * P],
                                   start=True, stop=True)
                mm.then_inc(m["tfull"], 1)

            def out_product(g, pair, bs):
                p = 2 * g + pair
                if bs[0] == 0:
                    m.wait(pe, "low", 4 * (p + 1))
                    m.wait(pe, "split", A.tile(g, 2 * pair + 1, "o") + 1)
                for b in bs:
                    m.wait(pe, "added", B * p + (b - 1))
                    pe_out(pe, b, (2 * pair, 2 * pair + 1)).then_inc(m["outfull"], 1)

            def step(g, j):
                out_g, pair, at_place = pending(A, g, j)

                def out_at(place):
                    if at_place[place]:
                        out_product(out_g, pair, at_place[place])

                for half in range(2):
                    u = unit(g, j, half)
                    if half == 0:
                        for i in range(2):
                            m.wait(pe, ("pfree", i), A.projection(g, j, "q") + 1)
                        if A.normed and j == 0:
                            m.wait(pe, "tfree", A.turn(g - 1, 3, "B1") + 1)
                    m.wait(pe, "exps" if A.layer == 3 else "sfree", u - 1)
                    for b in range(BH):
                        t = slice((half * BH + b) * S, (half * BH + b + 1) * S)
                        mm = pe.matmul(score[half][:, b * P:(b + 1) * P], qT[:, t], kT[:, t], start=True, stop=True)
                    mm.then_inc(m["sfull"], 1)
                for n, new in enumerate(needed_next(A, g, j)):
                    project(*new, squares=(5 * g + (5 if j == GH - 1 else j + 1)) if n == 0 else None)
                    if A.normed and j == GH - 1:
                        spread(g, j, g + 1, n)
                out_at(0)
                for half in range(2):
                    n = A.turn(g, j, f"T{half}")
                    use_turn(n)
                    m.wait(pe, "pready", unit(g, j, half) + 1)
                    for b in range(BH):
                        mm = pe.transpose(turn[:, b * P:(b + 1) * P], pbuf[:, half, b * P:(b + 1) * P], ident)
                    mm.then_inc(m["tfull"], 1)
                    out_at(1 + half)
                    m.wait(pe, "tfree", n + 1)
                    m.wait(pe, "low", unit(g, j, half))
                    for b in range(BH):
                        mm = pe.matmul(heado[:, b * P:(b + 1) * P], v[:, (half * BH + b) * S:(half * BH + b + 1) * S],
                                       ptbuf[:, half, b * P:(b + 1) * P], start=True, stop=True)
                    mm.then_inc(m["pv"], 1)
                if new_values(A, g, j):
                    turn_values(g, j, 0)
                for new in needed_next(A, g, j) if A.normed else []:
                    if new[2] != "v":
                        turn_for_sums(*new)
                out_at(3)
                if new_values(A, g, j):
                    turn_values(g, j, 1)
                out_at(4)

            def group(g):
                for j in range(GH):
                    step(g, j)

            if A.normed:
                turn_for_sums(0, 0, "k")
            project(0, 0, "q", squares=0)
            for half in range(2):
                if A.normed:
                    spread(-1, 3, 0, half)
            if A.normed:
                turn_for_sums(0, 0, "q")
            for half in range(2):
                turn_values(-1, 3, half)
            group(0)
            with pe.Fori(1, NG - 1) as g:
                group(g)
            group(NG - 1)
            pe_tail(pe, A.stage + 1, lambda b: out_product(NG - 1, 1, [b]))

        def copy_projection(engine, on_act, dst, src, bias):
            if on_act:
                if bias is None:
                    return engine.activation(dst, src, ACT.Copy)
                return engine.activation(dst, src, ACT.Identity, bias=bias)
            if bias is None:
                return engine.tensor_copy(dst, src)
            return engine.tensor_scalar(dst, src, bias, None, ALU.add)

        def take_projection(engine, on_act, A, g, j, what):
            m = A.events
            half = 0 if on_act else 1
            m.wait(engine, ("pfull", half), A.projection(g, j, what) + 1)
            dst = {"k": kraw if A.normed else kT, "v": vT, "q": qT}[what][:, half * HALF:(half + 1) * HALF]
            bias = None
            if A.layer == 3:
                base, n = {"k": (V_BK3, g), "v": (V_BV3, g), "q": (V_BQ3, GH * g + j)}[what]
                bias = vecs[:, bass.ds(base + n, 1)]
            copy_projection(engine, on_act, dst, proj[half][:, :], bias).then_inc(m["pfree", half], 1)

        def take_values(engine, on_act, A, g, j):
            m = A.events
            half = 0 if on_act else 1
            m.wait(engine, "tfull", A.turn(g, j, f"V{half}") + 1)
            dst = v[:, half * HALF:(half + 1) * HALF]
            copy_projection(engine, on_act, dst, turn[:, :], None).then_inc(m["tfree"], 1)

        def attention_act(act, A):
            m = A.events

            def sum_squares(g, j, what):
                c = rms_call(g, j, what)
                m.wait(act, "meaned", c)
                for half in range(2):
                    m.wait(act, "qturned", 2 * c + (half + 1))
                    for b in range(BH):
                        n = half * BH + b
                        a = act.activation(sq[:, n * P:(n + 1) * P], proj[half][:, b * P:(b + 1) * P], ACT.Square,
                                           accum_out=sumsq[:, n:n + 1])
                    a.then_inc(m["squared"], 1)

            def step(g, j):
                needed = needed_next(A, g, j)
                takes = [needed[:1], [], needed[1:]] if A.normed and len(needed) > 1 else [[], needed[:1], needed[1:]]
                for new in takes[0]:
                    take_projection(act, True, A, *new)
                for half in range(2):
                    u = 2 * (GH * g + j) + half
                    src = score[half] if A.layer == 3 else tbuf[:, half, :]
                    scale = A.scale if A.layer == 3 else 1.0
                    m.wait(act, "negmax", u + 1)
                    for b in range(BH):
                        a = act.activation(pbuf[:, half, b * P:(b + 1) * P], src[:, b * P:(b + 1) * P], ACT.Exp,
                                           bias=negmax[:, half, b:b + 1], scale=scale,
                                           accum_out=rowsum[:, half, b:b + 1])
                    a.then_inc(m["exps"], 1)
                    for new in takes[1 + half]:
                        take_projection(act, True, A, *new)
                for half in range(2):
                    u = 2 * (GH * g + j) + half
                    m.wait(act, "tfull", A.turn(g, j, f"T{half}") + 1)
                    act.activation(ptbuf[:, half, :], turn[:, :], ACT.Copy).then_inc(m["tfree"], 1)
                    m.wait(act, "pv", u + 1)
                    act.activation(acts[:, j, 0, half * HALF:(half + 1) * HALF], heado[:, :], ACT.Copy)\
                       .then_inc(m["high"], 1)
                if new_values(A, g, j):
                    take_values(act, True, A, g, j)
                for new in needed_next(A, g, j) if A.normed else []:
                    if new[2] != "v":
                        sum_squares(*new)

            def group(g):
                for j in range(GH):
                    step(g, j)

            if A.normed:
                sum_squares(0, 0, "k")
            take_projection(act, True, A, 0, 0, "q")
            if A.normed:
                sum_squares(0, 0, "q")
            take_values(act, True, A, -1, 3)
            group(0)
            with act.Fori(1, NG - 1) as g:
                group(g)
            group(NG - 1)
            act_tail(act, A.stage + 1)

        def attention_dve(dve, A):
            m = A.events

            def scores(g, j, half):
                h = GH * g + j
                u = 2 * h + half
                blocks = lambda ap: ap.rearrange("p (b k) -> p b k", b=BH)
                m.wait(dve, "sfull", u + 1)
                src = blocks(score[half][:, :])
                if A.layer == 0:
                    if half == 0:
                        m.wait(dve, ("bias_landed", j % 2), 16 * (2 * g + (j // 2 + 1)))
                    t = blocks(tbuf[:, half, :])
                    dve.tensor_tensor(t, src, biasbuf[:, j % 2:j % 2 + 1, :].broadcast_to([P, BH, S]), ALU.add)\
                       .then_inc(m["sfree"], 1)
                    m.wait(dve, "sfree", u + 1)
                    dve.tensor_tensor(t, t, maskadd[:, half * BH:(half + 1) * BH, :], ALU.add).then_inc(m["masked"], 1)
                    m.wait(dve, "masked", u + 1)
                    src = t
                elif A.layer == 2:
                    for b in range(BH):
                        n = half * BH + b
                        a = dve.scalar_tensor_tensor(tbuf[:, half, b * P:(b + 1) * P], score[half][:, b * P:(b + 1) * P],
                                                     rq[:, n:n + 1], maskadd[:, 0, :], ALU.mult, ALU.add)
                    a.then_inc(m["sfree"], 1)
                    m.wait(dve, "sfree", u + 1)
                    src = blocks(tbuf[:, half, :])
                dve.tensor_reduce(rowmax[:, half, 0:BH], src, AX.X, ALU.max).then_inc(m["rowmax"], 1)
                m.wait(dve, "rowmax", u + 1)
                dve.tensor_scalar(negmax[:, half, 0:BH], rowmax[:, half, 0:BH], -A.scale if A.layer == 3 else -1.0,
                                  None, ALU.mult).then_inc(m["negmax"], 1)

            def normalise(g, j, half):
                u = 2 * (GH * g + j) + half
                m.wait(dve, "exps", u + 1)
                dve.reciprocal(rinv[:, half, 0:BH], rowsum[:, half, 0:BH]).then_inc(m["rinv"], 1)
                m.wait(dve, "rinv", u + 1)
                if A.layer == 0:
                    dve.tensor_tensor(rinv[:, half, 0:BH], rinv[:, half, 0:BH], live[:, half * BH:(half + 1) * BH],
                                      ALU.mult).then_inc(m["rlive"], 1)
                    m.wait(dve, "rlive", u + 1)
                pb = pbuf[:, half, :].rearrange("p (b k) -> p b k", b=BH)
                dve.tensor_tensor(pb, pb, rinv[:, half, 0:BH].unsqueeze(2).broadcast_to([P, BH, S]), ALU.mult)\
                   .then_inc(m["pready"], 1)

            def rms(g, j, what):
                c = rms_call(g, j, what)
                dst = rk if what == "k" else rq
                m.wait(dve, "squared", 2 * c + 2)
                dve.tensor_scalar(nw_v[:, :], sumsq[:, :], 1.0 / P, EPS, ALU.mult, ALU.add).then_inc(m["meaned"], 1)
                m.wait(dve, "meaned", c + 1)
                dve_rsqrt(dve, dst[:, :], nw_v[:, :], nw_t[:, :], m["shifted"], m["newton"], c)

            def make_diagonals():
                for b in range(B):
                    a = dve.tensor_scalar(diagonals[:, b * P:(b + 1) * P], ident, rk[:, b:b + 1], None, ALU.mult)
                a.then_inc(m["diag"], 1)

            def norm_keys(g, j, g2, half):
                cols = slice(half * HALF, (half + 1) * HALF)
                m.wait(dve, "tfull", A.turn(g, j, f"B{half}") + 1)
                m.wait(dve, ("pfree", half), A.projection(g2, 0, "k") + 1)
                dve.scalar_tensor_tensor(kT[:, cols], kraw[:, cols], kqn[:, 0:1], turn[:, :], ALU.mult, ALU.mult)\
                   .then_inc(m["tfree"], 1)

            def add(p, b):
                m.wait(dve, "added", B * p + (b - B + 1))
                m.wait(dve, "outfull", B * p + (b + 1))
                dve.tensor_tensor(x[:, b, :], x[:, b, :], outp[b % 2][:, :], ALU.add).then_inc(m["added"], 1)

            def step(g, j):
                out_g, pair, at_place = pending(A, g, j)

                def add_at(place):
                    for b in at_place[place]:
                        add(2 * out_g + pair, b)

                new = needed_next(A, g, j)
                spreads = A.normed and j == GH - 1 and new
                for half in range(2):
                    scores(g, j, half)
                for n in new[:1]:
                    take_projection(dve, False, A, *n)
                normalise(g, j, 0)
                if spreads:
                    norm_keys(g, j, g + 1, 0)
                normalise(g, j, 1)
                for n in new[1:]:
                    take_projection(dve, False, A, *n)
                if spreads:
                    norm_keys(g, j, g + 1, 1)
                add_at(0)
                for half in range(2):
                    add_at(1 + half)
                    u = 2 * (GH * g + j) + half
                    m.wait(dve, "high", u + 1)
                    cols = slice(half * HALF, (half + 1) * HALF)
                    dve.tensor_tensor(acts[:, j, 1, cols], heado[:, :], acts[:, j, 0, cols].bitcast(F32), ALU.subtract)\
                       .then_inc(m["low"], 1)
                add_at(3)
                if new_values(A, g, j):
                    take_values(dve, False, A, g, j)
                for n in new if A.normed else []:
                    if n[2] == "q":
                        rms(*n)
                add_at(4)
                if A.normed and any(what == "k" for _, _, what in new):
                    rms(g + 1, 0, "k")
                    make_diagonals()

            def group(g):
                for j in range(GH):
                    step(g, j)

            if A.layer == 3:
                add_row(dve, 1)
            if A.normed:
                rms(0, 0, "k")
                make_diagonals()
            take_projection(dve, False, A, 0, 0, "q")
            for half in range(2):
                if A.normed:
                    norm_keys(-1, 3, 0, half)
            if A.normed:
                rms(0, 0, "q")
            take_values(dve, False, A, -1, 3)
            group(0)
            with dve.Fori(1, NG - 1) as g:
                group(g)
            group(NG - 1)

            def last_add(b):
                add(NPAIR - 1, b)
                m.wait(dve, "added", B * (NPAIR - 1) + b + 1)

            dve_tail(dve, A.stage + 1, last_add)

        def ffn_run(engine, A, emit):
            last = (A.chunks - 1) // GH
            emit(0, range(GH))
            if last > 2:
                with engine.Fori(1, last) as g:
                    emit(g, range(GH))
            else:
                emit(1, range(GH))
            emit(last, range(A.chunks - GH * last))

        def ffn_sp(sp, A):
            m = A.events
            if A.low_rank:
                sp.dma_start(brow[:, :], ins[f"{A.name}_pre"]).then_inc(m["pre_landed"], 16)
                for dst, src in A.small:
                    sp.dma_start(dst, src).then_inc(m["small_landed"], 16)

            def chunks(g, js):
                for j in js:
                    c = GH * g + j
                    for k, what in enumerate(A.what):
                        n = A.tile(g, j, k)
                        slot = (len(A.what) * j + k) % A.ring
                        m.wait(sp, "split", n - (A.ring - 1))
                        sp.dma_start(ring[:, slot, :], ins[f"{A.name}_{what}"][bass.ds(c, 1)].rearrange("a p n -> (a p) n"))\
                          .then_inc(m["landed", slot], 16)

            ffn_run(sp, A, chunks)

        def ffn_pool(pool, A):
            m = A.events

            def tiles_of(g, j):
                for k, what in enumerate(A.what):
                    r = (len(A.what) * j + k) % A.ring
                    n = A.tile(g, j, k)
                    early = isinstance(g, int) and g == 0
                    if what == "in":
                        dst = w_in[:, j % 2]
                        if not (early and j < 2):
                            m.wait(pool, ("pfull", 1), GH * g + (j - 2 + A.low_rank + 1))
                    elif what == "in2":
                        dst = w_kv[:, j % 2]
                        if not (early and j < 2):
                            m.wait(pool, "sfull", 2 * (GH * g + (j - 2)) + 2)
                        elif j == 1 and A.low_rank:
                            m.wait(pool, ("pfull", 1), 1)
                    else:
                        dst = w_out[:, j]
                        if early and j == 0:
                            wait_before(pool, A, out=True)
                        if not early:
                            m.wait(pool, "outfull", B * (2 * g + (j // 2 - 1)))
                    m.wait(pool, ("landed", r), 16 * ((GH * len(A.what) // A.ring) * g + ((len(A.what) * j + k) // A.ring + 1)))
                    pool.tensor_tensor(dst[:, 0, :], ring[:, r, :], zeros512, ALU.add).then_inc(m["high_w"], 1)
                    m.wait(pool, "high_w", n + 1)
                    pool.tensor_tensor(dst[:, 1, :], ring[:, r, :], dst[:, 0, :].bitcast(F32), ALU.subtract)\
                        .then_inc(m["split"], 1)

            def chunks(g, js):
                for j in js:
                    c = GH * g + j
                    for half in range(2 if A.kind == "pick" else 0):
                        u = 2 * c + half
                        m.wait(pool, "equal", u + 1)
                        e = ptbuf[:, half, :].rearrange("p (k i) -> p k i", i=32)
                        pool.tensor_tensor(e, e, consts[:, C_FIRST:C_FIRST + 32].unsqueeze(1).broadcast_to([P, 16, 32]),
                                           ALU.mult).then_inc(m["weighed"], 1)
                    if not (isinstance(c, int) and c == A.chunks - 1):
                        tiles_of(*after(g, j))
                    for half in range(2):
                        u = 2 * c + half
                        m.wait(pool, "made", u + 1)
                        if not (isinstance(g, int) and g == 0):
                            m.wait(pool, "outfull", B * (2 * g + (j // 2 - 1)))
                        pool.tensor_tensor(acts[:, j, 0, half * HALF:(half + 1) * HALF], pbuf[:, half, :], zeros512,
                                           ALU.add).then_inc(m["high"], 1)

            wait_before(pool, A, out=False)
            if A.low_rank:
                m.wait(pool, "pre_landed", 16)
                pool.tensor_tensor(w_kv[:, 1, 0, :], brow[:, :], zeros512, ALU.add).then_inc(m["pre_split"], 1)
                m.wait(pool, "pre_split", 1)
                pool.tensor_tensor(w_kv[:, 1, 1, :], brow[:, :], w_kv[:, 1, 0, :].bitcast(F32), ALU.subtract)\
                    .then_inc(m["pre_split"], 1)
            tiles_of(0, 0)
            ffn_run(pool, A, chunks)

        def ffn_pe(pe, A):
            m = A.events
            pre = int(A.low_rank)
            low = big[0:48, 0, :]

            def second_low(g, j):
                c = GH * g + j
                for half in range(2):
                    m.wait(pe, "made", 2 * c + half + 1)
                    mm = pe.matmul(ln_banks[half][0:16, :], a2[:, c * 16:(c + 1) * 16], pbuf[:, half, :], start=isinstance(c, int) and c == 0,
                                   stop=isinstance(c, int) and c == A.chunks - 1)
                    mm.then_inc(m["lowfull"], 1)

            def out_product(p, slots, bs, last):
                if bs[0] == 0:
                    m.wait(pe, "low", 4 * p + 2 * len(slots))
                    m.wait(pe, "split", A.out_tile(p, slots))
                for b in bs:
                    m.wait(pe, "added", B * p + (b - 1))
                    more = last and A.kind == "silu"
                    mm = pe_out(pe, b, slots, last=not more)
                    if more:
                        if b == 0:
                            m.wait(pe, "low2", 2)
                        mm = pe.matmul(outp[b % 2][:, :], sq[0:16, b * S:(b + 1) * S], b2, start=False, stop=True)
                    mm.then_inc(m["outfull"], 1)

            def chunks(g, js):
                for j in js:
                    c = GH * g + j
                    first = isinstance(c, int) and c == 0
                    if A.kind == "pick":
                        for half in range(2):
                            if half == 0:
                                m.wait(pe, "equal", 2 * c)
                            for b in range(BH):
                                t = half * BH + b
                                mm = pe.matmul(score[half][:, b * P:(b + 1) * P], low[0:16, t * S:(t + 1) * S],
                                               flat[0:16, bass.ds(T + P * c, P)], start=True, stop=True)
                            mm.then_inc(m["sfull"], 1)
                    m.wait(pe, "split", A.tile(g, j, 0) + 1)
                    for half in range(2):
                        if A.kind == "gelu":
                            m.wait(pe, "made", 2 * c + half - 1)
                        else:
                            m.wait(pe, ("pfree", half), c + pre)
                        mm = pe_matmuls(pe, proj[half][:, :], lambda a, k: w_in[:, j % 2, a, k * P:(k + 1) * P],
                                        lambda b, k: xnT[:, b, k, half * HALF:(half + 1) * HALF], last=A.kind != "silu")
                        if A.kind == "silu":
                            mm = pe.matmul(proj[half][:, :], flat[0:16, T + c * P:T + (c + 1) * P], big[0:16, 0, half * HALF:(half + 1) * HALF],
                                           start=False, stop=True)
                        mm.then_inc(m["pfull", half], 1)
                    if A.kind == "silu":
                        if not first:
                            second_low(*((g, j - 1) if j else (g - 1, GH - 1)))
                        m.wait(pe, "split", A.tile(g, j, 1) + 1)
                        for half in range(2):
                            m.wait(pe, "made", 2 * c + half - 1)
                            pe_matmuls(pe, score[half][:, :], lambda a, k: w_kv[:, j % 2, a, k * P:(k + 1) * P],
                                       lambda b, k: xnT[:, b, k, half * HALF:(half + 1) * HALF], last=False)
                            pe.matmul(score[half][:, :], flat[32:48, T + c * P:T + (c + 1) * P], big[32:48, 0, half * HALF:(half + 1) * HALF],
                                      start=False, stop=True).then_inc(m["sfull"], 1)
                    bs = A.out_batches(g, j)
                    if bs:
                        out_product(2 * g + (0 if j >= 2 else -1), (0, 1) if j >= 2 else (2, 3), bs, False)
                    if A.kind == "pick":
                        for half in range(2):
                            m.wait(pe, "made", 2 * c + half - 1)
                            m.wait(pe, "picked", 2 * c + half + 1)
                            for b in range(BH):
                                mm = pe.transpose(ln_banks[half][:, b * P:(b + 1) * P], ptbuf[:, half, b * P:(b + 1) * P],
                                                  ident)
                            mm.then_inc(m["tfull"], 1)

            if A.low_rank:
                m.wait(pe, "small_landed", 16 * len(A.small))
                low_rank_product(pe, A, 1)
                for half in range(2):
                    m.wait(pe, ("pfree", half), 1)
            else:
                pe.wait_ge(ln_low, 8 * ln_no(A.stage) + B)
            ffn_run(pe, A, chunks)
            if A.kind == "silu":
                second_low(*divmod(A.chunks - 1, GH))
            p = (A.chunks - 1) // 2
            s = 2 * (p % 2)
            slots = (s, s + 1) if A.chunks % 2 == 0 else (s,)
            pe_tail(pe, A.stage + 1, lambda b: out_product(p, slots, [b], True))

        def ffn_act(act, A):
            m = A.events
            pre = int(A.low_rank)

            def chunks(g, js):
                for j in js:
                    c = GH * g + j
                    for half in range(2):
                        m.wait(act, ("pfull", half), c + pre + 1)
                        if A.kind == "gelu":
                            m.wait(act, "low", 2 * c + half - 1)
                            a = act.activation(pbuf[:, half, :], proj[half][:, :], ACT.Gelu_apprx_tanh,
                                               bias=vecs[:, bass.ds(V_BI + 16 * half + c, 1)])
                            a.then_inc(m["made"], 1)
                            continue
                        m.wait(act, "made", 2 * c + half - 1)
                        act.activation(tbuf[:, half, :], proj[half][:, :], ACT.Silu if A.kind == "silu" else ACT.Relu)\
                           .then_inc(m["pfree", half], 1)

            if A.low_rank:
                take_low_rank(act, A, 1)
            ffn_run(act, A, chunks)
            if A.kind == "silu":
                m.wait(act, "lowfull", 2 * A.chunks)
                for half in range(2):
                    act.activation(sq[0:16, half * HALF:(half + 1) * HALF], ln_banks[half][0:16, :], ACT.Copy, scale=2.0)\
                       .then_inc(m["low2"], 1)
            act_tail(act, A.stage + 1)

        def ffn_dve(dve, A):
            m = A.events

            def add(p, b):
                m.wait(dve, "added", B * p + (b - B + 1))
                m.wait(dve, "outfull", B * p + (b + 1))
                dve.tensor_tensor(x[:, b, :], x[:, b, :], outp[b % 2][:, :], ALU.add).then_inc(m["added"], 1)

            def low_part(c, j, half):
                m.wait(dve, "high", 2 * c + half + 1)
                cols = slice(half * HALF, (half + 1) * HALF)
                dve.tensor_tensor(acts[:, j, 1, cols], pbuf[:, half, :], acts[:, j, 0, cols].bitcast(F32), ALU.subtract)\
                   .then_inc(m["low"], 1)

            def pick(c):
                blocks = lambda ap: ap.rearrange("p (k i) -> p k i", i=32)
                spread = lambda ap: ap.unsqueeze(2).broadcast_to([P, 16, 32])
                for half in range(2):
                    u = 2 * c + half
                    m.wait(dve, "sfull", u + 1)
                    dve.tensor_reduce(blockmax[:, half, :], blocks(score[half][:, :]), AX.X, ALU.max).then_inc(m["bmax"], 1)
                    m.wait(dve, "bmax", u + 1)
                    m.wait(dve, "tfull", u - 1)
                    dve.tensor_tensor(blocks(ptbuf[:, half, :]), blocks(score[half][:, :]), spread(blockmax[:, half, :]),
                                      ALU.is_equal).then_inc(m["equal"], 1)
                for half in range(2):
                    u = 2 * c + half
                    m.wait(dve, "weighed", u + 1)
                    dve.tensor_reduce(firstmax[:, half, :], blocks(ptbuf[:, half, :]), AX.X, ALU.max).then_inc(m["fmax"], 1)
                    m.wait(dve, "fmax", u + 1)
                    dve.tensor_tensor(blocks(ptbuf[:, half, :]), blocks(ptbuf[:, half, :]), spread(firstmax[:, half, :]),
                                      ALU.is_equal).then_inc(m["picked"], 1)

            def chunks(g, js):
                for j in js:
                    c = GH * g + j
                    first = isinstance(c, int) and c == 0
                    adds = A.out_batches(g, j)
                    p = 2 * g + (0 if j >= 2 else -1)
                    if A.kind == "silu":
                        for half in range(2):
                            u = 2 * c + half
                            m.wait(dve, "sfull", u + 1)
                            m.wait(dve, ("pfree", half), c + 2)
                            m.wait(dve, "lowfull", u - 1)
                            m.wait(dve, "low", u - 1)
                            dve.tensor_tensor(pbuf[:, half, :], score[half][:, :], tbuf[:, half, :], ALU.mult)\
                               .then_inc(m["made"], 1)
                    if A.kind == "pick":
                        pick(c)
                        for b in adds:
                            add(p, b)
                        for half in range(2):
                            u = 2 * c + half
                            m.wait(dve, "tfull", u + 1)
                            m.wait(dve, ("pfree", half), c + 2)
                            m.wait(dve, "low", u - 1)
                            dve.tensor_tensor(pbuf[:, half, :], ln_banks[half][:, :], tbuf[:, half, :], ALU.mult)\
                               .then_inc(m["made"], 1)
                        adds = []
                    for b in adds[:BH]:
                        add(p, b)
                    for half in range(2):
                        low_part(c, j, half)
                    for b in adds[BH:]:
                        add(p, b)

            if A.row is not None:
                add_row(dve, A.row)
            ffn_run(dve, A, chunks)
            p = (A.chunks - 1) // 2

            def last_add(b):
                add(p, b)
                m.wait(dve, "added", B * p + b + 1)

            dve_tail(dve, A.stage + 1, last_add)

        def row_sp(sp, n, name):
            wait(sp, row_added, B * n)
            if n == 0:
                sp.wait_ge(L1["v_made"], B)
                sp.wait_ge(L1["out_full"], B)
            sp.dma_start(brow[:, :], ins[name].partition_broadcast(P)).then_inc(row_landed, 16)

        def add_row(dve, n):
            dve.wait_ge(row_landed, 16 * (n + 1))
            for b in range(B):
                dve.tensor_tensor(x[:, b, :], x[:, b, :], brow[:, :], ALU.add).then_inc(row_added, 1)
            dve.wait_ge(row_added, B * (n + 1))

        PATCH = D // P
        H1, DH1 = 8, 8
        E1 = H1 * DH1
        xn1 = [sq[:, i * D:(i + 1) * D] for i in range(2)]
        wq1, wk1, wv1 = (brow[:, i * E1:(i + 1) * E1] for i in range(3))
        wo1 = brow[0:E1, 3 * E1:3 * E1 + P]
        bv1 = brow[:, 3 * E1 + P:4 * E1 + P]
        q1, k1 = ([maskadd[:, j * BH:(j + 1) * BH, :].rearrange("p a n -> p (a n)"),
                   flat[:, 3 * T + j * D:3 * T + (j + 1) * D]] for j in range(2))
        bq1 = rrms[0:E1, 0:1]
        turn1 = [turn, outp[0]]
        sum1 = [heado, outp[1]]
        o9 = [biasbuf[:, :, :].rearrange("p a n -> p (a n)"), mask_bytes[:, :].bitcast(F32)]
        v1 = [ring[:, 4 + i, 0:PATCH * H1 * (DH1 + 1)].rearrange("p (n h d) -> p n h d", n=PATCH, h=H1)
              for i in range(2)]
        o1 = flat[:, 0:B * PATCH * E1]
        og = [flat[0:E1, B * PATCH * E1 + i * D:B * PATCH * E1 + (i + 1) * D] for i in range(2)]

        UNITS = 2 * PATCH

        def in_pairs(engine, emit):
            for b in range(2):
                emit(b, b)
            with engine.Fori(1, B // 2 - 1) as i:
                for k in range(2):
                    emit(2 * i + k, k)
            for b in range(2):
                emit(B - 2 + b, b)

        def is_last(b):
            return isinstance(b, int) and b == B - 1

        def l1_sp(sp):
            m = L1
            F0.events.wait(sp, "pre_split", 2)
            sp.dma_start(brow[:, 0:3 * E1 + P], ins["L1_w"]).then_inc(m["w_landed"], 16)
            sp.dma_start(bv1, ins["L1_bv"].partition_broadcast(P)).then_inc(m["w_landed"], 16)
            F0.events.wait(sp, "split", 3 * F0.chunks)

            def mask_row(b):
                return ins["mask1"][bass.ds(b, 1)].rearrange("a n -> (a n)").partition_broadcast(P)

            def batch(b, k):
                wait(sp, m["v_full"], b - 1)
                sp.dma_start(ring[:, k, :], ins["ctx_tok"][bass.ds(b, 1)].rearrange("a p n -> (a p) n"))\
                  .then_inc(m["ctx_landed", k], 16)
                wait(sp, m["k_made"], 2 * b - 2)
                sp.dma_start(ring[:, 2 + k, :], mask_row(b)).then_inc(m["mask_landed", k], 16)

            in_pairs(sp, batch)
            for b in range(B):
                if b < 2:
                    sp.wait_ge(m["k_made"], 2 * (B - 1 + b))
                else:
                    sp.wait_ge(m["out_biased"], b - 1)
                sp.dma_start(ring[:, 2 + b % 2, :], mask_row(b)).then_inc(m["mask_landed", b % 2], 16)

        def l1_pool(pool):
            m = L1

            def batch(b, k):
                pool.wait_ge(m["k_made"], 2 * b + 2)
                for n in range(PATCH):
                    pn = PATCH * b + n
                    wait(pool, m["sfull"], 2 * (pn - 1))
                    pool.tensor_tensor(kblock[0:E1 + 1, n % 2, :, :],
                                       k1[k][0:E1 + 1, n * P:(n + 1) * P].unsqueeze(1).broadcast_to([E1 + 1, H1, P]),
                                       consts[0:E1 + 1, C_HEADS:C_HEADS + H1].unsqueeze(2).broadcast_to([E1 + 1, H1, P]),
                                       ALU.mult).then_inc(m["blocked"], 1)

            in_pairs(pool, batch)

        def l1_pe(pe):
            m = L1
            pe.wait_ge(m["w_landed"], 32)
            pe.wait_ge(m["ones"], 7)

            def project_qk(b, k):
                pe.wait_ge(m["normed"], b + 1)
                wait(pe, m["k_biased"], b)
                wait(pe, m["v_made"], b)
                pe.matmul(proj[0][0:E1, :], wq1, xn1[k], start=True, stop=True)
                pe.matmul(proj[1][0:E1, :], wk1, xn1[k], start=True, stop=True).then_inc(m["qk_full"], 1)

            def project_v(b, k):
                pe.wait_ge(m["ctx_landed", k], 16 * (b // 2 + 1) if isinstance(b, int) else 8 * (b - k) + 16)
                pe.wait_ge(m["q_made"], b + 1)
                for n in range(PATCH):
                    mm = pe.matmul(proj[0][:, n * E1:(n + 1) * E1], ring[:, k, n * P:(n + 1) * P], wv1, start=True, stop=True)
                mm.then_inc(m["v_full"], 1)

            def turn_and_sum(turned, summed):
                if turned:
                    u, s = turned
                    wait(pe, m["tfree"], u - 1)
                    pe.wait_ge(m["exps"], u + 1)
                    for h in range(4):
                        mm = pe.transpose(turn1[s][:, h * P:(h + 1) * P], pbuf[:, s, h * P:(h + 1) * P], ident)
                    mm.then_inc(m["tfull"], 1)
                if summed:
                    b, u2, k, n, s2 = summed
                    pe.wait_ge(m["tfree"], u2 + 1)
                    if s2 == 0:
                        wait(pe, m["onorm"], PATCH * b + (n - 1))
                        pe.wait_ge(m["v_made"], b + 1)
                    for h in range(4):
                        mm = pe.matmul(sum1[n % 2][32 * h:32 * h + 9, s2 * P:(s2 + 1) * P], v1[k][:, n, 4 * s2 + h, :],
                                       ptbuf[:, s2, h * P:(h + 1) * P], start=True, stop=True)
                    mm.then_inc(m["av"], 1)

            def turn_sums(pn, i):
                pe.wait_ge(m["osums"], pn + 1)
                for s in range(2):
                    mm = pe.transpose(sum1[i][:, (2 + s) * P:(3 + s) * P], o9[i][:, s * P:(s + 1) * P], ident)
                mm.then_inc(m["sturned"], 1)

            def back(b, k, n, s, steps):
                at = 2 * n + s - steps
                if at < 0:
                    b, k, at = b - 1, 1 - k, at + UNITS
                if isinstance(b, int) and b < 0:
                    return None
                return b, UNITS * b + at, k, at // 2, at % 2

            def batch(b, k):
                pe.wait_ge(m["q_made"], b + 1)
                for n in range(PATCH):
                    pn = PATCH * b + n
                    for s in range(2):
                        u = UNITS * b + (2 * n + s)
                        if s == 0:
                            pe.wait_ge(m["blocked"], pn + 1)
                        wait(pe, m["shifted"], u - 1)
                        pe.matmul(score[s][:, :], q1[k][0:E1 + 1, n * P:(n + 1) * P],
                                  kblock[0:E1 + 1, n % 2, 4 * s:4 * s + 4, :].rearrange("p h j -> p (h j)"),
                                  start=True, stop=True).then_inc(m["sfull"], 1)
                        if (n, s) == (1, 0) and not is_last(b):
                            project_qk(b + 1, 1 - k)
                        if (n, s) == (2, 0) and not is_last(b):
                            project_v(b + 1, 1 - k)
                        two = back(b, k, n, s, 2)
                        turn_and_sum(two and (two[1], s), back(b, k, n, s, 3))
                        if s == 1 and not (isinstance(pn, int) and pn < 2):
                            turn_sums(pn - 2, n % 2)

            project_qk(0, 0)
            project_v(0, 0)
            in_pairs(pe, batch)
            u = UNITS * B
            turn_and_sum((u - 2, 0), (B - 1, u - 3, 1, PATCH - 2, 1))
            turn_and_sum((u - 1, 1), (B - 1, u - 2, 1, PATCH - 1, 0))
            turn_sums(PATCH * B - 2, 0)
            turn_and_sum(None, (B - 1, u - 1, 1, PATCH - 1, 1))
            turn_sums(PATCH * B - 1, 1)

            def turn_outputs(b):
                wait(pe, m["oturned"], b - 1)
                for n in range(PATCH):
                    mm = pe.transpose(proj[b % 2][0:E1, n * P:(n + 1) * P], o1[:, (PATCH * b + n) * E1:(PATCH * b + n + 1) * E1],
                                      ident)
                mm.then_inc(m["osum"], 1)

            def out_product(b):
                if b + 1 < B:
                    turn_outputs(b + 1)
                pe.wait_ge(m["oturned"], b + 1)
                wait(pe, m["out_biased"], b - 1)
                pe.matmul(outp[b % 2][:, :], wo1, og[b % 2], start=True, stop=True).then_inc(m["out_full"], 1)

            pe.wait_ge(m["gelu"], 1)
            turn_outputs(0)
            pe_tail(pe, 3, out_product)

        def l1_act(act):
            m = L1

            def take_turned(u, s):
                act.wait_ge(m["tfull"], u + 1)
                wait(act, m["av"], u - 1)
                act.activation(ptbuf[:, s, :], turn1[s][:, :], ACT.Copy).then_inc(m["tfree"], 1)

            def take_sums(pn, i):
                act.wait_ge(m["av"], 2 * pn + 2)
                wait(act, m["sturned"], pn - 1)
                act.activation(o9[i], sum1[i][:, 0:2 * P], ACT.Copy).then_inc(m["osums"], 1)

            def take_qk(b, k):
                act.wait_ge(m["qk_full"], b + 1)
                wait(act, m["sfull"], UNITS * (b - 1))
                act.activation(q1[k][0:E1, :], proj[0][0:E1, :], ACT.Identity, bias=bq1, scale=float(DH1) ** -0.5)\
                   .then_inc(m["q_made"], 1)
                wait(act, m["blocked"], PATCH * (b - 1))
                act.activation(k1[k][0:E1, :], proj[1][0:E1, :], ACT.Identity, bias=vecs[0:E1, V_BK1:V_BK1 + 1])\
                   .then_inc(m["k_biased"], 1)

            def batch(b, k):
                for n in range(PATCH):
                    for s in range(2):
                        u = UNITS * b + (2 * n + s)
                        act.wait_ge(m["shifted"], u + 1)
                        wait(act, m["tfull"], u - 1)
                        act.activation(pbuf[:, s, :], tbuf[:, s, :], ACT.Exp).then_inc(m["exps"], 1)
                        if (n, s) == (1, 0) and not is_last(b):
                            take_qk(b + 1, 1 - k)
                        if not (isinstance(u, int) and u < 2):
                            take_turned(u - 2, s)
                        if s == 0 and not (isinstance(u, int) and u < 4):
                            take_sums(PATCH * b + (n - 2), n % 2)

            act.wait_ge(m["ones"], 7)
            take_qk(0, 0)
            in_pairs(act, batch)
            for s in range(2):
                take_turned(UNITS * B - 2 + s, s)
                take_sums(PATCH * B - 2 + s, s)
            act.wait_ge(m["onorm"], B * PATCH)
            act.activation(o1, o1, ACT.Gelu).then_inc(m["gelu"], 1)
            for b in range(B):
                act.wait_ge(m["osum"], b + 1)
                wait(act, m["out_full"], b - 1)
                act.activation(og[b % 2], proj[b % 2][0:E1, :], ACT.Copy).then_inc(m["oturned"], 1)
            act_tail(act, 3)

        def l1_dve(dve):
            m = L1
            F0.events.wait(dve, "split", 3 * F0.chunks)
            for i in range(2):
                dve.memset(v1[i][:, :, :, DH1:DH1 + 1], 1.0).then_inc(m["ones"], 1)
            for i in range(2):
                dve.memset(sum1[i][:, 0:2 * P], 0.0).then_inc(m["ones"], 1)
            for i in range(2):
                dve.memset(q1[i][E1:E1 + 1, :], 1.0).then_inc(m["ones"], 1)
            dve.tensor_scalar(bq1, vecs[0:E1, V_BQ1:V_BQ1 + 1], float(DH1) ** -0.5, None, ALU.mult).then_inc(m["ones"], 1)
            dve.wait_ge(ln_newton, 9 * LN_CALLS_AT_L1)
            dve.wait_ge(m["w_landed"], 32)

            def softmax(u, s):
                blocks = lambda ap: ap.rearrange("p (h j) -> p h j", h=4)
                dve.wait_ge(m["sfull"], u + 1)
                dve.tensor_reduce(rowmax[:, s, 0:4], blocks(score[s][:, :]), AX.X, ALU.max).then_inc(m["rowmax"], 1)
                dve.wait_ge(m["rowmax"], u + 1)
                wait(dve, m["exps"], u - 1)
                dve.tensor_tensor(blocks(tbuf[:, s, :]), blocks(score[s][:, :]),
                                  rowmax[:, s, 0:4].unsqueeze(2).broadcast_to([P, 4, P]), ALU.subtract).then_inc(m["shifted"], 1)

            def normalise(pn, n):
                dve.wait_ge(m["sturned"], pn + 1)
                o = sum1[n % 2][:, 2 * P:4 * P].rearrange("p (h d) -> p h d", h=H1)
                dve.reciprocal(rinv[:, n % 2, :], o[:, :, DH1]).then_inc(m["v_inv"], 1)
                dve.wait_ge(m["v_inv"], pn + 1)
                dve.tensor_tensor(o1[:, bass.ds(pn * E1, E1)].rearrange("p (h d) -> p h d", h=H1), o[:, :, 0:DH1],
                                  rinv[:, n % 2, :].unsqueeze(2).broadcast_to([P, H1, DH1]), ALU.mult).then_inc(m["onorm"], 1)

            def norm(b, k):
                wait(dve, m["qk_full"], b - 1)
                dve.tensor_scalar(xn1[k], x[:, bass.ds(b, 1), :].rearrange("p a n -> p (a n)"),
                                  moments[:, bass.ds(b, 1), 0], rstd[:, bass.ds(b, 1)], ALU.subtract, ALU.mult)\
                   .then_inc(m["normed"], 1)

            def mask_keys(b, k):
                dve.wait_ge(m["k_biased"], b + 1)
                dve.wait_ge(m["mask_landed", k], 16 * (b // 2 + 1) if isinstance(b, int) else 8 * (b - k) + 16)
                mask = ring[:, 2 + k, :]
                dve.scalar_tensor_tensor(k1[k][0:E1, :], mask[0:E1, :], 0.0, k1[k][0:E1, :], ALU.is_gt, ALU.mult)\
                   .then_inc(m["k_made"], 1)
                dve.tensor_scalar(k1[k][E1:E1 + 1, :], mask[E1:E1 + 1, :], 0.0, -1e9, ALU.is_le, ALU.mult)\
                   .then_inc(m["k_made"], 1)

            def take_values(b, k):
                dve.wait_ge(m["v_full"], b + 1)
                wait(dve, m["av"], UNITS * (b - 1))
                dve.tensor_tensor(v1[k][:, :, :, 0:DH1],
                                  proj[0][:, 0:PATCH * E1].rearrange("p (n h d) -> p n h d", n=PATCH, h=H1),
                                  bv1.rearrange("p (h d) -> p h d", h=H1).unsqueeze(1).broadcast_to([P, PATCH, H1, DH1]),
                                  ALU.add).then_inc(m["v_made"], 1)

            def batch(b, k):
                for n in range(PATCH):
                    pn = PATCH * b + n
                    for s in range(2):
                        softmax(UNITS * b + (2 * n + s), s)
                        if s == 0 and n == 1 and not is_last(b):
                            mask_keys(b + 1, 1 - k)
                        if s == 0 and not (isinstance(pn, int) and pn < 3):
                            normalise(pn - 3, n + 1)
                    if n == 0 and not is_last(b):
                        norm(b + 1, 1 - k)
                    if n == 2 and not is_last(b):
                        take_values(b + 1, 1 - k)

            norm(0, 0)
            mask_keys(0, 0)
            take_values(0, 0)
            in_pairs(dve, batch)
            for n in range(3):
                normalise(PATCH * B - 3 + n, n + 1)

            def add(b):
                dve.wait_ge(m["out_full"], b + 1)
                dve.wait_ge(m["mask_landed", b % 2], 16 * (B // 2 + b // 2 + 1))
                wait(dve, m["added"], b - 1)
                dve.scalar_tensor_tensor(ptbuf[:, b % 2, :], outp[b % 2][:, :], vecs[:, V_BO1:V_BO1 + 1],
                                         ring[:, 2 + b % 2, :], ALU.add, ALU.mult).then_inc(m["out_biased"], 1)
                dve.wait_ge(m["out_biased"], b + 1)
                dve.tensor_tensor(x[:, b, :], x[:, b, :], ptbuf[:, b % 2, :], ALU.add).then_inc(m["added"], 1)
                dve.wait_ge(m["added"], b + 1)

            dve_tail(dve, 3, add)

        EXPERTS, RANK = 8, 16
        ER = EXPERTS * RANK
        HL = ER + EXPERTS
        hl = spare[:, 0:B * HL].rearrange("p (b n) -> p b n", b=B)
        rt = [spare[:, B * HL + 64 * i:B * HL + 64 * (i + 1)].rearrange("p (b e) -> p b e", b=B) for i in range(6)]

        w_low = w_in[:, :, :, :].rearrange("p s a n -> p (s a n)")[:, 0:8 * HL].rearrange("p (c a n) -> p c a n", c=4, a=2)
        w_base = acts[:, 0:2, :, :].rearrange("p s a n -> p (s a n)").rearrange("p (c a n) -> p c a n", c=4, a=2)

        def m2_sp(sp):
            m = M2
            LA[2].events.wait(sp, "split", LA[2].tiles * NG)
            sp.dma_start(ring[:, 0:4, 0:HL], ins["M2_a"]).then_inc(m["a_landed"], 16)
            sp.dma_start(ring[:, 5, :], ins["M2_b"]).then_inc(m["b_landed"], 16)
            row_sp(sp, 0, "M2_bias")
            sp.wait_ge(m["a_split"], 1)
            sp.dma_start(ring[:, 0:4, :], ins["M2_w"]).then_inc(m["w_landed"], 16)

        def m2_pool(pool):
            m = M2
            LA[2].events.wait(pool, ("pfull", 1), LA[2].projections * NG)
            pool.wait_ge(m["a_landed"], 16)
            raw = ring[:, 0:4, 0:HL]
            zeros = consts[:, C_ZERO:C_ZERO + 1].unsqueeze(2)
            pool.tensor_tensor(w_low[:, :, 0, :], raw, zeros.broadcast_to([P, 4, HL]), ALU.add).then_inc(m["a_high"], 1)
            pool.wait_ge(m["a_high"], 1)
            pool.tensor_tensor(w_low[:, :, 1, :], raw, w_low[:, :, 0, :].bitcast(F32), ALU.subtract)\
                .then_inc(m["a_split"], 1)
            LA[2].events.wait(pool, "outfull", B * (NPAIR - 1))
            pool.wait_ge(m["w_landed"], 16)
            pool.tensor_tensor(w_base[:, :, 0, :], ring[:, 0:4, :], zeros.broadcast_to([P, 4, D]), ALU.add)\
                .then_inc(m["w_high"], 1)
            pool.wait_ge(m["w_high"], 1)
            pool.tensor_tensor(w_base[:, :, 1, :], ring[:, 0:4, :], w_base[:, :, 0, :].bitcast(F32), ALU.subtract)\
                .then_inc(m["w_split"], 1)

        def m2_pe(pe):
            m = M2
            pe.wait_ge(m["a_split"], 1)
            for b in range(B):
                pe.wait_ge(ln_low, 8 * ln_no(5) + b + 1)
                wait(pe, m["copied"], b - 1)
                mm = pe_matmuls(pe, proj[b % 2][:, 0:HL], lambda a, c: xnT[:, a, c, b * S:(b + 1) * S],
                                lambda a, c: w_low[:, c, a, :])
                mm.then_inc(m["full"], 1)
            pe.wait_ge(m["w_split"], 1)

            def base(b):
                wait(pe, m["added"], b - 1)
                pe_matmuls(pe, outp[b % 2][:, :], lambda a, c: xnT[:, a, c, b * S:(b + 1) * S],
                           lambda a, c: w_base[:, c, a, :], last=False)

            def turn_weighted(b):
                wait(pe, m["high"], b - 1)
                pe.transpose(proj[b % 2][:, 0:P], hl[:, b, 0:ER], ident).then_inc(m["turned"], 1)

            def product(b):
                if b >= 2:
                    base(b)
                if b + 1 < B:
                    turn_weighted(b + 1)
                pe.wait_ge(m["high"], b + 1)
                pe.matmul(outp[b % 2][:, :], ptbuf[:, b % 2, 0:P], ring[:, 5, :], start=False, stop=True)\
                  .then_inc(m["outfull"], 1)

            base(0)
            base(1)
            pe.wait_ge(m["b_landed"], 16)
            pe.wait_ge(m["weighted"], 1)
            turn_weighted(0)
            pe_tail(pe, 6, product)

        def m2_act(act):
            m = M2
            act.wait_ge(m["route"], 6)
            act.activation(rt[1], rt[1], ACT.Exp).then_inc(m["expd"], 1)
            for b in range(B):
                act.wait_ge(m["turned"], b + 1)
                wait(act, m["outfull"], b - 1)
                act.activation(ptbuf[:, b % 2, 0:P], proj[b % 2][:, 0:P], ACT.Copy).then_inc(m["high"], 1)
            act_tail(act, 6)

        def m2_dve(dve):
            m = M2
            for b in range(B):
                dve.wait_ge(m["full"], b + 1)
                dve.tensor_copy(hl[:, b, :], proj[b % 2][:, 0:HL]).then_inc(m["copied"], 1)
            dve.wait_ge(m["copied"], B)
            logits = hl[:, :, ER:HL]
            wide = [t.rearrange("p (b e f) -> p b e f", b=B, e=EXPERTS) for t in (tbuf[:, 0, :], tbuf[:, 1, :])]
            mine = logits.unsqueeze(3).broadcast_to([P, B, EXPERTS, EXPERTS])
            other = logits.unsqueeze(2).broadcast_to([P, B, EXPERTS, EXPERTS])
            dve.tensor_tensor(wide[0], other, mine, ALU.is_gt).then_inc(m["route"], 1)
            dve.tensor_tensor(wide[1], other, mine, ALU.is_equal).then_inc(m["route"], 1)
            dve.wait_ge(m["route"], 2)
            less = consts[:, C_LESS:C_LESS + 64].unsqueeze(1).broadcast_to([P, B, 64])
            dve.tensor_tensor(tbuf[:, 1, :].rearrange("p (b n) -> p b n", b=B), tbuf[:, 1, :].rearrange("p (b n) -> p b n", b=B),
                              less, ALU.mult).then_inc(m["route"], 1)
            dve.wait_ge(m["route"], 3)
            dve.tensor_tensor(tbuf[:, 0, :], tbuf[:, 0, :], tbuf[:, 1, :], ALU.add).then_inc(m["route"], 1)
            dve.tensor_reduce(rowmax[:, 0, :], logits, AX.X, ALU.max).then_inc(m["route"], 1)
            dve.wait_ge(m["route"], 5)
            dve.tensor_tensor(rt[1], logits, rowmax[:, 0, :].unsqueeze(2).broadcast_to([P, B, EXPERTS]), ALU.subtract)\
               .then_inc(m["route"], 1)
            dve.tensor_reduce(rt[0], wide[0], AX.X, ALU.add).then_inc(m["route"], 1)
            dve.wait_ge(m["route"], 7)
            dve.wait_ge(m["expd"], 1)
            dve.scalar_tensor_tensor(rt[2], rt[0], 1.5, rt[1], ALU.is_lt, ALU.mult).then_inc(m["routed"], 1)
            dve.wait_ge(m["routed"], 1)
            dve.tensor_reduce(rowmax[:, 1, :], rt[2], AX.X, ALU.add).then_inc(m["routed"], 1)
            dve.wait_ge(m["routed"], 2)
            dve.reciprocal(rinv[:, 0, :], rowmax[:, 1, :]).then_inc(m["routed"], 1)
            dve.wait_ge(m["routed"], 3)
            dve.scalar_tensor_tensor(rt[3], rt[2], 2.0, rinv[:, 0, :].unsqueeze(2).broadcast_to([P, B, EXPERTS]),
                                     ALU.mult, ALU.mult).then_inc(m["routed"], 1)
            dve.wait_ge(m["routed"], 4)
            act_hl = hl[:, :, 0:ER].rearrange("p b (e r) -> p b e r", e=EXPERTS)
            dve.tensor_tensor(act_hl, act_hl, rt[3].unsqueeze(3).broadcast_to([P, B, EXPERTS, RANK]), ALU.mult)\
               .then_inc(m["weighted"], 1)
            add_row(dve, 0)

            def add(b):
                dve.wait_ge(m["outfull"], b + 1)
                dve.tensor_tensor(x[:, b, :], x[:, b, :], outp[b % 2][:, :], ALU.add).then_inc(m["added"], 1)
                dve.wait_ge(m["added"], b + 1)

            dve_tail(dve, 6, add)

        def start_sp(sp):
            sp.dma_start(consts[:, :], ins["consts"]).then_inc(consts_landed, 16)
            sp.dma_start(vecs[:, :], ins["vecs"]).then_inc(consts_landed, 16)
            for n in range(8):
                if n % 4 == 0:
                    sp.dma_start(x[:, n:n + 4, :], ins["x"][:, n:n + 4, :]).then_inc(x_landed[n // 4], 16)
                if n == 4:
                    sp.dma_start(mask_bytes[:, :], ins["mask0"]).then_inc(mask_landed, 16)
                if n >= 4:
                    sp.wait_ge(ctx_split, n - 3)
                sp.dma_start(ring[:, n % 4, :], ins["ctxT"][:, n // 2, (n % 2) * HALF:(n % 2 + 1) * HALF])\
                  .then_inc(ctx_landed[n % 4], 16)
            sp.wait_ge(ctx_split, 8)

        def start_act(act):
            for n in range(8):
                cols = slice((n % 2) * HALF, (n % 2 + 1) * HALF)
                act.wait_ge(ctx_landed[n % 4], 16 * (n // 4 + 1))
                act.activation(ctxT[:, 0, n // 2, cols], ring[:, n % 4, :], ACT.Copy).then_inc(ctx_high, 1)

        def start_pool(pool):
            pool.wait_ge(consts_landed, 32)
            for n in range(8):
                cols = slice((n % 2) * HALF, (n % 2 + 1) * HALF)
                pool.wait_ge(ctx_high, n + 1)
                pool.tensor_tensor(ctxT[:, 1, n // 2, cols], ring[:, n % 4, :],
                                   ctxT[:, 0, n // 2, cols].bitcast(F32), ALU.subtract).then_inc(ctx_split, 1)

        def start_dve(dve):
            dve.wait_ge(consts_landed, 32)
            dve.scalar_tensor_tensor(kqn[:, :], vecs[:, V_QN:V_QN + 1], LA[2].scale, vecs[:, V_KN:V_KN + 1], ALU.mult,
                                     ALU.mult).then_inc(kqn_made, 1)
            dve_tail(dve, 0, None)
            dve.wait_ge(mask_landed, 16)
            dve.tensor_scalar(maskadd[:, :, :].rearrange("p b n -> p (b n)"), mask_bytes[:, :].bitcast(U8), -1.0, MASKED, ALU.add, ALU.mult).then_inc(mask_made, 1)
            dve.wait_ge(mask_made, 1)
            dve.tensor_reduce(live[:, :], maskadd[:, :, :], AX.X, ALU.max).then_inc(mask_made, 1)
            dve.wait_ge(mask_made, 2)
            dve.tensor_scalar(live[:, :], live[:, :], -1.0, None, ALU.is_gt).then_inc(mask_made, 1)
            dve.wait_ge(mask_made, 3)

        def finish_sp(sp):
            for b in range(B):
                F3.events.wait(sp, "added", B * (F3.chunks // 2 - 1) + b + 1)
                sp.dma_start(out[:, b, :], x[:, b, :]).then_inc(out_landed, 16)
            sp.wait_ge(out_landed, 16 * B)

        block = ctx.enter_context(nc.Block())

        @block.sync
        def _(sp):
            start_sp(sp)
            attention_sp(sp, LA[0])
            LA[0].events.wait(sp, "split", LA[0].tiles * NG)
            LA[0].events.wait(sp, "pv", 2 * NH)
            ffn_sp(sp, F0)
            l1_sp(sp)
            sp.wait_ge(L1["out_full"], B)
            sp.wait_ge(L1["out_biased"], B)
            ffn_sp(sp, F1)
            F1.events.wait(sp, "split", 2 * F1.chunks)
            sp.dma_start(maskadd[:, 0, :], ins["mask2"]).then_inc(mask_landed, 16)
            attention_sp(sp, LA[2])
            m2_sp(sp)
            row_sp(sp, 1, "L3_bo")
            sp.wait_ge(M2["w_split"], 1)
            attention_sp(sp, LA[3])
            row_sp(sp, 2, "F3_bias")
            LA[3].events.wait(sp, "split", LA[3].tiles * NG)
            ffn_sp(sp, F3)
            finish_sp(sp)

        @block.gpsimd
        def _(pool):
            start_pool(pool)
            attention_pool(pool, LA[0])
            ffn_pool(pool, F0)
            l1_pool(pool)
            ffn_pool(pool, F1)
            attention_pool(pool, LA[2])
            m2_pool(pool)
            attention_pool(pool, LA[3])
            ffn_pool(pool, F3)

        @block.tensor
        def _(pe):
            pe.wait_ge(consts_landed, 32)
            pe_tail(pe, 0, None)
            attention_pe(pe, LA[0])
            ffn_pe(pe, F0)
            l1_pe(pe)
            ffn_pe(pe, F1)
            attention_pe(pe, LA[2])
            m2_pe(pe)
            attention_pe(pe, LA[3])
            ffn_pe(pe, F3)

        @block.scalar
        def _(act):
            act.wait_ge(consts_landed, 32)
            start_act(act)
            act_tail(act, 0)
            attention_act(act, LA[0])
            ffn_act(act, F0)
            l1_act(act)
            ffn_act(act, F1)
            attention_act(act, LA[2])
            m2_act(act)
            attention_act(act, LA[3])
            ffn_act(act, F3)

        @block.vector
        def _(dve):
            start_dve(dve)
            attention_dve(dve, LA[0])
            ffn_dve(dve, F0)
            l1_dve(dve)
            ffn_dve(dve, F1)
            dve.wait_ge(mask_landed, 32)
            attention_dve(dve, LA[2])
            m2_dve(dve)
            attention_dve(dve, LA[3])
            ffn_dve(dve, F3)


def constants():
    c = np.zeros((P, C_COUNT), np.float32)
    c[:, C_IDENT:C_IDENT + P] = np.eye(P)
    c[:, C_ONES:C_ONES + P] = 1
    for e in range(64):
        c[e, C_HEADS + e // 8] = 1
    c[64, C_HEADS:C_HEADS + 8] = 1
    c[:, C_FIRST:C_FIRST + 32] = np.arange(32, 0, -1)
    c[:, C_LESS:C_LESS + 64] = np.tril(np.ones((8, 8)), -1).reshape(64)
    return c


def tiles(w):
    n = w.shape[0] // P
    return w.reshape(n, P, -1, P).transpose(0, 3, 2, 1).reshape(n, P, -1)


def pad_rows(w, rows):
    return np.concatenate([w, np.zeros((rows - w.shape[0], w.shape[1]), w.dtype)])


def layout(inputs):
    i = {k: np.asarray(a) for k, a in inputs.items()}
    a = {"consts": constants()}
    a["x"] = i["x"].transpose(1, 0, 2)
    a["ctxT"] = i["ctx_4096"].reshape(T, DC, P).transpose(2, 1, 0)
    a["mask0"] = i["mask_BxSxS2_bk0"].transpose(1, 0, 2).reshape(S, T).view(np.int32)
    a["position_bias"] = i["L0_xattn_position_bias"]
    vecs = np.zeros((P, V_COUNT), np.float32)
    vecs[:, V_LNW:V_LNW + 4] = i["L0_xattn_ln_weight"].reshape(DC, P).T
    vecs[:, V_BQ3:V_BQ3 + 32] = i["L3_xattn_bq"].reshape(NH, P).T
    vecs[:, V_BK3:V_BK3 + 16] = i["L3_xattn_bkv"].reshape(16, P).T
    vecs[:, V_QN] = i["L2_xattn_q_norm_w"]
    vecs[:, V_KN] = i["L2_xattn_k_norm_w"]
    vecs[:64, V_BQ1] = i["L1_xattn_bq"]
    vecs[:64, V_BK1] = i["L1_xattn_bk"]
    vecs[:, V_BO1] = i["L1_xattn_bo"]
    vecs[:, V_BI:V_BI + 16] = i["L3_ffn_inter_b"].reshape(16, P).T
    vecs[:, V_BI + 16:V_BI + 32] = vecs[:, V_BI:V_BI + 16]
    a["vecs"] = vecs
    a["L0_wq"], a["L0_wk"], a["L0_wv"] = (tiles(i[f"L0_xattn_w_{n}"]) for n in "qkv")
    a["L0_wo"] = i["L0_xattn_w_out"].T.reshape(NH, P, D)
    a["L2_wq"], a["L2_wk"], a["L2_wv"] = (tiles(i[f"L2_xattn_W{n}"]) for n in "qkv")
    a["L2_wo"] = i["L2_xattn_Wo"].T.reshape(NH, P, D)
    a["L3_wq"] = tiles(i["L3_xattn_Wq"].T)
    a["L3_wk"] = tiles(i["L3_xattn_Wkv"][:, :1024].T)
    a["L3_wv"] = tiles(i["L3_xattn_Wkv"][:, 1024:].T)
    a["L3_wo"] = i["L3_xattn_Wo"].reshape(NH, P, D)
    hid0 = 11 * P
    w1, w3, b1, b3 = (pad_rows(i[f"L0_ffn_{n}"], hid0) for n in ("w1", "w3", "lora_B1", "lora_B3"))
    a["F0_in"], a["F0_in2"] = tiles(w1), tiles(w3)
    a["F0_out"] = pad_rows(i["L0_ffn_w2"].T, hid0).reshape(11, P, D)
    pre = np.zeros((P, D), np.float32)
    pre[0:16], pre[32:48] = i["L0_ffn_lora_A1"], i["L0_ffn_lora_A3"]
    a["F0_pre"] = tiles(pre)[0]
    a["F0_b1"], a["F0_b3"], a["F0_b2"] = b1.T, b3.T, i["L0_ffn_lora_B2"].T
    a["F0_a2"] = pad_rows(i["L0_ffn_lora_A2"].T, hid0).reshape(11, P, 16).transpose(1, 0, 2).reshape(P, -1)
    a["L1_w"] = np.concatenate([i["L1_xattn_Wq"].T, i["L1_xattn_Wk"].T, i["L1_xattn_Wv"].T,
                                pad_rows(i["L1_xattn_Wo"].T, P)], axis=1)
    a["L1_bv"] = i["L1_xattn_bv"]
    a["ctx_tok"] = i["ctx_4096"]
    a["mask1"] = i["mask_Bx1x4096_ff1"].reshape(B, D)
    a["F1_pre"] = tiles(pad_rows(i["L1_ffn_c1_w"], P))[0]
    a["F1_c2"] = i["L1_ffn_c2_w"].T
    a["F1_in"] = tiles(i["L1_ffn_w1"])
    a["F1_out"] = i["L1_ffn_w2t"].reshape(14, P, D)
    a["mask2"] = i["mask_1x1xSxS2_ff0"].reshape(S, S)
    experts = np.concatenate([i["L2_ffn_A"].reshape(P, D), i["L2_ffn_W_router"]])
    a["M2_a"] = experts.T.reshape(DC, P, -1).transpose(1, 0, 2)
    a["M2_w"] = i["L2_ffn_W_base"].T.reshape(DC, P, D).transpose(1, 0, 2)
    a["M2_b"] = i["L2_ffn_B"].transpose(0, 2, 1).reshape(P, D)
    a["M2_bias"], a["L3_bo"], a["F3_bias"] = i["L2_ffn_b_base"], i["L3_xattn_bo"], i["L3_ffn_output_b"]
    a["F3_in"] = tiles(i["L3_ffn_inter_w"].T)
    a["F3_out"] = i["L3_ffn_output_w"].reshape(16, P, D)
    return {k: np.ascontiguousarray(n) for k, n in a.items()}


def kernel(**inputs):
    from concourse import bacc
    from concourse.bass_utils import run_bass_kernel_spmd

    arrays = layout(inputs)
    nc = bacc.Bacc("TRN2", target_bir_lowering=False, num_devices=1)
    ins = {k: nc.dram_tensor(f"in_{k}", a.shape, mybir.dt.from_np(a.dtype), kind="ExternalInput").ap()
           for k, a in arrays.items()}
    out = nc.dram_tensor("out", (P, B, D), F32, kind="ExternalOutput").ap()
    build(nc, ins, out)
    r = run_bass_kernel_spmd(nc, [{f"in_{k}": a for k, a in arrays.items()}], core_ids=[0])
    return np.ascontiguousarray(np.asarray(r.results[0]["out"]).transpose(1, 0, 2))
```
